# Optimizing a Trainium2 kernel written in Bass

```python
import numpy as np
import jax
import jax.numpy as jnp

def _softmax(x, axis=-1):
    return jax.nn.softmax(x, axis=axis)

def _gelu(x):
    return jax.nn.gelu(x, approximate=True)

def _silu(x):
    return jax.nn.silu(x)

def _sigmoid(x):
    return jax.nn.sigmoid(x)

def _layernorm(x, axis=-1, eps=1e-05):
    m = jnp.mean(x, axis=axis, keepdims=True)
    v = jnp.var(x, axis=axis, keepdims=True)
    return (x - m) / jnp.sqrt(v + eps)

def _scatter_add(tgt, idx, src, axis=0):
    return tgt.at[idx].add(src)

def _segment_sum(src, seg, n):
    return jax.ops.segment_sum(src, seg, n)
kernel_name = 'mk_cond_seq_d4_seqx_r4_7095fa'

def setup_inputs(seed: int=0):
    np.random.seed(seed)
    _w = jnp.asarray

    def _rec_inputs():
        import jax
        import jax.numpy as jnp
        _rk = jax.random.key(seed)
        x = -0.0002928 + 1 * jax.random.normal(jax.random.fold_in(_rk, 1), (2, 1024, 256), jnp.float32)
        _lenS = 1024 - jax.random.randint(jax.random.fold_in(_rk, 7), (2,), 0, max(1, 1024 // 4) + 1, jnp.int32)
        _lenS2 = 1024 - jax.random.randint(jax.random.fold_in(_rk, 8), (2,), 0, max(1, 1024 // 4) + 1, jnp.int32)
        cond_2048 = 0.0061147 + 1.02565 * jax.random.normal(jax.random.fold_in(_rk, 11), (2, 512), jnp.float32)
        cond_1024 = 0.00786388 + 1.0143 * jax.random.normal(jax.random.fold_in(_rk, 12), (2, 256), jnp.float32)
        _validS = jnp.arange(1024)[None, :] < _lenS[:, None]
        _validS2 = jnp.arange(1024)[None, :] < _lenS2[:, None]
        _causal = jnp.tril(jnp.ones((1024, 1024), dtype=bool))
        mask_BxS_ik0 = jnp.where(jnp.broadcast_to(_validS[:, :], (2, 1024)), 0, 1).astype(jnp.int32)
        mask_BxS_ff1 = jnp.where(jnp.ones((2, 1024), dtype=bool), 1.0, 0.0).astype(jnp.float32)
        return (x, cond_2048, cond_1024, mask_BxS_ik0, mask_BxS_ff1)
    x, cond_2048, cond_1024, mask_BxS_ik0, mask_BxS_ff1 = _rec_inputs()

    def _L0_cond_setup():
        import jax, jax.numpy as jnp
        import numpy as np
        D = 256
        DI = 512
        N = 16
        DT_RANK = 64
        D_CONV = 4
        EPS = 1e-05

        def _layernorm(x, g, b):
            mu = jnp.mean(x, axis=-1, keepdims=True)
            var = jnp.mean((x - mu) ** 2, axis=-1, keepdims=True)
            return (x - mu) * jax.lax.rsqrt(var + EPS) * g + b

        def _mamba(xn, in_proj_w, conv_w, conv_b, x_proj_w, dt_proj_w, dt_proj_b, A_log, D_param, out_proj_w):
            b, sl, _ = xn.shape
            xz = jnp.einsum('bsd,ed->bse', xn, in_proj_w)
            x_in, z = jnp.split(xz, 2, axis=-1)
            xt = jnp.transpose(x_in, (0, 2, 1))
            u = jax.lax.conv_general_dilated(xt, conv_w[:, None, :], (1,), [(D_CONV - 1, 0)], feature_group_count=DI, dimension_numbers=('NCH', 'OIH', 'NCH')) + conv_b[None, :, None]
            u = jax.nn.silu(jnp.transpose(u, (0, 2, 1)))
            x_dbl = jnp.einsum('bsd,ed->bse', u, x_proj_w)
            dt_r, B, C = jnp.split(x_dbl, [DT_RANK, DT_RANK + N], axis=-1)
            dt = jax.nn.softplus(jnp.einsum('bsr,dr->bsd', dt_r, dt_proj_w) + dt_proj_b)
            A = -jnp.exp(A_log)

            def step(h, inp):
                dt_t, B_t, C_t, u_t = inp
                dA = jnp.exp(dt_t[:, :, None] * A)
                h = h * dA + (dt_t * u_t)[:, :, None] * B_t[:, None, :]
                y = jnp.einsum('bdn,bn->bd', h, C_t)
                return (h, y)
            seq = (jnp.transpose(dt, (1, 0, 2)), jnp.transpose(B, (1, 0, 2)), jnp.transpose(C, (1, 0, 2)), jnp.transpose(u, (1, 0, 2)))
            h0 = jnp.zeros((b, DI, N), xn.dtype)
            _, ys = jax.lax.scan(step, h0, seq)
            y = jnp.transpose(ys, (1, 0, 2)) + u * D_param
            y = y * jax.nn.silu(z)
            return jnp.einsum('bsd,ed->bse', y, out_proj_w)
        key = jax.random.key(seed)
        ks = jax.random.split(key, 16)
        s = lambda fan: 1.0 / np.sqrt(fan)
        inp = {'x': jax.random.normal(ks[0], (2, 512, D), jnp.float32), 'c': jax.random.normal(ks[1], (2, 2 * D), jnp.float32), 'ln_g': jnp.ones((D,), jnp.float32), 'ln_b': jnp.zeros((D,), jnp.float32), 'ada_w': jax.random.normal(ks[2], (3 * D, 2 * D), jnp.float32) * s(2 * D), 'ada_b': jnp.zeros((3 * D,), jnp.float32), 'in_proj_w': jax.random.normal(ks[3], (2 * DI, D), jnp.float32) * s(D), 'conv_w': jax.random.normal(ks[4], (DI, D_CONV), jnp.float32) * s(D_CONV), 'conv_b': jnp.zeros((DI,), jnp.float32), 'x_proj_w': jax.random.normal(ks[5], (DT_RANK + 2 * N, DI), jnp.float32) * s(DI), 'dt_proj_w': jax.random.normal(ks[6], (DI, DT_RANK), jnp.float32) * s(DT_RANK), 'dt_proj_b': jax.random.uniform(ks[7], (DI,), jnp.float32, -4.0, -2.0), 'A_log': jnp.tile(jnp.log(jnp.arange(1, N + 1, dtype=jnp.float32)), (DI, 1)), 'D_param': jnp.ones((DI,), jnp.float32), 'out_proj_w': jax.random.normal(ks[8], (D, DI), jnp.float32) * s(DI)}
        return inp
    _L0_cond_all = _L0_cond_setup()
    _L0_cond_in = {k: v for k, v in _L0_cond_all.items() if k in ('ln_g', 'ln_b', 'ada_w', 'ada_b', 'in_proj_w', 'conv_w', 'conv_b', 'x_proj_w', 'dt_proj_w', 'dt_proj_b', 'A_log', 'D_param', 'out_proj_w')}
    del _L0_cond_all

    def _L1_cond_setup():
        import jax, jax.numpy as jnp
        import numpy as np
        B, S, D, E, N, R = (2, 256, 256, 512, 16, 64)
        EPS = 1e-05

        def _ln(x, g, b):
            m = jnp.mean(x, -1, keepdims=True)
            v = jnp.mean((x - m) ** 2, -1, keepdims=True)
            return (x - m) * jax.lax.rsqrt(v + EPS) * g + b

        def _ssm(u, Wdbc, Wdt, bdt, Alog, Dp):
            dbc = jnp.einsum('bse,re->bsr', u, Wdbc)
            dlt, Bm, Cm = jnp.split(dbc, [R, R + N], axis=-1)
            delta = jax.nn.softplus(jnp.einsum('bsr,er->bse', dlt, Wdt) + bdt)
            A = -jnp.exp(Alog)
            dA = jnp.exp(delta[..., None] * A)
            dBu = delta[..., None] * Bm[:, :, None, :] * u[..., None]

            def step(h, xs):
                dA_t, dBu_t, C_t = xs
                h = dA_t * h + dBu_t
                y = jnp.einsum('ben,bn->be', h, C_t)
                return (h, y)
            h0 = jnp.zeros((u.shape[0], u.shape[2], N), u.dtype)
            _, ys = jax.lax.scan(step, h0, (dA.swapaxes(0, 1), dBu.swapaxes(0, 1), Cm.swapaxes(0, 1)))
            return ys.swapaxes(0, 1) + u * Dp
        key = jax.random.key(seed)
        ks = jax.random.split(key, 16)
        f = lambda k, sh, s=0.02: jax.random.normal(k, sh, jnp.float32) * s
        Alog = jnp.log(jnp.tile(jnp.arange(1, N + 1, dtype=jnp.float32), (E, 1)))
        return dict(x=f(ks[0], (B, S, D), 1.0), c=f(ks[1], (B, 2 * D), 1.0), w=f(ks[2], (B, D), 1.0), norm1_g=jnp.ones((D,)), norm1_b=jnp.zeros((D,)), norm2_g=jnp.ones((D,)), norm2_b=jnp.zeros((D,)), Wx=f(ks[3], (E, D)), bx=jnp.zeros((E,)), Wz=f(ks[4], (E, D)), bz=jnp.zeros((E,)), Wf=f(ks[5], (D, E)), bf=jnp.zeros((D,)), Wada=f(ks[6], (3 * D, 2 * D)), bada=jnp.zeros((3 * D,)), Wc1=f(ks[7], (E, E)), bc1=jnp.zeros((E,)), Wc2=f(ks[8], (E, E)), bc2=jnp.zeros((E,)), Wdbc1=f(ks[9], (R + 2 * N, E)), Wdt1=f(ks[10], (E, R)), bdt1=jnp.zeros((E,)), Alog1=Alog, Dp1=jnp.ones((E,)), Wdbc2=f(ks[11], (R + 2 * N, E)), Wdt2=f(ks[12], (E, R)), bdt2=jnp.zeros((E,)), Alog2=Alog, Dp2=jnp.ones((E,)))
    _L1_cond_all = _L1_cond_setup()
    _L1_cond_in = {k: v for k, v in _L1_cond_all.items() if k in ('norm1_g', 'norm1_b', 'norm2_g', 'norm2_b', 'Wx', 'bx', 'Wz', 'bz', 'Wf', 'bf', 'Wada', 'bada', 'Wc1', 'bc1', 'Wc2', 'bc2', 'Wdbc1', 'Wdt1', 'bdt1', 'Alog1', 'Dp1', 'Wdbc2', 'Wdt2', 'bdt2', 'Alog2', 'Dp2')}
    del _L1_cond_all

    def _L2_cond_setup():
        import jax, jax.numpy as jnp
        import numpy as np
        H = 16
        LN_EPS = 1e-05

        def _layernorm(x, scale, bias):
            mu = jnp.mean(x, axis=-1, keepdims=True)
            var = jnp.var(x, axis=-1, keepdims=True)
            return (x - mu) * jax.lax.rsqrt(var + LN_EPS) * scale + bias
        key = jax.random.key(seed)
        ks = jax.random.split(key, 8)
        B, T, D, E = (4, 1024, 256, 512)
        s = 0.02
        return {'x': jax.random.normal(ks[0], (B, T, D), jnp.float32), 'emb': jax.random.normal(ks[1], (B, E), jnp.float32), 'src_mask': jax.random.randint(ks[2], (B, T), 0, 2).astype(jnp.int32), 'norm_scale': jnp.ones((D,), jnp.float32), 'norm_bias': jnp.zeros((D,), jnp.float32), 'Wq': jax.random.normal(ks[3], (D, D), jnp.float32) * s, 'bq': jnp.zeros((D,), jnp.float32), 'Wk': jax.random.normal(ks[4], (D, D), jnp.float32) * s, 'bk': jnp.zeros((D,), jnp.float32), 'Wv': jax.random.normal(ks[5], (D, D), jnp.float32) * s, 'bv': jnp.zeros((D,), jnp.float32), 'film_emb_W': jax.random.normal(ks[6], (E, 2 * D), jnp.float32) * s, 'film_emb_b': jnp.zeros((2 * D,), jnp.float32), 'film_norm_scale': jnp.ones((D,), jnp.float32), 'film_norm_bias': jnp.zeros((D,), jnp.float32), 'film_out_W': jax.random.normal(ks[7], (D, D), jnp.float32) * s, 'film_out_b': jnp.zeros((D,), jnp.float32)}
    _L2_cond_all = _L2_cond_setup()
    _L2_cond_in = {k: v for k, v in _L2_cond_all.items() if k in ('norm_scale', 'norm_bias', 'Wq', 'bq', 'Wk', 'bk', 'Wv', 'bv', 'film_emb_W', 'film_emb_b', 'film_norm_scale', 'film_norm_bias', 'film_out_W', 'film_out_b')}
    del _L2_cond_all

    def _L3_cond_setup():
        import jax, jax.numpy as jnp
        import numpy as np
        B, T, D, H, TE = (8, 256, 256, 16, 512)
        LN_EPS = 1e-05

        def layer_norm(x, w, b):
            m = jnp.mean(x, axis=-1, keepdims=True)
            v = jnp.var(x, axis=-1, keepdims=True)
            return (x - m) / jnp.sqrt(v + LN_EPS) * w + b
        key = jax.random.key(seed)
        ks = jax.random.split(key, 8)
        s = lambda k, sh: jax.random.normal(k, sh, jnp.float32) * 0.02
        return dict(x=jax.random.normal(ks[0], (B, T, D), jnp.float32), emb=jax.random.normal(ks[1], (B, TE), jnp.float32), src_mask=jnp.ones((B, T), jnp.float32), norm_w=jnp.ones((D,), jnp.float32), norm_b=jnp.zeros((D,), jnp.float32), q_w=s(ks[2], (D, D)), q_b=jnp.zeros((D,), jnp.float32), k_w=s(ks[3], (D, D)), k_b=jnp.zeros((D,), jnp.float32), v_w=s(ks[4], (D, D)), v_b=jnp.zeros((D,), jnp.float32), emb_w=s(ks[5], (TE, 2 * D)), emb_b=jnp.zeros((2 * D,), jnp.float32), sb_norm_w=jnp.ones((D,), jnp.float32), sb_norm_b=jnp.zeros((D,), jnp.float32), out_w=s(ks[6], (D, D)), out_b=jnp.zeros((D,), jnp.float32))
    _L3_cond_all = _L3_cond_setup()
    _L3_cond_in = {k: v for k, v in _L3_cond_all.items() if k in ('norm_w', 'norm_b', 'q_w', 'q_b', 'k_w', 'k_b', 'v_w', 'v_b', 'emb_w', 'emb_b', 'sb_norm_w', 'sb_norm_b', 'out_w', 'out_b')}
    del _L3_cond_all
    return {'x': x, 'cond_2048': cond_2048, 'cond_1024': cond_1024, 'mask_BxS_ik0': mask_BxS_ik0, 'mask_BxS_ff1': mask_BxS_ff1, 'L0_cond_ln_g': _L0_cond_in['ln_g'], 'L0_cond_ln_b': _L0_cond_in['ln_b'], 'L0_cond_ada_w': _L0_cond_in['ada_w'], 'L0_cond_ada_b': _L0_cond_in['ada_b'], 'L0_cond_in_proj_w': _L0_cond_in['in_proj_w'], 'L0_cond_conv_w': _L0_cond_in['conv_w'], 'L0_cond_conv_b': _L0_cond_in['conv_b'], 'L0_cond_x_proj_w': _L0_cond_in['x_proj_w'], 'L0_cond_dt_proj_w': _L0_cond_in['dt_proj_w'], 'L0_cond_dt_proj_b': _L0_cond_in['dt_proj_b'], 'L0_cond_A_log': _L0_cond_in['A_log'], 'L0_cond_D_param': _L0_cond_in['D_param'], 'L0_cond_out_proj_w': _L0_cond_in['out_proj_w'], 'L1_cond_norm1_g': _L1_cond_in['norm1_g'], 'L1_cond_norm1_b': _L1_cond_in['norm1_b'], 'L1_cond_norm2_g': _L1_cond_in['norm2_g'], 'L1_cond_norm2_b': _L1_cond_in['norm2_b'], 'L1_cond_Wx': _L1_cond_in['Wx'], 'L1_cond_bx': _L1_cond_in['bx'], 'L1_cond_Wz': _L1_cond_in['Wz'], 'L1_cond_bz': _L1_cond_in['bz'], 'L1_cond_Wf': _L1_cond_in['Wf'], 'L1_cond_bf': _L1_cond_in['bf'], 'L1_cond_Wada': _L1_cond_in['Wada'], 'L1_cond_bada': _L1_cond_in['bada'], 'L1_cond_Wc1': _L1_cond_in['Wc1'], 'L1_cond_bc1': _L1_cond_in['bc1'], 'L1_cond_Wc2': _L1_cond_in['Wc2'], 'L1_cond_bc2': _L1_cond_in['bc2'], 'L1_cond_Wdbc1': _L1_cond_in['Wdbc1'], 'L1_cond_Wdt1': _L1_cond_in['Wdt1'], 'L1_cond_bdt1': _L1_cond_in['bdt1'], 'L1_cond_Alog1': _L1_cond_in['Alog1'], 'L1_cond_Dp1': _L1_cond_in['Dp1'], 'L1_cond_Wdbc2': _L1_cond_in['Wdbc2'], 'L1_cond_Wdt2': _L1_cond_in['Wdt2'], 'L1_cond_bdt2': _L1_cond_in['bdt2'], 'L1_cond_Alog2': _L1_cond_in['Alog2'], 'L1_cond_Dp2': _L1_cond_in['Dp2'], 'L2_cond_norm_scale': _L2_cond_in['norm_scale'], 'L2_cond_norm_bias': _L2_cond_in['norm_bias'], 'L2_cond_Wq': _L2_cond_in['Wq'], 'L2_cond_bq': _L2_cond_in['bq'], 'L2_cond_Wk': _L2_cond_in['Wk'], 'L2_cond_bk': _L2_cond_in['bk'], 'L2_cond_Wv': _L2_cond_in['Wv'], 'L2_cond_bv': _L2_cond_in['bv'], 'L2_cond_film_emb_W': _L2_cond_in['film_emb_W'], 'L2_cond_film_emb_b': _L2_cond_in['film_emb_b'], 'L2_cond_film_norm_scale': _L2_cond_in['film_norm_scale'], 'L2_cond_film_norm_bias': _L2_cond_in['film_norm_bias'], 'L2_cond_film_out_W': _L2_cond_in['film_out_W'], 'L2_cond_film_out_b': _L2_cond_in['film_out_b'], 'L3_cond_norm_w': _L3_cond_in['norm_w'], 'L3_cond_norm_b': _L3_cond_in['norm_b'], 'L3_cond_q_w': _L3_cond_in['q_w'], 'L3_cond_q_b': _L3_cond_in['q_b'], 'L3_cond_k_w': _L3_cond_in['k_w'], 'L3_cond_k_b': _L3_cond_in['k_b'], 'L3_cond_v_w': _L3_cond_in['v_w'], 'L3_cond_v_b': _L3_cond_in['v_b'], 'L3_cond_emb_w': _L3_cond_in['emb_w'], 'L3_cond_emb_b': _L3_cond_in['emb_b'], 'L3_cond_sb_norm_w': _L3_cond_in['sb_norm_w'], 'L3_cond_sb_norm_b': _L3_cond_in['sb_norm_b'], 'L3_cond_out_w': _L3_cond_in['out_w'], 'L3_cond_out_b': _L3_cond_in['out_b']}

def reference(x, cond_2048, cond_1024, mask_BxS_ik0, mask_BxS_ff1, L0_cond_ln_g, L0_cond_ln_b, L0_cond_ada_w, L0_cond_ada_b, L0_cond_in_proj_w, L0_cond_conv_w, L0_cond_conv_b, L0_cond_x_proj_w, L0_cond_dt_proj_w, L0_cond_dt_proj_b, L0_cond_A_log, L0_cond_D_param, L0_cond_out_proj_w, L1_cond_norm1_g, L1_cond_norm1_b, L1_cond_norm2_g, L1_cond_norm2_b, L1_cond_Wx, L1_cond_bx, L1_cond_Wz, L1_cond_bz, L1_cond_Wf, L1_cond_bf, L1_cond_Wada, L1_cond_bada, L1_cond_Wc1, L1_cond_bc1, L1_cond_Wc2, L1_cond_bc2, L1_cond_Wdbc1, L1_cond_Wdt1, L1_cond_bdt1, L1_cond_Alog1, L1_cond_Dp1, L1_cond_Wdbc2, L1_cond_Wdt2, L1_cond_bdt2, L1_cond_Alog2, L1_cond_Dp2, L2_cond_norm_scale, L2_cond_norm_bias, L2_cond_Wq, L2_cond_bq, L2_cond_Wk, L2_cond_bk, L2_cond_Wv, L2_cond_bv, L2_cond_film_emb_W, L2_cond_film_emb_b, L2_cond_film_norm_scale, L2_cond_film_norm_bias, L2_cond_film_out_W, L2_cond_film_out_b, L3_cond_norm_w, L3_cond_norm_b, L3_cond_q_w, L3_cond_q_b, L3_cond_k_w, L3_cond_k_b, L3_cond_v_w, L3_cond_v_b, L3_cond_emb_w, L3_cond_emb_b, L3_cond_sb_norm_w, L3_cond_sb_norm_b, L3_cond_out_w, L3_cond_out_b):
    import jax
    import jax.numpy as jnp

    def _L0_cond_ref(x, c, ln_g, ln_b, ada_w, ada_b, in_proj_w, conv_w, conv_b, x_proj_w, dt_proj_w, dt_proj_b, A_log, D_param, out_proj_w):
        import jax, jax.numpy as jnp
        import numpy as np
        D = 256
        DI = 512
        N = 16
        DT_RANK = 64
        D_CONV = 4
        EPS = 1e-05

        def _layernorm(x, g, b):
            mu = jnp.mean(x, axis=-1, keepdims=True)
            var = jnp.mean((x - mu) ** 2, axis=-1, keepdims=True)
            return (x - mu) * jax.lax.rsqrt(var + EPS) * g + b

        def _mamba(xn, in_proj_w, conv_w, conv_b, x_proj_w, dt_proj_w, dt_proj_b, A_log, D_param, out_proj_w):
            b, sl, _ = xn.shape
            xz = jnp.einsum('bsd,ed->bse', xn, in_proj_w)
            x_in, z = jnp.split(xz, 2, axis=-1)
            xt = jnp.transpose(x_in, (0, 2, 1))
            u = jax.lax.conv_general_dilated(xt, conv_w[:, None, :], (1,), [(D_CONV - 1, 0)], feature_group_count=DI, dimension_numbers=('NCH', 'OIH', 'NCH')) + conv_b[None, :, None]
            u = jax.nn.silu(jnp.transpose(u, (0, 2, 1)))
            x_dbl = jnp.einsum('bsd,ed->bse', u, x_proj_w)
            dt_r, B, C = jnp.split(x_dbl, [DT_RANK, DT_RANK + N], axis=-1)
            dt = jax.nn.softplus(jnp.einsum('bsr,dr->bsd', dt_r, dt_proj_w) + dt_proj_b)
            A = -jnp.exp(A_log)

            def step(h, inp):
                dt_t, B_t, C_t, u_t = inp
                dA = jnp.exp(dt_t[:, :, None] * A)
                h = h * dA + (dt_t * u_t)[:, :, None] * B_t[:, None, :]
                y = jnp.einsum('bdn,bn->bd', h, C_t)
                return (h, y)
            seq = (jnp.transpose(dt, (1, 0, 2)), jnp.transpose(B, (1, 0, 2)), jnp.transpose(C, (1, 0, 2)), jnp.transpose(u, (1, 0, 2)))
            h0 = jnp.zeros((b, DI, N), xn.dtype)
            _, ys = jax.lax.scan(step, h0, seq)
            y = jnp.transpose(ys, (1, 0, 2)) + u * D_param
            y = y * jax.nn.silu(z)
            return jnp.einsum('bsd,ed->bse', y, out_proj_w)
        ada = jnp.einsum('bc,ec->be', jax.nn.silu(c), ada_w) + ada_b
        shift, scale, gate = jnp.split(ada, 3, axis=1)
        xn = _layernorm(x, ln_g, ln_b)
        xn = xn * (1.0 + scale[:, None, :]) + shift[:, None, :]
        x_ssm = _mamba(xn, in_proj_w, conv_w, conv_b, x_proj_w, dt_proj_w, dt_proj_b, A_log, D_param, out_proj_w)
        return x + gate[:, None, :] * x_ssm

    def _L1_cond_ref(x, c, w, norm1_g, norm1_b, norm2_g, norm2_b, Wx, bx, Wz, bz, Wf, bf, Wada, bada, Wc1, bc1, Wc2, bc2, Wdbc1, Wdt1, bdt1, Alog1, Dp1, Wdbc2, Wdt2, bdt2, Alog2, Dp2):
        import jax, jax.numpy as jnp
        import numpy as np
        B, S, D, E, N, R = (2, 256, 256, 512, 16, 64)
        EPS = 1e-05

        def _ln(x, g, b):
            m = jnp.mean(x, -1, keepdims=True)
            v = jnp.mean((x - m) ** 2, -1, keepdims=True)
            return (x - m) * jax.lax.rsqrt(v + EPS) * g + b

        def _ssm(u, Wdbc, Wdt, bdt, Alog, Dp):
            dbc = jnp.einsum('bse,re->bsr', u, Wdbc)
            dlt, Bm, Cm = jnp.split(dbc, [R, R + N], axis=-1)
            delta = jax.nn.softplus(jnp.einsum('bsr,er->bse', dlt, Wdt) + bdt)
            A = -jnp.exp(Alog)
            dA = jnp.exp(delta[..., None] * A)
            dBu = delta[..., None] * Bm[:, :, None, :] * u[..., None]

            def step(h, xs):
                dA_t, dBu_t, C_t = xs
                h = dA_t * h + dBu_t
                y = jnp.einsum('ben,bn->be', h, C_t)
                return (h, y)
            h0 = jnp.zeros((u.shape[0], u.shape[2], N), u.dtype)
            _, ys = jax.lax.scan(step, h0, (dA.swapaxes(0, 1), dBu.swapaxes(0, 1), Cm.swapaxes(0, 1)))
            return ys.swapaxes(0, 1) + u * Dp
        ada = jax.nn.silu(c) @ Wada.T + bada
        shift, scale, gate = jnp.split(ada, 3, axis=1)
        x_ssm = _ln(x, norm1_g, norm1_b)
        x_ssm = x_ssm * (1.0 + scale[:, None, :]) + shift[:, None, :]
        skip = x_ssm
        x_ssm = _ln(x_ssm, norm2_g, norm2_b)
        mz = jnp.einsum('bsd,ed->bse', x_ssm, Wz) + bz
        mx = jnp.einsum('bsd,ed->bse', x_ssm, Wx) + bx
        act_mx = jax.nn.silu(mx)
        z1 = jnp.einsum('bse,fe->bsf', mz, Wc1) + bc1
        z1 = _ssm(z1, Wdbc1, Wdt1, bdt1, Alog1, Dp1)
        y1 = act_mx * z1
        z2 = jnp.einsum('bse,fe->bsf', mz, Wc2) + bc2
        z2 = jnp.flip(z2, axis=1)
        z2 = _ssm(z2, Wdbc2, Wdt2, bdt2, Alog2, Dp2)
        z2 = jnp.flip(z2, axis=1)
        y2 = act_mx * z2
        out = jnp.einsum('bse,de->bsd', y1 + y2, Wf) + bf + skip
        return x + gate[:, None, :] * out

    def _L2_cond_ref(x, emb, src_mask, norm_scale, norm_bias, Wq, bq, Wk, bk, Wv, bv, film_emb_W, film_emb_b, film_norm_scale, film_norm_bias, film_out_W, film_out_b):
        import jax, jax.numpy as jnp
        import numpy as np
        H = 16
        LN_EPS = 1e-05

        def _layernorm(x, scale, bias):
            mu = jnp.mean(x, axis=-1, keepdims=True)
            var = jnp.var(x, axis=-1, keepdims=True)
            return (x - mu) * jax.lax.rsqrt(var + LN_EPS) * scale + bias
        B, T, D = x.shape
        dh = D // H
        xn = _layernorm(x, norm_scale, norm_bias)
        q = xn @ Wq + bq
        k = xn @ Wk + bk
        v = xn @ Wv + bv
        mask = (src_mask == 1)[:, :, None]
        k = jnp.where(mask, -jnp.inf, k)
        v = jnp.where(mask, 0.0, v)
        q = q.reshape(B, T, H, dh).transpose(0, 2, 1, 3)
        k = k.reshape(B, T, H, dh).transpose(0, 2, 1, 3)
        v = v.reshape(B, T, H, dh).transpose(0, 2, 1, 3)
        q = jax.nn.softmax(q, axis=-1)
        k = jax.nn.softmax(k, axis=2)
        attn = jnp.einsum('bhse,bhsd->bhed', k, v)
        y = jnp.einsum('bhtd,bhed->bhte', q, attn)
        y = y.transpose(0, 2, 1, 3).reshape(B, T, D)
        emb_out = jax.nn.silu(emb) @ film_emb_W + film_emb_b
        scale, shift = jnp.split(emb_out, 2, axis=-1)
        h = _layernorm(y, film_norm_scale, film_norm_bias) * (1.0 + scale[:, None, :]) + shift[:, None, :]
        h = jax.nn.silu(h) @ film_out_W + film_out_b
        return x + h

    def _L3_cond_ref(x, emb, src_mask, norm_w, norm_b, q_w, q_b, k_w, k_b, v_w, v_b, emb_w, emb_b, sb_norm_w, sb_norm_b, out_w, out_b):
        import jax, jax.numpy as jnp
        import numpy as np
        B, T, D, H, TE = (8, 256, 256, 16, 512)
        LN_EPS = 1e-05

        def layer_norm(x, w, b):
            m = jnp.mean(x, axis=-1, keepdims=True)
            v = jnp.var(x, axis=-1, keepdims=True)
            return (x - m) / jnp.sqrt(v + LN_EPS) * w + b
        Bx, Tx, Dx = x.shape
        xn = layer_norm(x, norm_w, norm_b)
        q = (xn @ q_w + q_b).reshape(Bx, Tx, H, -1)
        k = (xn @ k_w + k_b).reshape(Bx, Tx, H, -1)
        att = jnp.einsum('bnhl,bmhl->bnmh', q, k)
        mask = src_mask.reshape(Bx, 1, Tx, 1)
        att = att + (1.0 - mask) * -1000000.0
        att = jax.nn.softmax(att, axis=2)
        v = ((xn @ v_w + v_b) * src_mask[:, :, None]).reshape(Bx, Tx, H, -1)
        y = jnp.einsum('bnmh,bmhl->bnhl', att, v).reshape(Bx, Tx, Dx)
        e = jax.nn.silu(emb) @ emb_w + emb_b
        scale, shift = jnp.split(e[:, None, :], 2, axis=2)
        h = layer_norm(y, sb_norm_w, sb_norm_b) * (1.0 + scale) + shift
        h = jax.nn.silu(h) @ out_w + out_b
        return x + h
    x = _L0_cond_ref(x, cond_2048, L0_cond_ln_g, L0_cond_ln_b, L0_cond_ada_w, L0_cond_ada_b, L0_cond_in_proj_w, L0_cond_conv_w, L0_cond_conv_b, L0_cond_x_proj_w, L0_cond_dt_proj_w, L0_cond_dt_proj_b, L0_cond_A_log, L0_cond_D_param, L0_cond_out_proj_w)
    x = _L1_cond_ref(x, cond_2048, cond_1024, L1_cond_norm1_g, L1_cond_norm1_b, L1_cond_norm2_g, L1_cond_norm2_b, L1_cond_Wx, L1_cond_bx, L1_cond_Wz, L1_cond_bz, L1_cond_Wf, L1_cond_bf, L1_cond_Wada, L1_cond_bada, L1_cond_Wc1, L1_cond_bc1, L1_cond_Wc2, L1_cond_bc2, L1_cond_Wdbc1, L1_cond_Wdt1, L1_cond_bdt1, L1_cond_Alog1, L1_cond_Dp1, L1_cond_Wdbc2, L1_cond_Wdt2, L1_cond_bdt2, L1_cond_Alog2, L1_cond_Dp2)
    x = _L2_cond_ref(x, cond_2048, mask_BxS_ik0, L2_cond_norm_scale, L2_cond_norm_bias, L2_cond_Wq, L2_cond_bq, L2_cond_Wk, L2_cond_bk, L2_cond_Wv, L2_cond_bv, L2_cond_film_emb_W, L2_cond_film_emb_b, L2_cond_film_norm_scale, L2_cond_film_norm_bias, L2_cond_film_out_W, L2_cond_film_out_b)
    x = _L3_cond_ref(x, cond_2048, mask_BxS_ff1, L3_cond_norm_w, L3_cond_norm_b, L3_cond_q_w, L3_cond_q_b, L3_cond_k_w, L3_cond_k_b, L3_cond_v_w, L3_cond_v_b, L3_cond_emb_w, L3_cond_emb_b, L3_cond_sb_norm_w, L3_cond_sb_norm_b, L3_cond_out_w, L3_cond_out_b)
    return x

_drawn_inputs = setup_inputs


def setup_inputs(seed=0):
    import zlib

    import numpy as np

    out = dict(_drawn_inputs(seed))
    spreads = {'L0_cond_ln_g': (1.0, 0.2),
     'L0_cond_ln_b': (0.0, 0.1),
     'L0_cond_ada_b': (0.0, 0.1),
     'L0_cond_conv_b': (0.0, 0.1),
     'L0_cond_D_param': (1.0, 0.2),
     'L1_cond_norm1_g': (1.0, 0.2),
     'L1_cond_norm1_b': (0.0, 0.1),
     'L1_cond_norm2_g': (1.0, 0.2),
     'L1_cond_norm2_b': (0.0, 0.1),
     'L1_cond_bx': (0.0, 0.1),
     'L1_cond_bz': (0.0, 0.1),
     'L1_cond_bf': (0.0, 0.1),
     'L1_cond_bada': (0.0, 0.1),
     'L1_cond_bc1': (0.0, 0.1),
     'L1_cond_bc2': (0.0, 0.1),
     'L1_cond_bdt1': (0.0, 0.1),
     'L1_cond_Dp1': (1.0, 0.2),
     'L1_cond_bdt2': (0.0, 0.1),
     'L1_cond_Dp2': (1.0, 0.2),
     'L2_cond_norm_scale': (1.0, 0.2),
     'L2_cond_norm_bias': (0.0, 0.1),
     'L2_cond_bq': (0.0, 0.1),
     'L2_cond_bk': (0.0, 0.1),
     'L2_cond_bv': (0.0, 0.1),
     'L2_cond_film_emb_b': (0.0, 0.1),
     'L2_cond_film_norm_scale': (1.0, 0.2),
     'L2_cond_film_norm_bias': (0.0, 0.1),
     'L2_cond_film_out_b': (0.0, 0.1),
     'L3_cond_norm_w': (1.0, 0.2),
     'L3_cond_norm_b': (0.0, 0.1),
     'L3_cond_q_b': (0.0, 0.1),
     'L3_cond_k_b': (0.0, 0.1),
     'L3_cond_v_b': (0.0, 0.1),
     'L3_cond_emb_b': (0.0, 0.1),
     'L3_cond_sb_norm_w': (1.0, 0.2),
     'L3_cond_sb_norm_b': (0.0, 0.1),
     'L3_cond_out_b': (0.0, 0.1)}
    factors = {}
    for name, (base, spread) in spreads.items():
        noise = np.random.default_rng([zlib.crc32(name.encode()), seed]).standard_normal(out[name].shape)
        drawn = base * np.exp(spread * noise) if base else spread * noise
        out[name] = jnp.asarray(drawn.astype(out[name].dtype))
    for name, factor in factors.items():
        out[name] = (out[name] * factor).astype(out[name].dtype)
    return out
```

```python
import concourse.bass as bass
import concourse.mybir as mybir
from concourse.alu_op_type import AluOpType as ALU
from contextlib import ExitStack

F32 = mybir.dt.float32
BF16 = mybir.dt.bfloat16
I32 = mybir.dt.int32
ACT = mybir.ActivationFunctionType
AX = mybir.AxisListType

P = 128
BATCH = 2
SEQ = 1024
D = 256
DI = 512
NS = 16
RANK = 64
CONV = 4
HEADS = 16
HD = D // HEADS
EPS = 1e-5
KD = D // P
KE = DI // P
TT = SEQ // P
TC = 512
CHUNKS = SEQ // TC
XP = RANK + 2 * NS
PAIRS = KE // 2

C_CONVW, C_CONVB, C_DTB, C_A = 0, 16, 20, 32
C_D = 24
C_BX, C_BZ, C_BC, C_BDT, C_D1, C_A1 = 96, 100, 104, 112, 120, 128
C_BK2, C_BQ3, C_BK3 = 256, 258, 260
NCOLS = 262

R_G0, R_B0, R_G1, R_B1, R_G2, R_B2, R_BF = 0, 256, 512, 768, 1024, 1280, 1536
R_NG, R_NB, R_FG, R_FB, R_BQ, R_BV, R_OB = 0, 256, 512, 768, 1024, 1280, 1536
NROWS = 1792
ADA = [768, 768, 512, 512]
ADA0 = [0, 768, 1536, 2048]
NADA = sum(ADA)
ADA_PIECES = [[(0, 384), (384, 384)], [(768, 384), (1152, 384), (1536, 512), (2048, 512)]]
NREST = NADA - ADA[0]

W0_IN, W0_XP, W0_OUT, NW0 = 0, KD * 2 * DI, KD * 2 * DI + KE * XP, KD * 2 * DI + KE * XP + KE * D
W1_X, W1_Z = 0, KD * DI
W1_C = 2 * KD * DI
W1_XP = W1_C + 2 * KE * DI
W1_F = W1_XP + 2 * KE * XP
NW1 = W1_F + KE * D
WA_Q, WA_K, WA_V, WA_O, NWA = 0, KD * D, 2 * KD * D, 3 * KD * D, 4 * KD * D

TERMS = [(0, 0), (0, 1), (1, 0), (1, 1), (0, 2), (2, 0)]
K_MAX = len(TERMS) * HD + 3
K_EXP = K_MAX + 3
MASKED = -1000000.0
LAYERS = 4
NEVER = -1e30

STAGES = [("ada", 0, len(ADA_PIECES[0]))]
for _b in range(BATCH):
    STAGES += [("0xT", _b, 4), ("0in", _b, 16), ("0xp", _b, 2), ("0dt", _b, 8), ("0out", _b, 4)]
    if _b == 0:
        STAGES += [("ada", 1, len(ADA_PIECES[1]))]
for _b in range(BATCH):
    STAGES += [("1xT", _b, 4), ("1xz", _b, 16), ("1c", _b, 16)]
    for _d in range(2):
        STAGES += [(f"1xp{_d}", _b, 2), (f"1dt{_d}", _b, 8)]
    STAGES += [("1out", _b, 4)]
for _b in range(BATCH):
    STAGES += [("2xT", _b, 4), ("2q", _b, 4), ("2v", _b, 4), ("2kT", _b, 4), ("2k", _b, 4), ("2m", _b, 1),
               ("2qT", _b, 4), ("2y", _b, 4), ("2hT", _b, 4), ("2out", _b, 4)]
for _b in range(BATCH):
    STAGES += [("3xT", _b, 4), ("3qT", _b, 4), ("3kT", _b, 4), ("3v", _b, 4), ("3mx", _b, 1), ("3hT", _b, 4),
               ("3out", _b, 4)]
FIRST = {}
_n = 0
for _name, _b, _count in STAGES:
    FIRST[_name, _b] = _n
    _n += _count


def build(nc, x, cond_t, cols_in, rows_in, ada_w, ada_b, w0, w1, wdt, w23, mask2_row, mask2_col, mask3_row, mask3_col,
          out):
    ctx = ExitStack()
    with ctx:
        def sb(name, shape, dt=F32):
            return ctx.enter_context(nc.sbuf_tensor(name, shape, dt))

        def sem(name):
            return ctx.enter_context(nc.semaphore(name))

        xt = sb("xt", [P, BATCH * TT, D])
        slots = sb("slots", [P, 5, KE * SEQ])
        wl1 = sb("wl1", [P, max(NW1, 4 * TT * D)])
        wdts = sb("wdts", [RANK, 3, DI])
        wl23 = sb("wl23", [P, 2, NWA])
        rows = sb("rows", [P, NROWS])
        ada = sb("ada", [P, BATCH, 768])
        cols = sb("cols", [P, NCOLS])
        hbuf = sb("hbuf", [P, 2, KE, TC])
        cbuf = sb("cbuf", [P, 2, TC])
        hlast = sb("hlast", [P, KE, NS])
        bcs = sb("bcs", [3 * 2 * NS, SEQ], BF16)
        ident = sb("ident", [P, P])
        pick = sb("pick", [3 * 2 * NS, 2 * NS], BF16)
        heads = sb("heads", [P, P])
        diag_d = sb("diag_d", [P, 3, KE, P])
        stats = sb("stats", [P, TT, 6])
        mv = sb("mv", [P, TT, 2])
        std = sb("std", [P, TT])
        rstd = sb("rstd", [P, TT])
        gain = sb("gain", [P, D])
        shift = sb("shift", [P, D])
        sct = sb("sct", [P, KE, BATCH])
        eps = sb("eps", [P, 1])
        keep2 = sb("keep2", [P, BATCH * TT])
        m2c = sb("m2c", [P, BATCH * TT], I32)
        m3c = sb("m3c", [P, BATCH * TT])
        small = sb("small", [P, 8])
        head_scale = sb("head_scale", [P, 32])
        psum = ctx.enter_context(nc.psum_tensor("psum", [P, 8, 512], F32))

        scr_ada = nc.dram_tensor("scr_ada", [BATCH, NADA], F32)
        scr_qk = nc.dram_tensor("scr_qk", [2, 3, D, SEQ], BF16)
        scr_mask = nc.dram_tensor("scr_mask", [3, SEQ], BF16)
        scr_max = nc.dram_tensor("scr_max", [3, HEADS * TT, P], BF16)

        A, B, C, E, F = range(5)

        def chan(s):
            return slots[:, s, :].rearrange("p (e t) -> p e t", e=KE)

        def tok(s, half):
            return slots[:, s, half * TT * D:(half + 1) * TT * D].rearrange("p (i d) -> p i d", i=TT)

        def wide(s, half):
            return slots[:, s, half * KD * SEQ:(half + 1) * KD * SEQ].rearrange("p (k t) -> p k t", k=KD)

        def per_token(v):
            return v.rearrange("p (i o) -> p i o", o=1).to_broadcast([P, TT, D])

        def per_column(v):
            return v.rearrange("p (o d) -> p o d", o=1).to_broadcast([P, TT, D])

        w0s = slots[:, F, :]
        adaw = [slots[:, A, 0:KE * ADA[0]].rearrange("p (k n) -> p k n", k=KE),
                wl1[:, 0:KE * NREST].rearrange("p (k n) -> p k n", k=KE)]
        hflat = hbuf[:, :, :, :].rearrange("p a e t -> p (a e t)")
        adas = [hflat[0:BATCH, 0:ADA[0]], wl23[0:BATCH, 0, 0:NREST]]
        adab = [slots[0:BATCH, E, 0:ADA[0]], wl23[0:BATCH, 1, 0:NREST]]
        xp_out = hflat[0:XP, 0:SEQ]
        dt_low, bc_raw, bc_rest = xp_out[0:RANK, :], xp_out[RANK:XP, :], hflat[RANK:XP, SEQ:2 * SEQ]
        bc_hi = hflat[RANK:XP, 2 * SEQ:2 * SEQ + SEQ // 2].bitcast(BF16)
        bc_mid = hflat[RANK:XP, 2 * SEQ + SEQ // 2:3 * SEQ].bitcast(BF16)
        SCANS = [("0", 0, 0, C, False), ("0", 1, 0, C, False)]
        for b in range(BATCH):
            SCANS += [("1", b, 1, C, False), ("1", b, 2, F, True)]

        ld_x, ld_ada = ([sem(f"{n}{i}") for i in range(2)] for n in ("ld_x", "ld_ada"))
        ld_small, ld_w0, ld_w1, ld_w23 = (sem(n) for n in ("ld_small", "ld_w0", "ld_w1", "ld_w23"))
        ld_rows, ld_adarows = sem("ld_rows"), sem("ld_adarows")
        made, consts_ready = sem("made"), sem("consts_ready")
        prod, evac = sem("prod"), sem("evac")
        dve_step, act_step, pool_step = sem("dve_step"), sem("act_step"), sem("pool_step")
        sct_ready, ada_ready, ada_stored = sem("sct_ready"), sem("ada_ready"), sem("ada_stored")
        cols_ready = sem("cols_ready")
        a_ready = sem("a_ready")
        var_ready, std_ready, xn_ready = sem("var_ready"), sem("std_ready"), sem("xn_ready")
        conv_ready, u_ready = sem("conv_ready"), sem("u_ready")
        bc_ready, skip_added = sem("bc_ready"), sem("skip_added")
        abs_ready, exp_ready, log_ready, dt_ready, w_ready = (sem(n) for n in (
            "abs_ready", "exp_ready", "log_ready", "dt_ready", "w_ready"))
        bcast, c_out = sem("bcast"), sem("c_out")
        dbu, decay = sem("dbu"), sem("decay")
        scanned, weighed, summed = sem("scanned"), sem("weighed"), sem("summed")
        saved = sem("saved")
        y_out = sem("y_out")
        both_added, gated, x_updated = sem("both_added"), sem("gated"), sem("x_updated")
        rows_used = sem("rows_used")
        stored = sem("stored")
        ld_mask2, q_shifted, q_exp, qn_ready = sem("ld_mask2"), sem("q_shifted"), sem("q_exp"), sem("qn_ready")
        v_ready, k_masked, k_exp, kn_ready = sem("v_ready"), sem("k_masked"), sem("k_exp"), sem("kn_ready")
        outer_ready, h_conditioned, h_ready = sem("outer_ready"), sem("h_conditioned"), sem("h_ready")
        ld_mask3, mask_split, qk_split, parts_stored = sem("ld_mask3"), sem("mask_split"), sem("qk_split"), sem("parts_stored")
        ones_set, ld_stack, scored, maxed = sem("ones_set"), sem("ld_stack"), sem("scored"), sem("maxed")
        max_split, max_stored, ld_max = sem("max_split"), sem("max_stored"), sem("ld_max")
        v_aug_ready, v_quad_ready = sem("v_aug_ready"), sem("v_quad_ready")
        shifted, exped, weighed_v = sem("shifted"), sem("exped"), sem("weighed_v")
        o_out, o_turned, inverted, normalized = sem("o_out"), sem("o_turned"), sem("inverted"), sem("normalized")

        q2, v2, k2T, k2, q2T, y2, h2T = tok(B, 0), tok(B, 1), wide(C, 0), tok(E, 0), wide(E, 1), tok(F, 0), wide(F, 1)
        slot_c = slots[:, C, 2 * SEQ:4 * SEQ]
        outer = slot_c[:, 0:KD * P].rearrange("p (k e) -> p k e", k=KD)
        never = slot_c[:, 256:256 + SEQ]
        head_max = slot_c[:, 1280:1280 + TT * HEADS]
        head_inv = slot_c[:, 1408:1408 + TT * HEADS]
        mask2 = cbuf[:, :, :].rearrange("p a t -> p (a t)").bitcast(I32)
        k_neg_max, k_den, k_inv = small[:, 0:KD], small[:, KD:2 * KD], small[:, 2 * KD:3 * KD]

        def part(flat, dims, **kw):
            return flat.rearrange(dims, **kw)

        x3, x3T = part(wl1[:, 0:2048], "p (i d) -> p i d", i=TT), part(wl1[:, 2048:4096], "p (k t) -> p k t", k=KD)
        q3T, k3T = (part(wl1[:, a:a + 2048], "p (k t) -> p k t", k=KD) for a in (4096, 6144))
        v3 = part(hflat[:, 0:2048], "p (i d) -> p i d", i=TT)
        rest3 = wl1[:, 0:2048]
        q_parts = [slots[:, F, n * 1024:n * 1024 + 1024].bitcast(BF16) for n in range(3)]
        k_parts = [slots[:, F, 3072:4096].bitcast(BF16), hflat[:, 2048:3072].bitcast(BF16), hflat[:, 3072:4096].bitcast(BF16)]
        q_rows = part(slots[:, A:B + 1, :], "p s n -> p (s n)").bitcast(BF16).rearrange("p (h t) -> p h t", h=HEADS)
        k_rows = part(slots[:, C:E + 1, :], "p s n -> p (s n)").bitcast(BF16).rearrange("p (h t) -> p h t", h=HEADS)
        v_aug = part(wl1[:, 4096:8192], "p (i h c) -> p i h c", i=TT, h=HEADS)
        v_quad = part(wl1[:, 0:1024], "p (i c) -> p i c", i=TT)
        oT = wl1[:, 1024:2048]
        y3 = part(wl1[:, 2048:4096], "p (i d) -> p i d", i=TT)
        h3T = part(wl1[:, 4096:6144], "p (k t) -> p k t", k=KD)
        o3 = x3
        probs = slots[:, F, :].rearrange("p (n t) -> p n t", n=4)
        row_max, neg_max = gain[:, 0:P], gain[:, P:2 * P]
        max_rest = shift[:, 0:P]
        max_parts = [shift[:, P:P + 64].bitcast(BF16), shift[:, P + 64:2 * P].bitcast(BF16), heads[:, 0:64].bitcast(BF16)]
        inv3 = head_scale[:, :].rearrange("p (i h) -> p i h", i=TT)
        QUADS, QH = HEADS // 4, 4
        UNITS = QH * TT

        def sync_layer2(sp):
            for b in range(BATCH):
                if b:
                    sp.wait_ge(k_masked, b)
                sp.dma_start(mask2, mask2_row[b:b + 1, :].to_broadcast([P, SEQ])).then_inc(ld_mask2, 16)

        def sync_layer3(sp):
            for b in range(BATCH):
                if b:
                    sp.wait_ge(x_updated, 3 * BATCH + b)
                sp.dma_start(bc_raw, mask3_row[b:b + 1, :].to_broadcast([XP - RANK, SEQ])).then_inc(ld_mask3, 16)
                sp.wait_ge(mask_split, b + 1)
                for n in range(3):
                    sp.dma_start(scr_mask[n:n + 1, :], bcs[32 * n:32 * n + 1, :]).then_inc(parts_stored, 16)
                for side, parts in enumerate((q_parts, k_parts)):
                    sp.wait_ge(qk_split, 2 * b + side + 1)
                    for n in range(3):
                        sp.dma_start(scr_qk[side, n].rearrange("(k p) t -> p k t", p=P),
                                     parts[n].rearrange("p (k t) -> p k t", k=KD)).then_inc(parts_stored, 16)
                sp.wait_ge(parts_stored, 16 * 9 * (b + 1))
                sp.wait_ge(ones_set, b + 1)
                for r, pair in enumerate(TERMS):
                    for side, dst in enumerate((q_rows, k_rows)):
                        sp.dma_start(dst[r * HD:(r + 1) * HD, :, :],
                                     scr_qk[side, pair[side]].rearrange("(h d) t -> d h t", d=HD)).then_inc(ld_stack, 16)
                mask_src = scr_mask[:, :].rearrange("r (o t) -> r o t", o=1).to_broadcast([3, HEADS, SEQ])
                sp.dma_start(k_rows[K_MAX - 3:K_MAX, :, :], mask_src).then_inc(ld_stack, 16)
                sp.wait_ge(max_split, b + 1)
                for n in range(3):
                    sp.dma_start(scr_max[n], max_parts[n]).then_inc(max_stored, 16)
                sp.wait_ge(max_stored, 48 * (b + 1))
                sp.dma_start(q_rows[K_MAX:K_EXP, :, :], scr_max[:, :, :].rearrange("r (h i) n -> r h (i n)", i=TT)).then_inc(ld_max, 16)

        def pool_chunk(pool, s, c):
            cc = s * CHUNKS + c

            def state(n, k):
                pool.wait_ge(c_out, cc * NS + n + 1)
                for p in range(PAIRS):
                    if c < CHUNKS - 1:
                        pool.wait_ge(saved, s * (CHUNKS - 1) * NS * PAIRS + n * PAIRS + p + 1)
                    else:
                        pool.wait_ge(scanned, cc * NS * KE + n * KE + 2 * p + 2)
                    h = hbuf[:, k, 2 * p:2 * p + 2, :]
                    pool.tensor_tensor(h, h, cbuf[:, k:k + 1, :].to_broadcast([P, 2, TC]), ALU.mult).then_inc(weighed, 1)

            with pool.Fori(0, NS // 2) as i:
                for k in range(2):
                    state(i * 2 + k, k)

        def pool_attention(pool):
            for b in range(BATCH):
                pool.wait_ge(qk_split, 2 * b + 2)
                pool.memset(q_rows[96:K_EXP, :, :], 1.0)
                pool.memset(k_rows[96:K_EXP, :, :], 1.0).then_inc(ones_set, 1)
                pool.wait_ge(ones_set, b + 1)
                pool.wait_ge(v_aug_ready, b + 1)
                with pool.Fori(0, QUADS) as quad:
                    pool.wait_ge(weighed_v, quad * UNITS + (b * QUADS * UNITS + 4))
                    for h in range(QH):
                        ins = pool.tensor_copy(v_quad[:, :, h * 32:h * 32 + 32], v_aug[:, :, bass.ds(quad * QH + h, 1), :]
                                               .rearrange("p i o c -> p i (o c)"))
                    ins.then_inc(v_quad_ready, 1)

        def tensor_attention(pe, bank, to_wide, project, to_tokens):
            w2, w3 = (wl23[:, n, :].rearrange("p (w k m) -> p w k m", w=4, k=KD) for n in range(2))
            if LAYERS < 3:
                return
            pe.wait_ge(ld_w23, 48)
            for b in range(BATCH):
                pe.wait_ge(xn_ready, 2 * BATCH + b + 1)
                to_wide(FIRST["2xT", b], tok(A, 0))
                pe.wait_ge(evac, FIRST["2q", b])
                to_tokens(FIRST["2q", b], wide(A, 1), w2[:, 0], KD)
                to_tokens(FIRST["2v", b], wide(A, 1), w2[:, 2], KD)
                project(FIRST["2kT", b], w2[:, 1], wide(A, 1), KD, KD)
                pe.wait_ge(kn_ready, b + 1)
                g = FIRST["2k", b]
                for pair in range(TT // 2):
                    ps = bank(g)
                    for q in range(2):
                        t0 = (pair * 2 + q) * P
                        for k in range(KD):
                            last = pe.transpose(ps[:, q * D + k * P:q * D + (k + 1) * P], k2T[:, k, t0:t0 + P], ident[:, :])
                    last.then_inc(prod, 1)
                    g += 1
                pe.wait_ge(evac, FIRST["2m", b])
                pe.wait_ge(v_ready, b + 1)
                ps = bank(g)
                for k in range(KD):
                    for i in range(TT):
                        last = pe.matmul(ps[:, k * P:(k + 1) * P], v2[:, i, k * P:(k + 1) * P], k2[:, i, k * P:(k + 1) * P],
                                         start=i == 0, stop=i == TT - 1)
                last.then_inc(prod, 1)
                pe.wait_ge(qn_ready, b + 1)
                to_wide(FIRST["2qT", b], q2)
                pe.wait_ge(evac, FIRST["2y", b])
                pe.wait_ge(outer_ready, b + 1)
                g = FIRST["2y", b]
                for pair in range(TT // 2):
                    ps = bank(g)
                    for q in range(2):
                        t0 = (pair * 2 + q) * P
                        for k in range(KD):
                            last = pe.matmul(ps[:, q * D + k * P:q * D + (k + 1) * P], q2T[:, k, t0:t0 + P], outer[:, k, :],
                                             start=True, stop=True)
                    last.then_inc(prod, 1)
                    g += 1
                film_products(pe, "2", b, b, y2, h2T, w2[:, 3], to_wide, to_tokens)
            if LAYERS < 4:
                return
            pe.sem_inc(weighed_v, 4)
            for b in range(BATCH):
                pe.wait_ge(xn_ready, 3 * BATCH + b + 1)
                to_wide(FIRST["3xT", b], x3)
                pe.wait_ge(evac, FIRST["3qT", b])
                project(FIRST["3qT", b], w3[:, 0], x3T, KD, KD)
                project(FIRST["3kT", b], w3[:, 1], x3T, KD, KD)
                to_tokens(FIRST["3v", b], x3T, w3[:, 2], KD)
                pe.wait_ge(evac, FIRST["3mx", b])
                pe.wait_ge(ld_stack, 16 * (2 * len(TERMS) + 1) * (b + 1))
                with pe.Fori(0, HEADS) as h:
                    for i in range(TT):
                        pe.wait_ge(maxed, h * TT + (b * HEADS * TT + i + 1))
                        for half in range(2):
                            last = pe.matmul(psum[:, i % 4 * 2 + half, :],
                                             q_rows[0:K_MAX, bass.ds(h, 1), i * P:(i + 1) * P].rearrange("p o t -> p (o t)"),
                                             k_rows[0:K_MAX, bass.ds(h, 1), half * 512:half * 512 + 512].rearrange("p o t -> p (o t)"),
                                             start=True, stop=True)
                        last.then_inc(scored, 1)
                pe.wait_ge(maxed, (b + 1) * HEADS * TT + 4)
                pe.transpose(bank(FIRST["3mx", b])[:, 0:P], row_max, ident[:, :]).then_inc(prod, 1)
                pe.wait_ge(evac, FIRST["3mx", b] + 1)
                pe.wait_ge(ld_max, 16 * (b + 1))
                with pe.Fori(0, QUADS) as quad:
                    def scores(u):
                        i, h = u // QH, u % QH
                        pe.wait_ge(exped, quad * UNITS + (b * QUADS * UNITS + u + 1))
                        for half in range(2):
                            last = pe.matmul(psum[:, 2 + u % 3 * 2 + half, :],
                                             k_rows[0:K_EXP, bass.ds(quad * QH + h, 1), i * P:(i + 1) * P].rearrange("p o t -> p (o t)"),
                                             q_rows[0:K_EXP, bass.ds(quad * QH + h, 1), half * 512:half * 512 + 512].rearrange("p o t -> p (o t)"),
                                             start=True, stop=True)
                        last.then_inc(shifted, 1)

                    def weigh(u):
                        i, h = u // QH, u % QH
                        pe.wait_ge(exped, quad * UNITS + (b * QUADS * UNITS + u + 4))
                        for half in range(2):
                            last = pe.matmul(psum[h * 32:h * 32 + 32, half, :], v_quad[:, i, h * 32:h * 32 + 32],
                                             probs[:, u % 4, half * 512:half * 512 + 512], start=i == 0, stop=i == TT - 1)
                        last.then_inc(weighed_v, 1)

                    pe.wait_ge(normalized, quad + (b * QUADS + 1))
                    scores(0)
                    scores(1)
                    pe.wait_ge(v_quad_ready, quad + (b * QUADS + 1))
                    pe.wait_ge(o_out, quad + (b * QUADS + 1))
                    for u in range(UNITS):
                        if u + 2 < UNITS:
                            scores(u + 2)
                        weigh(u)
                    pe.wait_ge(o_out, quad + (b * QUADS + 2))
                    for i in range(TT):
                        last = pe.transpose(psum[:, 2 + i // 4, i % 4 * P:(i % 4 + 1) * P], oT[:, i * P:(i + 1) * P], ident[:, :])
                    last.then_inc(o_turned, 1)
                pe.wait_ge(normalized, (b + 1) * QUADS + 1)
                film_products(pe, "3", b, BATCH + b, y3, h3T, w3[:, 3], to_wide, to_tokens)

        def film_products(pe, layer, b, n, h, hT, w, to_wide, to_tokens):
            pe.wait_ge(h_ready, n + 1)
            to_wide(FIRST[layer + "hT", b], h)
            pe.wait_ge(evac, FIRST[layer + "out", b])
            to_tokens(FIRST[layer + "out", b], hT, w, KD)

        def scalar_attention(act, move, wide_out, tokens_out, project_out, deviation, link):
            if LAYERS < 3:
                return
            for b in range(BATCH):
                deviation()
                wide_out(FIRST["2xT", b], wide(A, 1))
                tokens_out(FIRST["2q", b], q2)
                tokens_out(FIRST["2v", b], v2)
                project_out(FIRST["2kT", b], k2T, KD, bias=C_BK2)
                act.wait_ge(q_shifted, b + 1)
                act.activation(slots[:, B, 0:2 * SEQ], slots[:, B, 0:2 * SEQ], ACT.Exp).then_inc(q_exp, 1)
                act.wait_ge(k_masked, b + 1)
                for k in range(KD):
                    ins = act.activation(k2T[:, k, :], k2T[:, k, :], ACT.Exp, bias=k_neg_max[:, k:k + 1],
                                         accum_out=k_den[:, k:k + 1])
                ins.then_inc(k_exp, 1)
                tokens_out(FIRST["2k", b], k2)
                g = FIRST["2m", b]
                move(g, outer, psum[:, g % 8, 0:KD * P].rearrange("p (k e) -> p k e", k=KD))
                wide_out(FIRST["2qT", b], q2T)
                tokens_out(FIRST["2y", b], y2)
                film_moves(act, "2", b, b, y2, h2T, tok(A, 0), wide_out, tokens_out, deviation)
            if LAYERS < 4:
                return
            act.sem_inc(exped, 3)
            for b in range(BATCH):
                deviation()
                wide_out(FIRST["3xT", b], x3T)
                project_out(FIRST["3qT", b], q3T, KD, bias=C_BQ3)
                project_out(FIRST["3kT", b], k3T, KD, bias=C_BK3)
                act.wait_ge(mask_split, b + 1)
                tokens_out(FIRST["3v", b], v3)
                g = FIRST["3mx", b]
                move(g, neg_max, psum[:, g % 8, 0:P], scale=-1.0)
                with act.Fori(0, QUADS) as quad:
                    for u in range(UNITS):
                        act.wait_ge(shifted, quad * UNITS + (b * QUADS * UNITS + u + 1))
                        act.wait_ge(weighed_v, quad * UNITS + (b * QUADS * UNITS + u + 1))
                        act.activation(probs[:, u % 4, :], psum[:, 2 + u % 3 * 2:4 + u % 3 * 2, :].rearrange("p a t -> p (a t)"),
                                       ACT.Exp).then_inc(exped, 1)
                film_moves(act, "3", b, BATCH + b, y3, h3T, o3, wide_out, tokens_out, deviation)

        def film_moves(act, layer, b, n, h, hT, o, wide_out, tokens_out, deviation):
            deviation()
            act.wait_ge(h_conditioned, n + 1)
            act.activation(h, h, ACT.Silu).then_inc(h_ready, 1)
            wide_out(FIRST[layer + "hT", b], hT)
            tokens_out(FIRST[layer + "out", b], o)

        def vector_attention(dve, link, normalize, condition, split_rows):
            def affine(t, at):
                link(dve.tensor_tensor(t, t, per_column(rows[:, at:at + D]), ALU.mult))
                return dve.tensor_tensor(t, t, per_column(rows[:, at + D:at + 2 * D]), ALU.add)

            def film(layer, b, n, h, o):
                normalize(h, h)
                condition((ada[:, b, 0:D], ada[:, b, D:2 * D]), b, R_FG, R_FB, h).then_inc(h_conditioned, 1)
                dve.wait_ge(evac, FIRST[layer + "out", b] + 4)
                xb = xt[:, b * TT:(b + 1) * TT, :]
                link(dve.tensor_tensor(o, o, per_column(rows[:, R_OB:R_OB + D]), ALU.add))
                dve.tensor_tensor(xb, xb, o, ALU.add).then_inc(x_updated, 1)
                dve.wait_ge(x_updated, int(layer) * BATCH + b + 1)

            by_head = lambda t: t.rearrange("p i (h d) -> p (i h) d", d=HD)
            over_head = lambda v: v.rearrange("p (n o) -> p n o", o=1).to_broadcast([P, TT * HEADS, HD])
            if LAYERS < 3:
                return
            dve.wait_ge(x_updated, 2 * BATCH)
            dve.sem_inc(rows_used, 1)
            dve.wait_ge(ld_w23, 48)
            dve.tensor_scalar(keep2[:, :], m2c[:, :], 1.0, None, ALU.not_equal)
            for b in range(BATCH):
                xb = xt[:, b * TT:(b + 1) * TT, :]
                normalize(xb, tok(A, 0))
                if b == 0:
                    dve.wait_ge(ld_rows, 32)
                    dve.wait_ge(ld_adarows, 96)
                affine(tok(A, 0), R_NG).then_inc(xn_ready, 1)
                dve.wait_ge(ld_mask2, 16 * (b + 1))
                dve.tensor_scalar(never, mask2, 1.0, NEVER, ALU.is_equal, ALU.mult)
                dve.wait_ge(evac, FIRST["2q", b] + 4)
                link(dve.tensor_tensor(q2, q2, per_column(rows[:, R_BQ:R_BQ + D]), ALU.add))
                link(dve.tensor_reduce(head_max, by_head(q2), AX.X, ALU.max))
                dve.tensor_tensor(by_head(q2), by_head(q2), over_head(head_max), ALU.subtract).then_inc(q_shifted, 1)
                dve.wait_ge(evac, FIRST["2v", b] + 4)
                link(dve.tensor_tensor(v2, v2, per_column(rows[:, R_BV:R_BV + D]), ALU.add))
                dve.tensor_tensor(v2, v2, per_token(keep2[:, b * TT:(b + 1) * TT]), ALU.mult).then_inc(v_ready, 1)
                dve.wait_ge(evac, FIRST["2kT", b] + 4)
                link(dve.tensor_tensor(k2T, k2T, never.rearrange("p (o t) -> p o t", o=1).to_broadcast([P, KD, SEQ]), ALU.add))
                dve.tensor_reduce(k_neg_max, k2T, AX.X, ALU.max, negate=True).then_inc(k_masked, 1)
                dve.wait_ge(q_exp, b + 1)
                link(dve.tensor_reduce(head_inv, by_head(q2), AX.X, ALU.add))
                link(dve.reciprocal(head_inv, head_inv))
                dve.tensor_tensor(by_head(q2), by_head(q2), over_head(head_inv), ALU.mult).then_inc(qn_ready, 1)
                dve.wait_ge(k_exp, b + 1)
                link(dve.reciprocal(k_inv, k_den))
                for k in range(KD):
                    ins = dve.tensor_scalar(k2T[:, k, :], k2T[:, k, :], k_inv[:, k:k + 1], None, ALU.mult)
                ins.then_inc(kn_ready, 1)
                dve.wait_ge(evac, FIRST["2m", b] + 1)
                dve.tensor_tensor(outer, outer, heads[:, :].rearrange("p (o e) -> p o e", o=1).to_broadcast([P, KD, P]),
                                  ALU.mult).then_inc(outer_ready, 1)
                dve.wait_ge(evac, FIRST["2y", b] + 4)
                film("2", b, b, y2, tok(A, 0))
            if LAYERS < 4:
                return
            dve.sem_inc(rows_used, 1)
            dve.sem_inc(maxed, 4)
            dve.sem_inc(o_out, 1)
            dve.sem_inc(normalized, 1)
            for b in range(BATCH):
                xb = xt[:, b * TT:(b + 1) * TT, :]
                normalize(xb, x3)
                if b == 0:
                    dve.wait_ge(ld_rows, 48)
                    dve.wait_ge(ld_adarows, 128)
                affine(x3, R_NG).then_inc(xn_ready, 1)
                dve.wait_ge(ld_mask3, 16 * (b + 1))
                link(dve.tensor_scalar(bc_raw, bc_raw, 1.0, -MASKED, ALU.subtract, ALU.mult))
                split_rows().then_inc(mask_split, 1)
                for side, (src, parts) in enumerate(((q3T, q_parts), (k3T, k_parts))):
                    dve.wait_ge(evac, FIRST[("3qT", "3kT")[side], b] + 4)
                    flat = src.rearrange("p k t -> p (k t)")
                    link(dve.tensor_copy(parts[0], flat))
                    link(dve.tensor_tensor(rest3, flat, parts[0], ALU.subtract))
                    link(dve.tensor_copy(parts[1], rest3))
                    ins = dve.tensor_tensor(parts[2], rest3, parts[1], ALU.subtract)
                    ins.then_inc(qk_split, 1)
                    dve.wait_ge(qk_split, 2 * b + side + 1)
                dve.wait_ge(evac, FIRST["3v", b] + 4)
                link(dve.memset(wl1[:, 4096:8192], 0.0))
                dve.memset(v_aug[:, :, :, HD:HD + 1], 1.0)
                link(dve.tensor_tensor(v3, v3, per_column(rows[:, R_BV:R_BV + D]), ALU.add))
                token_mask = m3c[:, b * TT:(b + 1) * TT].rearrange("p (i o q) -> p i o q", o=1, q=1).to_broadcast([P, TT, HEADS, HD])
                dve.tensor_tensor(v_aug[:, :, :, 0:HD], v3.rearrange("p i (h d) -> p i h d", d=HD), token_mask,
                                  ALU.mult).then_inc(v_aug_ready, 1)
                with dve.Fori(0, HEADS) as h:
                    for i in range(TT):
                        dve.wait_ge(scored, h * TT + (b * HEADS * TT + i + 1))
                        dve.tensor_reduce(row_max[:, bass.ds(h * TT + i, 1)],
                                          psum[:, i % 4 * 2:i % 4 * 2 + 2, :].rearrange("p a t -> p (a t)"),
                                          AX.X, ALU.max).then_inc(maxed, 1)
                dve.wait_ge(evac, FIRST["3mx", b] + 1)
                link(dve.tensor_copy(max_parts[0], neg_max))
                link(dve.tensor_tensor(max_rest, neg_max, max_parts[0], ALU.subtract))
                link(dve.tensor_copy(max_parts[1], max_rest))
                dve.tensor_tensor(max_parts[2], max_rest, max_parts[1], ALU.subtract).then_inc(max_split, 1)
                with dve.Fori(0, QUADS) as quad:
                    dve.wait_ge(weighed_v, quad * UNITS + (b * QUADS * UNITS + UNITS + 4))
                    dve.tensor_copy(oT, psum[:, 0:2, :].rearrange("p a t -> p (a t)")).then_inc(o_out, 1)
                    dve.wait_ge(o_turned, quad + (b * QUADS + 1))
                    sums = psum[:, 2:4, :].rearrange("p a (i h c) -> p (a i) h c", h=QH, c=32)
                    dve.reciprocal(inv3, sums[:, :, :, HD:HD + 1].rearrange("p i h o -> p i (h o)")).then_inc(inverted, 1)
                    dve.wait_ge(inverted, quad + (b * QUADS + 1))
                    dst = y3.rearrange("p i (g n) -> p i g n", g=QUADS)[:, :, bass.ds(quad, 1), :].rearrange(
                        "p i o (h d) -> p i (o h) d", d=HD)
                    dve.tensor_tensor(dst, sums[:, :, :, 0:HD], inv3.rearrange("p i (h o) -> p i h o", o=1)
                                      .to_broadcast([P, TT, QH, HD]), ALU.mult).then_inc(normalized, 1)
                dve.wait_ge(normalized, (b + 1) * QUADS + 1)
                film("3", b, BATCH + b, y3, o3)

        block = ctx.enter_context(nc.Block())

        @block.sync
        def _(sp):
            parts = (slice(0, ADA[0]), slice(ADA[0], NADA))
            x_in = x.rearrange("b (i p) d -> p b i d", p=P)

            def load_x(b):
                sp.dma_start(xt[:, b * TT:(b + 1) * TT, :], x_in[:, b]).then_inc(ld_x[b], 16)

            def load_conditioning(n):
                sp.dma_start(adab[n], ada_b[:, parts[n]].to_broadcast([BATCH, parts[n].stop - parts[n].start])).then_inc(ld_ada[n], 16)
                sp.dma_start(adaw[n], ada_w[:, :, parts[n]]).then_inc(ld_ada[n], 16)

            def store_conditioning(n):
                sp.wait_ge(ada_ready, n + 1)
                sp.dma_start(scr_ada[:, parts[n]], adas[n]).then_inc(ada_stored, 16)

            sp.dma_start(sct[:, :, :], cond_t).then_inc(ld_small, 16)
            sp.dma_start(cols[:, :], cols_in).then_inc(ld_small, 16)
            load_conditioning(0)
            load_x(0)
            sp.dma_start(rows[:, :], rows_in[0:1, :].to_broadcast([P, NROWS])).then_inc(ld_rows, 16)
            sp.dma_start(w0s[:, 0:NW0], w0).then_inc(ld_w0, 16)
            sp.dma_start(wdts[:, :, :], wdt).then_inc(ld_w0, 16)
            store_conditioning(0)
            sp.wait_ge(ada_stored, 16)
            for layer in range(LAYERS):
                if layer:
                    sp.wait_ge(rows_used, layer)
                for b in range(BATCH):
                    src = scr_ada[b:b + 1, ADA0[layer]:ADA0[layer] + ADA[layer]]
                    sp.dma_start(ada[:, b, 0:ADA[layer]], src.to_broadcast([P, ADA[layer]])).then_inc(ld_adarows, 16)
                if layer == 0:
                    load_x(1)
                    load_conditioning(1)
                    sp.dma_start(m2c[:, :], mask2_col).then_inc(ld_w23, 16)
                    sp.dma_start(m3c[:, :], mask3_col).then_inc(ld_w23, 16)
                    store_conditioning(1)
                    sp.dma_start(wl1[:, 0:NW1], w1).then_inc(ld_w1, 16)
                    sp.wait_ge(ada_stored, 32)
                    sp.dma_start(wl23[:, :, :], w23).then_inc(ld_w23, 16)
                if layer >= 2:
                    sp.dma_start(rows[:, :], rows_in[layer - 1:layer, :].to_broadcast([P, NROWS])).then_inc(ld_rows, 16)
                if layer == 2:
                    sync_layer2(sp)
                if layer == 3:
                    sync_layer3(sp)
            for b in range(BATCH):
                sp.wait_ge(x_updated, LAYERS * BATCH - BATCH + b + 1)
                sp.dma_start(out[b].rearrange("(i p) d -> p i d", p=P), xt[:, b * TT:(b + 1) * TT, :]).then_inc(stored, 16)
            sp.wait_ge(stored, 16 * BATCH)

        @block.gpsimd
        def _(pool):
            pool.memset(ident[:, :], 0.0).then_inc(made, 1)
            pool.memset(pick[:, :], 0.0).then_inc(made, 1)
            pool.memset(heads[:, :], 1.0).then_inc(made, 1)
            pool.wait_ge(made, 3)
            pool.affine_select(out=ident[:, :], in_=ident[:, :], compare_op=ALU.not_equal, fill=1.0, base=0,
                               pattern=[[-1, P]], channel_multiplier=1).then_inc(made, 1)
            for part in range(3):
                pool.affine_select(out=pick[:, :], in_=pick[:, :], compare_op=ALU.not_equal, fill=1.0,
                                   base=-2 * NS * part, pattern=[[-1, 2 * NS]], channel_multiplier=1).then_inc(made, 1)
                pool.wait_ge(made, 5 + part)
            by_head = heads[:, :].rearrange("p (j d) -> p j d", d=HD)
            pool.affine_select(out=by_head, in_=by_head, compare_op=ALU.is_ge, fill=0.0, base=0,
                               pattern=[[-HD, P // HD], [0, HD]], channel_multiplier=1).then_inc(made, 1)
            pool.wait_ge(made, 8)
            pool.affine_select(out=by_head, in_=by_head, compare_op=ALU.is_ge, fill=0.0, base=HD - 1,
                               pattern=[[HD, P // HD], [0, HD]], channel_multiplier=-1).then_inc(made, 1)
            pool.wait_ge(made, 9)
            pool.memset(eps[:, :], EPS).then_inc(consts_ready, 1)

            for s in range(len(SCANS) if LAYERS > 1 else 2):
                for c in range(CHUNKS):
                    pool_chunk(pool, s, c)
            if LAYERS == 4:
                pool_attention(pool)

        @block.tensor
        def _(pe):
            def bank(g):
                if g >= 8:
                    pe.wait_ge(evac, g - 7)
                return psum[:, g % 8, :]

            def to_wide(g, src):
                for k in range(KD):
                    for half in range(2):
                        ps = bank(g)
                        for q in range(4):
                            last = pe.transpose(ps[:, q * P:(q + 1) * P], src[:, half * 4 + q, k * P:(k + 1) * P], ident[:, :])
                        last.then_inc(prod, 1)
                        g += 1

            def project(g, w, src, m_tiles, k_tiles, m=P):
                for mt in range(m_tiles):
                    for half in range(2):
                        ps = bank(g)
                        for k in range(k_tiles):
                            last = pe.matmul(ps[0:m, :], w[:, k, mt * m:(mt + 1) * m], src[:, k, half * 512:half * 512 + 512],
                                             start=k == 0, stop=k == k_tiles - 1)
                        last.then_inc(prod, 1)
                        g += 1

            def to_tokens(g, src, w, k_tiles):
                for pair in range(TT // 2):
                    ps = bank(g)
                    for q in range(2):
                        t0 = (pair * 2 + q) * P
                        for k in range(k_tiles):
                            last = pe.matmul(ps[:, q * D:(q + 1) * D], src[:, k, t0:t0 + P], w[:, k, :],
                                             start=k == 0, stop=k == k_tiles - 1)
                    last.then_inc(prod, 1)
                    g += 1

            def conditioning(n):
                pe.wait_ge(ld_ada[n], 32)
                for g, (at, size) in enumerate(ADA_PIECES[n]):
                    ps = bank(FIRST["ada", n] + g)
                    for k in range(KE):
                        a0 = at - ADA0[n]
                        last = pe.matmul(ps[0:BATCH, 0:size], sct[:, k, :], adaw[n][:, k, a0:a0 + size], start=k == 0, stop=k == KE - 1)
                    last.then_inc(prod, 1)

            pe.wait_ge(sct_ready, 1)
            conditioning(0)
            pe.wait_ge(consts_ready, 1)
            pe.wait_ge(ld_w0, 32)
            w_in = w0s[:, W0_IN:W0_XP].rearrange("p (k m) -> p k m", k=KD)
            w_xp = w0s[:, W0_XP:W0_OUT].rearrange("p (k m) -> p k m", k=KE)
            w_out = w0s[:, W0_OUT:NW0].rearrange("p (k m) -> p k m", k=KE)

            def scan_inputs(s, b, xp, dt, wx, wt, src):
                project(FIRST[xp, b], wx, src, 1, KE, XP)
                pe.wait_ge(evac, FIRST[xp, b] + 2)
                g = FIRST[dt, b]
                for mt in range(KE):
                    for half in range(2):
                        pe.matmul(bank(g), wt[:, mt * P:(mt + 1) * P], dt_low[:, half * 512:half * 512 + 512],
                                  start=True, stop=True).then_inc(prod, 1)
                        g += 1
                pe.wait_ge(evac, g)
                pe.wait_ge(bc_ready, s + 1)
                for c in range(CHUNKS):
                    chunk(s, c)
                pe.wait_ge(y_out, (s + 1) * CHUNKS * KE)

            def chunk(s, c):
                _, b, which, slot, backward = SCANS[s]
                cc = s * CHUNKS + c
                at = (CHUNKS - 1 - c if backward else c) * TC

                def spread(n, c=c):
                    cc = s * CHUNKS + c
                    at = (CHUNKS - 1 - c if backward else c) * TC
                    if cc or not isinstance(n, int) or n:
                        pe.wait_ge(dbu, n * PAIRS + cc * NS * PAIRS)
                        pe.wait_ge(c_out, cc * NS + n)
                    for half in range(2):
                        row = pick[:, half * NS + n:half * NS + n + 1] if isinstance(n, int) else \
                            pick[:, bass.ds(n + half * NS, 1)]
                        last = pe.matmul(psum[:, 4 + half, :], row.to_broadcast([96, P]), bcs[:, at:at + TC],
                                         start=True, stop=True)
                    last.then_inc(bcast, 1)

                def add_state(n, k, pair, final=False):
                    for e in (2 * pair, 2 * pair + 1):
                        if e % 2 == 0:
                            pe.wait_ge(weighed, cc * NS * PAIRS + n * PAIRS + e // 2 + 1)
                        pe.matmul(psum[:, e, :], ident[:, :], hbuf[:, k, e, :], start=False, stop=final,
                                  skip_group_check=True).then_inc(summed, 1)

                if c == 0:
                    spread(0)
                src = chan(slot)
                for e in range(KE):
                    if c:
                        pe.wait_ge(y_out, (cc - 1) * KE + e + 1)
                    pe.matmul(psum[:, e, :], diag_d[:, which, e, :], src[:, e, at:at + TC], start=True, stop=False,
                              skip_group_check=True)
                if c == 0:
                    spread(1)
                with pe.Fori(0, NS // 2 - 1) as i:
                    for k in range(2):
                        add_state(i * 2 + k, k, 0)
                        spread(i * 2 + (k + 2))
                        add_state(i * 2 + k, k, 1)
                for k in range(2):
                    add_state(NS - 2 + k, k, 0, k == 1)
                    if c < CHUNKS - 1:
                        spread(k, c + 1)
                    add_state(NS - 2 + k, k, 1, k == 1)

            pe.wait_ge(a_ready, 1)
            for b in range(BATCH):
                pe.wait_ge(xn_ready, b + 1)
                to_wide(FIRST["0xT", b], tok(E, 0))
                pe.wait_ge(evac, FIRST["0in", b])
                project(FIRST["0in", b], w_in, wide(E, 1), 2 * KE, KD)
                pe.wait_ge(u_ready, (b + 1) * KE)
                scan_inputs(b, b, "0xp", "0dt", w_xp, wdts[:, 0, :], chan(C))
                pe.wait_ge(gated, (b + 1) * KE)
                to_tokens(FIRST["0out", b], chan(C), w_out, KE)
                if b == 0:
                    conditioning(1)

            if LAYERS < 2:
                return
            pe.wait_ge(ld_w1, 16)
            wx1 = wl1[:, W1_X:W1_Z].rearrange("p (k m) -> p k m", k=KD)
            wz1 = wl1[:, W1_Z:W1_C].rearrange("p (k m) -> p k m", k=KD)
            wc1 = wl1[:, W1_C:W1_XP].rearrange("p (d k m) -> p d k m", d=2, k=KE)
            wxp1 = wl1[:, W1_XP:W1_F].rearrange("p (d k m) -> p d k m", d=2, k=KE)
            wf1 = wl1[:, W1_F:NW1].rearrange("p (k m) -> p k m", k=KE)
            for b in range(BATCH):
                pe.wait_ge(xn_ready, BATCH + b + 1)
                to_wide(FIRST["1xT", b], tok(E, 0))
                pe.wait_ge(evac, FIRST["1xz", b])
                project(FIRST["1xz", b], wx1, wide(E, 1), KE, KD)
                project(FIRST["1xz", b] + 8, wz1, wide(E, 1), KE, KD)
                pe.wait_ge(evac, FIRST["1c", b])
                for d in range(2):
                    project(FIRST["1c", b] + 8 * d, wc1[:, d], chan(A), KE, KE)
                pe.wait_ge(evac, FIRST["1xp0", b])
                for d in range(2):
                    scan_inputs(2 + 2 * b + d, b, f"1xp{d}", f"1dt{d}", wxp1[:, d], wdts[:, 1 + d, :], chan((C, F)[d]))
                pe.wait_ge(gated, (BATCH + b + 1) * KE)
                to_tokens(FIRST["1out", b], chan(C), wf1, KE)
            tensor_attention(pe, bank, to_wide, project, to_tokens)

        @block.scalar
        def _(act):
            steps = [0]

            def link(ins):
                steps[0] += 1
                ins.then_inc(act_step, 1)
                act.wait_ge(act_step, steps[0])

            def move(g, dst, src=None, func=ACT.Identity, **kw):
                act.wait_ge(prod, g + 1)
                ps = psum[:, g % 8, :] if src is None else src
                act.activation(dst, ps, func, **kw).then_inc(evac, 1)

            def wide_out(g, dst):
                for k in range(KD):
                    for half in range(2):
                        move(g, dst[:, k, half * 512:half * 512 + 512])
                        g += 1

            def tokens_out(g, dst):
                for pair in range(TT // 2):
                    move(g, dst[:, pair * 2:pair * 2 + 2, :], psum[:, g % 8, :].rearrange("p (q d) -> p q d", q=2))
                    g += 1

            def project_out(g, dst, m_tiles, func=ACT.Identity, bias=None):
                for mt in range(m_tiles):
                    for half in range(2):
                        kw = {} if bias is None else {"bias": cols[:, bias + mt:bias + mt + 1]}
                        move(g, dst[:, mt, half * 512:half * 512 + 512], func=func, **kw)
                        g += 1

            norms = [0]

            def deviation():
                norms[0] += 1
                act.wait_ge(var_ready, norms[0])
                act.activation(std[:, :], mv[:, :, 1], ACT.Sqrt, bias=eps[:, 0:1]).then_inc(std_ready, 1)

            def scan_inputs(s, b, xp, dt, c_dtb):
                g = FIRST[xp, b]
                for half in range(2):
                    move(g + half, xp_out[:, half * 512:half * 512 + 512], psum[0:XP, (g + half) % 8, :])
                tmp = chan(E)
                for step in range(KE + 2):
                    if step < KE:
                        project_out(FIRST[dt, b] + 2 * step, chan(A)[:, step:step + 1, :], 1, bias=c_dtb + step)
                    if 0 <= step - 1 < KE:
                        e = step - 1
                        act.wait_ge(abs_ready, s * KE + e + 1)
                        act.activation(tmp[:, e, :], tmp[:, e, :], ACT.Exp).then_inc(exp_ready, 1)
                    if step >= 2:
                        e = step - 2
                        act.wait_ge(exp_ready, s * KE + e + 1)
                        act.activation(tmp[:, e, :], tmp[:, e, :], ACT.Ln, bias=1.0).then_inc(log_ready, 1)
                act.wait_ge(dt_ready, (s + 1) * KE)
                for c in range(CHUNKS):
                    chunk(s, c)

            def chunk(s, c):
                _, b, which, slot, backward = SCANS[s]
                cc = s * CHUNKS + c
                at = (CHUNKS - 1 - c if backward else c) * TC
                end = 0 if backward else TC - 1
                dt = chan(A)
                c_a = C_A if which == 0 else C_A1 + (which - 1) * KE * NS

                def state(n, k, first):
                    act.wait_ge(bcast, cc * NS + n + 1)
                    if not first:
                        act.wait_ge(weighed, cc * NS * PAIRS + (n - 1) * PAIRS)
                    elif cc:
                        act.wait_ge(weighed, (cc - 1) * NS * PAIRS + (NS - 1 + k) * PAIRS)
                    act.activation(cbuf[:, k, :], psum[:, 5, :], ACT.Identity).then_inc(c_out, 1)
                    for e in range(KE):
                        u = cc * NS * KE + n * KE + e
                        if not (isinstance(u, int) and u < 2):
                            act.wait_ge(scanned, u - 1)
                        a = cols[:, bass.ds(n + (c_a + e * NS), 1)] if not isinstance(n, int) else \
                            cols[:, c_a + e * NS + n:c_a + e * NS + n + 1]
                        if c < CHUNKS - 1 and e == 1 and not (first and k == 0):
                            save(n + (-1), 1 - k, 1)
                        if c < CHUNKS - 1 and e == 3:
                            save(n, k, 0)
                        act.activation(psum[:, 6 + e % 2, :], dt[:, e, at:at + TC], ACT.Exp, scale=a).then_inc(decay, 1)

                def save(n, k, pair):
                    col = hlast[:, 2 * pair:2 * pair + 2, n:n + 1] if isinstance(n, int) else \
                        hlast[:, 2 * pair:2 * pair + 2, bass.ds(n, 1)]
                    act.activation(col, hbuf[:, k, 2 * pair:2 * pair + 2, end:end + 1], ACT.Identity).then_inc(saved, 1)

                def sums_out(c):
                    cc = s * CHUNKS + c
                    at = (CHUNKS - 1 - c if backward else c) * TC
                    act.wait_ge(summed, (cc + 1) * NS * KE)
                    for e in range(KE):
                        act.activation(chan(slot)[:, e, at:at + TC], psum[:, e, :], ACT.Identity).then_inc(y_out, 1)

                state(0, 0, True)
                if c:
                    sums_out(c - 1)
                state(1, 1, True)
                with act.Fori(1, NS // 2) as i:
                    for k in range(2):
                        state(i * 2 + k, k, False)
                if c < CHUNKS - 1:
                    act.wait_ge(scanned, (cc + 1) * NS * KE)
                    save(NS - 1, 1, 1)
                else:
                    sums_out(c)

            def conditioning_out(n):
                for g, (at, size) in enumerate(ADA_PIECES[n], FIRST["ada", n]):
                    move(g, adas[n][:, at - ADA0[n]:at - ADA0[n] + size], psum[0:BATCH, g % 8, 0:size])

            act.wait_ge(ld_small, 32)
            act.activation(sct[:, :, :], sct[:, :, :], ACT.Silu).then_inc(sct_ready, 1)
            act.activation(cols[:, C_A:C_A + KE * NS], cols[:, C_A:C_A + KE * NS], ACT.Exp).then_inc(cols_ready, 1)
            act.activation(cols[:, C_A1:C_A1 + 2 * KE * NS], cols[:, C_A1:C_A1 + 2 * KE * NS], ACT.Exp).then_inc(cols_ready, 1)
            conditioning_out(0)
            act.wait_ge(consts_ready, 1)
            for b in range(BATCH):
                deviation()
                wide_out(FIRST["0xT", b], wide(E, 1))
                project_out(FIRST["0in", b], chan(A), KE)
                for e in range(KE):
                    act.wait_ge(conv_ready, b * KE + e + 1)
                    act.activation(chan(C)[:, e, :], chan(C)[:, e, :], ACT.Silu,
                                   bias=cols[:, C_CONVB + e:C_CONVB + e + 1]).then_inc(u_ready, 1)
                    project_out(FIRST["0in", b] + 8 + 2 * e, chan(B)[:, e:e + 1, :], 1, ACT.Silu)
                scan_inputs(b, b, "0xp", "0dt", C_DTB)
                tokens_out(FIRST["0out", b], tok(E, 0))
                if b == 0:
                    act.wait_ge(ld_ada[1], 32)
                    conditioning_out(1)
            if LAYERS < 2:
                return
            for b in range(BATCH):
                deviation()
                deviation()
                wide_out(FIRST["1xT", b], wide(E, 1))
                project_out(FIRST["1xz", b], chan(B), KE, ACT.Silu, C_BX)
                project_out(FIRST["1xz", b] + 8, chan(A), KE, bias=C_BZ)
                for d in range(2):
                    if d == 0:
                        act.wait_ge(skip_added, b + 1)
                    project_out(FIRST["1c", b] + 8 * d, chan((C, F)[d]), KE, bias=C_BC + d * KE)
                for d in range(2):
                    scan_inputs(2 + 2 * b + d, b, f"1xp{d}", f"1dt{d}", C_BDT + d * KE)
                tokens_out(FIRST["1out", b], tok(E, 0))
            scalar_attention(act, move, wide_out, tokens_out, project_out, deviation, link)

        @block.vector
        def _(dve):
            steps = [0]

            def link(ins):
                steps[0] += 1
                ins.then_inc(dve_step, 1)
                dve.wait_ge(dve_step, steps[0])

            norms = [0]

            def normalize(src, dst):
                norms[0] += 1
                for i in range(TT):
                    last = dve.bn_stats(stats[:, i, :], src[:, i, :])
                link(last)
                for i in range(TT):
                    last = dve.bn_aggr(mv[:, i, :], stats[:, i, :])
                last.then_inc(var_ready, 1)
                dve.wait_ge(std_ready, norms[0])
                link(dve.reciprocal(rstd[:, :], std[:, :]))
                for i in range(TT):
                    last = dve.tensor_scalar(dst[:, i, :], src[:, i, :], mv[:, i, 0:1], rstd[:, i:i + 1], ALU.subtract, ALU.mult)
                link(last)

            def condition(g, b, r_gain, r_shift, dst):
                scale, sh = g
                dve.scalar_tensor_tensor(gain[:, :], scale, 1.0, rows[:, r_gain:r_gain + D], ALU.add, ALU.mult)
                link(dve.scalar_tensor_tensor(shift[:, :], scale, 1.0, rows[:, r_shift:r_shift + D], ALU.add, ALU.mult))
                link(dve.tensor_tensor(shift[:, :], shift[:, :], sh, ALU.add))
                link(dve.tensor_tensor(dst, dst, per_column(gain[:, :]), ALU.mult))
                return dve.tensor_tensor(dst, dst, per_column(shift[:, :]), ALU.add)

            def split_rows():
                link(dve.tensor_copy(bc_hi, bc_raw))
                link(dve.tensor_tensor(bc_rest, bc_raw, bc_hi, ALU.subtract))
                link(dve.tensor_copy(bc_mid, bc_rest))
                dve.tensor_copy(bcs[0:2 * NS, :], bc_hi)
                dve.tensor_copy(bcs[2 * NS:4 * NS, :], bc_mid)
                return dve.tensor_tensor(bcs[4 * NS:6 * NS, :], bc_rest, bc_mid, ALU.subtract)

            def scan_inputs(s, b, xp, dt, slot):
                dve.wait_ge(evac, FIRST[xp, b] + 2)
                split_rows().then_inc(bc_ready, 1)
                v, tmp, src = chan(A), chan(E), chan(slot)
                for e in range(KE):
                    dve.wait_ge(evac, FIRST[dt, b] + 2 * e + 2)
                    dve.scalar_tensor_tensor(tmp[:, e, :], v[:, e, :], -1.0, v[:, e, :], ALU.mult, ALU.min).then_inc(abs_ready, 1)
                for step in range(KE + 1):
                    if step < KE:
                        e = step
                        dve.wait_ge(log_ready, s * KE + e + 1)
                        dve.scalar_tensor_tensor(v[:, e, :], v[:, e, :], 0.0, tmp[:, e, :], ALU.max, ALU.add).then_inc(dt_ready, 1)
                    if step:
                        e = step - 1
                        dve.wait_ge(dt_ready, s * KE + e + 1)
                        dve.tensor_tensor(tmp[:, e, :], v[:, e, :], src[:, e, :], ALU.mult).then_inc(w_ready, 1)
                dve.wait_ge(w_ready, (s + 1) * KE)
                for c in range(CHUNKS):
                    chunk(s, c)

            def chunk(s, c):
                backward = SCANS[s][4]
                cc = s * CHUNKS + c
                at = (CHUNKS - 1 - c if backward else c) * TC
                w = chan(E)
                way = slice(None, None, -1) if backward else slice(None)

                def load(n, k, p, c=c):
                    cc = s * CHUNKS + c
                    at = (CHUNKS - 1 - c if backward else c) * TC
                    dve.wait_ge(bcast, n + (cc * NS + 1))
                    if cc or not isinstance(n, int) or n >= 2:
                        dve.wait_ge(summed, n * KE + ((cc * NS - 2) * KE + 2 * p + 2))
                    dve.tensor_tensor(hbuf[:, k, 2 * p:2 * p + 2, :], w[:, 2 * p:2 * p + 2, at:at + TC],
                                      psum[:, 4, :].rearrange("p (o t) -> p o t", o=1).to_broadcast([P, 2, TC]),
                                      ALU.mult).then_inc(dbu, 1)

                def scan(n, k, p):
                    dve.wait_ge(dbu, n * PAIRS + (cc * NS * PAIRS + p + 1))
                    for e in (2 * p, 2 * p + 1):
                        dve.wait_ge(decay, n * KE + (cc * NS * KE + e + 1))
                        h = hbuf[:, k, e, way]
                        if c == 0:
                            start = 0.0
                        else:
                            start = hlast[:, e, n:n + 1] if isinstance(n, int) else hlast[:, e, bass.ds(n, 1)]
                        dve.tensor_tensor_scan(h, psum[:, 6 + e % 2, way], h, start, ALU.mult, ALU.add).then_inc(scanned, 1)

                def state(n, k):
                    load(n, k, 1)
                    scan(n, k, 0)
                    load(n + 1, 1 - k, 0)
                    scan(n, k, 1)

                if c == 0:
                    load(0, 0, 0)
                else:
                    dve.wait_ge(saved, (s * (CHUNKS - 1) + c) * NS * PAIRS)
                for k in range(2):
                    state(k, k)
                with dve.Fori(1, NS // 2 - 1) as i:
                    for k in range(2):
                        state(i * 2 + k, k)
                state(NS - 2, 0)
                load(NS - 1, 1, 1)
                scan(NS - 1, 1, 0)
                if c < CHUNKS - 1:
                    load(0, 0, 0, c + 1)
                scan(NS - 1, 1, 1)

            dve.wait_ge(cols_ready, 2)
            for at, n in ((C_A, KE * NS), (C_A1, 2 * KE * NS)):
                dve.tensor_scalar(cols[:, at:at + n], cols[:, at:at + n], -1.0, None, ALU.mult)
            dve.wait_ge(consts_ready, 1)
            for which in range(3):
                for e in range(KE):
                    col = (C_D if which == 0 else C_D1 + (which - 1) * KE) + e
                    last = dve.tensor_scalar(diag_d[:, which, e, :], ident[:, :], cols[:, col:col + 1], None, ALU.mult)
            last.then_inc(a_ready, 1)

            def conditioning_bias(n):
                dve.wait_ge(evac, FIRST["ada", n] + len(ADA_PIECES[n]))
                dve.tensor_tensor(adas[n], adas[n], adab[n], ALU.add).then_inc(ada_ready, 1)

            conditioning_bias(0)
            for b in range(BATCH):
                xb = xt[:, b * TT:(b + 1) * TT, :]
                xn = tok(E, 0)
                dve.wait_ge(ld_x[b], 16)
                normalize(xb, xn)
                if b == 0:
                    dve.wait_ge(ld_rows, 16)
                    dve.wait_ge(ld_adarows, 32)
                condition((ada[:, b, D:2 * D], ada[:, b, 0:D]), b, R_G0, R_B0, xn).then_inc(xn_ready, 1)
                xi, u = chan(A), chan(C)
                for e in range(KE):
                    dve.wait_ge(evac, FIRST["0in", b] + 2 * e + 2)
                    for tap in range(CONV):
                        wcol = cols[:, C_CONVW + e * CONV + CONV - 1 - tap:C_CONVW + e * CONV + CONV - tap]
                        if tap == 0:
                            last = dve.tensor_scalar(u[:, e, :], xi[:, e, :], wcol, None, ALU.mult)
                        else:
                            last = dve.scalar_tensor_tensor(u[:, e, tap:SEQ], xi[:, e, 0:SEQ - tap], wcol, u[:, e, tap:SEQ],
                                                            ALU.mult, ALU.add)
                        if tap < CONV - 1:
                            link(last)
                    last.then_inc(conv_ready, 1)
                scan_inputs(b, b, "0xp", "0dt", C)
                for e in range(KE):
                    dve.wait_ge(y_out, ((b + 1) * CHUNKS - 1) * KE + e + 1)
                    dve.tensor_tensor(chan(C)[:, e, :], chan(C)[:, e, :], chan(B)[:, e, :], ALU.mult).then_inc(gated, 1)
                dve.wait_ge(evac, FIRST["0out", b] + 4)
                ssm = tok(E, 0)
                link(dve.tensor_tensor(ssm, ssm, per_column(ada[:, b, 2 * D:3 * D]), ALU.mult))
                ins = dve.tensor_tensor(xb, xb, ssm, ALU.add)
                ins.then_inc(x_updated, 1)
                dve.wait_ge(x_updated, b + 1)
                if b == 0:
                    conditioning_bias(1)
            if LAYERS < 2:
                return
            dve.wait_ge(x_updated, BATCH)
            dve.sem_inc(rows_used, 1)
            for b in range(BATCH):
                xb = xt[:, b * TT:(b + 1) * TT, :]
                x1, xn = tok(C, 0), tok(E, 0)
                normalize(xb, x1)
                if b == 0:
                    dve.wait_ge(ld_adarows, 64)
                link(condition((ada[:, b, D:2 * D], ada[:, b, 0:D]), b, R_G1, R_B1, x1))
                normalize(x1, xn)
                link(dve.tensor_tensor(xn, xn, per_column(rows[:, R_G2:R_G2 + D]), ALU.mult))
                dve.tensor_tensor(xn, xn, per_column(rows[:, R_B2:R_B2 + D]), ALU.add).then_inc(xn_ready, 1)
                gate = per_column(ada[:, b, 2 * D:3 * D])
                link(dve.tensor_tensor(x1, x1, per_column(rows[:, R_BF:R_BF + D]), ALU.add))
                link(dve.tensor_tensor(x1, x1, gate, ALU.mult))
                dve.tensor_tensor(xb, xb, x1, ALU.add).then_inc(skip_added, 1)
                for d in range(2):
                    scan_inputs(2 + 2 * b + d, b, f"1xp{d}", f"1dt{d}", (C, F)[d])
                for step in range(KE + 1):
                    if step < KE:
                        dve.wait_ge(y_out, ((4 + 2 * b) * CHUNKS - 1) * KE + step + 1)
                        dve.tensor_tensor(chan(C)[:, step, :], chan(C)[:, step, :], chan(F)[:, step, :], ALU.add).then_inc(both_added, 1)
                    if step:
                        e = step - 1
                        dve.wait_ge(both_added, b * KE + e + 1)
                        dve.tensor_tensor(chan(C)[:, e, :], chan(C)[:, e, :], chan(B)[:, e, :], ALU.mult).then_inc(gated, 1)
                dve.wait_ge(evac, FIRST["1out", b] + 4)
                ssm = tok(E, 0)
                link(dve.tensor_tensor(ssm, ssm, gate, ALU.mult))
                dve.tensor_tensor(xb, xb, ssm, ALU.add).then_inc(x_updated, 1)
                dve.wait_ge(x_updated, BATCH + b + 1)
            vector_attention(dve, link, normalize, condition, split_rows)


def pack(inputs):
    import numpy as np

    def arr(name):
        return np.asarray(inputs[name])

    def kmajor(w):
        k, m = w.shape
        return w.reshape(k // P, P, m).transpose(1, 0, 2).reshape(P, -1)

    def xproj(w):
        return kmajor(w.T)

    def chans(v):
        v = v.reshape(v.shape[0], -1)
        return v.reshape(-1, P, v.shape[1]).transpose(1, 0, 2).reshape(P, -1)

    g0 = lambda n: arr("L0_cond_" + n)
    g1 = lambda n: arr("L1_cond_" + n)
    g2 = lambda n: arr("L2_cond_" + n)
    g3 = lambda n: arr("L3_cond_" + n)
    cols = np.zeros((P, NCOLS), np.float32)

    def put(at, v):
        v = chans(v)
        cols[:, at:at + v.shape[1]] = v

    put(C_CONVW, g0("conv_w")), put(C_CONVB, g0("conv_b")), put(C_DTB, g0("dt_proj_b"))
    put(C_D, g0("D_param")), put(C_A, g0("A_log"))
    put(C_BX, g1("bx")), put(C_BZ, g1("bz"))
    for d in range(2):
        put(C_BC + d * KE, g1(f"bc{d + 1}")), put(C_BDT + d * KE, g1(f"bdt{d + 1}"))
        put(C_D1 + d * KE, g1(f"Dp{d + 1}")), put(C_A1 + d * KE * NS, g1(f"Alog{d + 1}"))
    put(C_BK2, g2("bk")), put(C_BQ3, g3("q_b")), put(C_BK3, g3("k_b"))
    rows = np.stack([
        np.concatenate([g0("ln_g"), g0("ln_b"), g1("norm1_g"), g1("norm1_b"), g1("norm2_g"), g1("norm2_b"), g1("bf")]),
        np.concatenate([g2(n) for n in ("norm_scale", "norm_bias", "film_norm_scale", "film_norm_bias", "bq", "bv", "film_out_b")]),
        np.concatenate([g3(n) for n in ("norm_w", "norm_b", "sb_norm_w", "sb_norm_b", "q_b", "v_b", "out_b")]),
    ])
    ada_w = np.concatenate([g0("ada_w").T, g1("Wada").T, g2("film_emb_W"), g3("emb_w")], 1)
    ada_b = np.concatenate([g0("ada_b"), g1("bada"), g2("film_emb_b"), g3("emb_b")])[None]
    w0 = np.concatenate([kmajor(g0("in_proj_w").T), xproj(g0("x_proj_w")), kmajor(g0("out_proj_w").T)], 1)
    w1 = np.concatenate([kmajor(g1("Wx").T), kmajor(g1("Wz").T), kmajor(g1("Wc1").T), kmajor(g1("Wc2").T),
                         xproj(g1("Wdbc1")), xproj(g1("Wdbc2")), kmajor(g1("Wf").T)], 1)
    wdt = np.stack([g0("dt_proj_w").T, g1("Wdt1").T, g1("Wdt2").T], 1)
    w23 = np.stack([np.concatenate([kmajor(w) for w in (g2("Wq"), g2("Wk"), g2("Wv"), g2("film_out_W"))], 1),
                    np.concatenate([kmajor(w) for w in (g3("q_w"), g3("k_w"), g3("v_w"), g3("out_w"))], 1)], 1)

    def by_token(m):
        return m.reshape(BATCH * TT, P).T

    m2, m3 = arr("mask_BxS_ik0"), arr("mask_BxS_ff1")
    return {
        "x": arr("x"), "cond_t": arr("cond_2048").T.reshape(KE, P, BATCH).transpose(1, 0, 2), "cols_in": cols, "rows_in": rows,
        "ada_w": ada_w.reshape(KE, P, NADA).transpose(1, 0, 2), "ada_b": ada_b, "w0": w0, "w1": w1, "wdt": wdt, "w23": w23,
        "mask2_row": m2, "mask2_col": by_token(m2), "mask3_row": m3, "mask3_col": by_token(m3),
    }


def kernel(**inputs):
    import numpy as np
    import concourse.bacc as bacc
    from concourse import mybir as mb
    from concourse.bass_utils import run_bass_kernel_spmd

    nc = bacc.Bacc("TRN2", target_bir_lowering=False, num_devices=1)
    arrays, args = {}, []
    for name, value in pack(inputs).items():
        value = np.ascontiguousarray(value)
        arrays["in_" + name] = value
        args.append(nc.dram_tensor("in_" + name, value.shape, mb.dt.from_np(value.dtype), kind="ExternalInput").ap())
    args.append(nc.dram_tensor("out_0", (BATCH, SEQ, D), mb.dt.float32, kind="ExternalOutput").ap())
    build(nc, *args)
    r = run_bass_kernel_spmd(nc, [arrays], core_ids=[0])
    return r.results[0]["out_0"]
```

```python
import concourse.bass as bass
import concourse.mybir as mybir
from concourse.alu_op_type import AluOpType as ALU
from contextlib import ExitStack

F32 = mybir.dt.float32
BF16 = mybir.dt.bfloat16
I32 = mybir.dt.int32
ACT = mybir.ActivationFunctionType
AX = mybir.AxisListType

P = 128
BATCH = 2
SEQ = 1024
D = 256
DI = 512
NS = 16
RANK = 64
CONV = 4
HEADS = 16
HD = D // HEADS
EPS = 1e-5
KD = D // P
KE = DI // P
TT = SEQ // P
TC = 512
CHUNKS = SEQ // TC
XP = RANK + 2 * NS
PAIRS = KE // 2

C_CONVW, C_CONVB, C_DTB, C_A = 0, 16, 20, 32
C_D = 24
C_BX, C_BZ, C_BC, C_BDT, C_D1, C_A1 = 96, 100, 104, 112, 120, 128
C_BK2, C_BQ3, C_BK3 = 256, 258, 260
NCOLS = 262

R_G0, R_B0, R_G1, R_B1, R_G2, R_B2, R_BF = 0, 256, 512, 768, 1024, 1280, 1536
R_NG, R_NB, R_FG, R_FB, R_BQ, R_BV, R_OB = 0, 256, 512, 768, 1024, 1280, 1536
NROWS = 1792
ADA = [768, 768, 512, 512]
ADA0 = [0, 768, 1536, 2048]
NADA = sum(ADA)
ADA_PIECES = [[(0, 384), (384, 384)], [(768, 384), (1152, 384), (1536, 512), (2048, 512)]]
NREST = NADA - ADA[0]

W0_IN, W0_XP, W0_OUT, NW0 = 0, KD * 2 * DI, KD * 2 * DI + KE * XP, KD * 2 * DI + KE * XP + KE * D
W1_X, W1_Z = 0, KD * DI
W1_C = 2 * KD * DI
W1_XP = W1_C + 2 * KE * DI
W1_F = W1_XP + 2 * KE * XP
NW1 = W1_F + KE * D
WA_Q, WA_K, WA_V, WA_O, NWA = 0, KD * D, 2 * KD * D, 3 * KD * D, 4 * KD * D

TERMS = [(0, 0), (0, 1), (1, 0), (1, 1), (0, 2), (2, 0)]
K_MAX = len(TERMS) * HD + 3
K_EXP = K_MAX + 3
MASKED = -1000000.0
QH = 4
QUADS = HEADS // QH
JOBS = BATCH * QUADS
AHEAD = 2
UNITS = QH * TT
LOADS = 2 * len(TERMS) + 1
TWO_ONES = 1.0019378662109375
LAYERS = 4
NEVER = -1e30

STAGES = [("ada", 0, len(ADA_PIECES[0]))]
for _b in range(BATCH):
    STAGES += [("0xT", _b, 4), ("0in", _b, 16), ("0xp", _b, 2), ("0dt", _b, 8), ("0out", _b, 4)]
    if _b == 0:
        STAGES += [("ada", 1, len(ADA_PIECES[1]))]
for _b in range(BATCH):
    STAGES += [("1xT", _b, 4), ("1xz", _b, 16), ("1c", _b, 16)]
    for _d in range(2):
        STAGES += [(f"1xp{_d}", _b, 2), (f"1dt{_d}", _b, 8)]
    STAGES += [("1out", _b, 4)]
STAGES += [("2xT", _b, 4) for _b in range(BATCH)]
for _b in range(BATCH):
    STAGES += [("2q", _b, 4), ("2v", _b, 4), ("2kT", _b, 4)]
for _name, _count in (("2k", 4), ("2m", 1), ("2qT", 4), ("2y", 4), ("2hT", 4), ("2out", 4)):
    STAGES += [(_name, _b, _count) for _b in range(BATCH)]
for _b in range(BATCH):
    STAGES += [("3xT", _b, 4), ("3qT", _b, 4), ("3v", _b, 4), ("3kT", _b, 4)]
for _name in ("3hT", "3out"):
    STAGES += [(_name, _b, 4) for _b in range(BATCH)]
FIRST = {}
_n = 0
for _name, _b, _count in STAGES:
    FIRST[_name, _b] = _n
    _n += _count


def build(nc, x, cond_t, cols_in, rows_in, ada_w, ada_b, w0, w1, wdt, w23, mask2_row, mask2_col, mask3_row, mask3_col,
          out):
    ctx = ExitStack()
    with ctx:
        def sb(name, shape, dt=F32):
            return ctx.enter_context(nc.sbuf_tensor(name, shape, dt))

        def sem(name):
            return ctx.enter_context(nc.semaphore(name))

        xt = sb("xt", [P, BATCH * TT, D])
        slots = sb("slots", [P, 5, KE * SEQ])
        wl1 = sb("wl1", [P, max(NW1, 4 * TT * D)])
        wdts = sb("wdts", [RANK, 3, DI])
        wl23 = sb("wl23", [P, 2, NWA])
        rows = sb("rows", [P, NROWS])
        ada = sb("ada", [P, BATCH, 768])
        cols = sb("cols", [P, NCOLS])
        hbuf = sb("hbuf", [P, 2, KE, TC])
        cbuf = sb("cbuf", [P, 2, TC])
        hlast = sb("hlast", [P, KE, NS])
        bcs = sb("bcs", [3 * 2 * NS, SEQ], BF16)
        ident = sb("ident", [P, P])
        pick = sb("pick", [3 * 2 * NS, 2 * NS], BF16)
        heads = sb("heads", [P, P])
        diag_d = sb("diag_d", [P, 3, KE, P])
        stats = sb("stats", [P, TT, 6])
        mv = sb("mv", [P, TT, 2])
        std = sb("std", [P, TT])
        rstd = sb("rstd", [P, TT])
        gain = sb("gain", [P, D])
        shift = sb("shift", [P, D])
        sct = sb("sct", [P, KE, BATCH])
        eps = sb("eps", [P, 1])
        keep2 = sb("keep2", [P, BATCH * TT])
        m2c = sb("m2c", [P, BATCH * TT], I32)
        m3c = sb("m3c", [P, BATCH * TT])
        small = sb("small", [P, 6 * KD])
        head_scale = sb("head_scale", [P, 32])
        psum = ctx.enter_context(nc.psum_tensor("psum", [P, 8, 512], F32))

        scr_ada = nc.dram_tensor("scr_ada", [BATCH, NADA], F32)
        scr_qk = nc.dram_tensor("scr_qk", [BATCH, 2, 3, D, SEQ], BF16)
        scr_mask = nc.dram_tensor("scr_mask", [BATCH, 3, SEQ], BF16)
        scr_max = nc.dram_tensor("scr_max", [JOBS, 3, UNITS, P], BF16)

        A, B, C, E, F = range(5)

        def chan(s):
            return slots[:, s, :].rearrange("p (e t) -> p e t", e=KE)

        def tok(s, half):
            return slots[:, s, half * TT * D:(half + 1) * TT * D].rearrange("p (i d) -> p i d", i=TT)

        def wide(s, half):
            return slots[:, s, half * KD * SEQ:(half + 1) * KD * SEQ].rearrange("p (k t) -> p k t", k=KD)

        def per_token(v):
            return v.rearrange("p (i o) -> p i o", o=1).to_broadcast([P, TT, D])

        def per_column(v):
            return v.rearrange("p (o d) -> p o d", o=1).to_broadcast([P, TT, D])

        w0s = slots[:, F, :]
        adaw = [slots[:, A, 0:KE * ADA[0]].rearrange("p (k n) -> p k n", k=KE),
                wl1[:, 0:KE * NREST].rearrange("p (k n) -> p k n", k=KE)]
        hflat = hbuf[:, :, :, :].rearrange("p a e t -> p (a e t)")
        adas = [hflat[0:BATCH, 0:ADA[0]], wl23[0:BATCH, 0, 0:NREST]]
        adab = [slots[0:BATCH, E, 0:ADA[0]], wl23[0:BATCH, 1, 0:NREST]]
        xp_out = hflat[0:XP, 0:SEQ]
        dt_low, bc_raw, bc_rest = xp_out[0:RANK, :], xp_out[RANK:XP, :], hflat[RANK:XP, SEQ:2 * SEQ]
        bc_hi = hflat[RANK:XP, 2 * SEQ:2 * SEQ + SEQ // 2].bitcast(BF16)
        bc_mid = hflat[RANK:XP, 2 * SEQ + SEQ // 2:3 * SEQ].bitcast(BF16)
        SCANS = [("0", 0, 0, C, False), ("0", 1, 0, C, False)]
        for b in range(BATCH):
            SCANS += [("1", b, 1, C, False), ("1", b, 2, F, True)]

        ld_x, ld_ada = ([sem(f"{n}{i}") for i in range(2)] for n in ("ld_x", "ld_ada"))
        ld_small, ld_w0, ld_w1, ld_w23 = (sem(n) for n in ("ld_small", "ld_w0", "ld_w1", "ld_w23"))
        ld_rows, ld_adarows = sem("ld_rows"), sem("ld_adarows")
        made, consts_ready = sem("made"), sem("consts_ready")
        prod, evac = sem("prod"), sem("evac")
        dve_step, act_step, pool_step = sem("dve_step"), sem("act_step"), sem("pool_step")
        sct_ready, ada_ready, ada_stored = sem("sct_ready"), sem("ada_ready"), sem("ada_stored")
        cols_ready = sem("cols_ready")
        a_ready = sem("a_ready")
        var_ready, std_ready, xn_ready = sem("var_ready"), sem("std_ready"), sem("xn_ready")
        conv_ready, u_ready = sem("conv_ready"), sem("u_ready")
        bc_ready, skip_added = sem("bc_ready"), sem("skip_added")
        abs_ready, exp_ready, log_ready, dt_ready, w_ready = (sem(n) for n in (
            "abs_ready", "exp_ready", "log_ready", "dt_ready", "w_ready"))
        bcast, c_out = sem("bcast"), sem("c_out")
        dbu, decay = sem("dbu"), sem("decay")
        scanned, weighed, summed = sem("scanned"), sem("weighed"), sem("summed")
        saved = sem("saved")
        y_out = sem("y_out")
        both_added, gated, x_updated = sem("both_added"), sem("gated"), sem("x_updated")
        rows_used = sem("rows_used")
        stored = sem("stored")
        ld_mask2, q_shifted, q_exp, qn_ready = sem("ld_mask2"), sem("q_shifted"), sem("q_exp"), sem("qn_ready")
        v_ready, k_masked, k_exp, kn_ready = sem("v_ready"), sem("k_masked"), sem("k_exp"), sem("kn_ready")
        outer_ready, h_conditioned, h_ready = sem("outer_ready"), sem("h_conditioned"), sem("h_ready")
        ld_mask3, mask_split, mask_stored = sem("ld_mask3"), sem("mask_split"), sem("mask_stored")
        qk_split, parts_stored, ones_set = sem("qk_split"), sem("parts_stored"), sem("ones_set")
        ld_stack = [sem(f"ld_stack{n}") for n in range(QUADS)]
        ld_max = [sem(f"ld_max{n}") for n in range(QUADS)]
        scored, maxed = sem("scored"), sem("maxed")
        max_found, max_turned, max_read = sem("max_found"), sem("max_turned"), sem("max_read")
        max_split, max_stored = sem("max_split"), sem("max_stored")
        v3_ready, quads_clear, v_quad_ready = sem("v3_ready"), sem("quads_clear"), sem("v_quad_ready")
        shifted, exped, weighed_v = sem("shifted"), sem("exped"), sem("weighed_v")
        o_out, o_turned, inverted, normalized = sem("o_out"), sem("o_turned"), sem("inverted"), sem("normalized")

        class Layer2:
            def __init__(self, areas, scalars):
                as_tok = lambda a: a.rearrange("p (i d) -> p i d", i=TT)
                as_wide = lambda a: a.rearrange("p (k t) -> p k t", k=KD)
                self.xn, self.xT = as_tok(areas[0]), as_wide(areas[1])
                self.k, self.o, self.qT = as_tok(areas[0]), as_tok(areas[0]), as_wide(areas[1])
                self.q_flat, self.q, self.y, self.v = areas[2], as_tok(areas[2]), as_tok(areas[2]), as_tok(areas[3])
                self.kT, self.hT = as_wide(areas[4]), as_wide(areas[4])
                self.outer = areas[5][:, 0:KD * P].rearrange("p (k e) -> p k e", k=KD)
                self.never = areas[5][:, KD * P:KD * P + SEQ]
                self.mask = self.never.bitcast(I32)
                self.head_max = areas[5][:, 1280:1280 + TT * HEADS]
                self.head_inv = areas[5][:, 1408:1408 + TT * HEADS]
                self.k_neg_max, self.k_den, self.k_inv = (scalars[:, n * KD:(n + 1) * KD] for n in range(3))

        half_slot = TT * D
        L2 = [Layer2([slots[:, n, a:a + half_slot] for n in (A, B, C) for a in (0, half_slot)], small[:, 0:3 * KD]),
              Layer2([wl1[:, n * half_slot:(n + 1) * half_slot] for n in range(4)] +
                     [hflat[:, n * half_slot:(n + 1) * half_slot] for n in range(2)], small[:, 3 * KD:6 * KD])]

        def part(flat, dims, **kw):
            return flat.rearrange(dims, **kw)

        x3, x3T = part(wl1[:, 0:2048], "p (i d) -> p i d", i=TT), part(wl1[:, 2048:4096], "p (k t) -> p k t", k=KD)
        q3T, k3T = (part(wl1[:, a:a + 2048], "p (k t) -> p k t", k=KD) for a in (4096, 6144))
        v3 = [part(hflat[:, b * 2048:(b + 1) * 2048], "p (i d) -> p i d", i=TT) for b in range(BATCH)]
        rest3 = wl1[:, 0:2048]
        q_parts = [slots[:, F, n * 1024:n * 1024 + 1024].bitcast(BF16) for n in range(3)]
        k_parts = [slots[:, F, 3072:4096].bitcast(BF16), wl1[:, 2048:3072].bitcast(BF16), wl1[:, 3072:4096].bitcast(BF16)]
        stacks = [slots[:, n, :].bitcast(BF16).rearrange("p (s h t) -> p s h t", s=2, h=QH) for n in range(QUADS)]
        y3 = [part(wl1[:, b * 2048:(b + 1) * 2048], "p (i d) -> p i d", i=TT) for b in range(BATCH)]
        h3T = [part(wl1[:, a:a + 2048], "p (k t) -> p k t", k=KD) for a in (4096, 6144)]
        v_quad = [part(wl1[:, a:a + 1024], "p (i h c) -> p i h c", i=TT, h=QH) for a in (4096, 5120)]
        oT = wl1[:, 6144:7168]
        o3 = [tok(F, b) for b in range(BATCH)]
        probs = slots[:, F, :].rearrange("p (n t) -> p n t", n=4)
        half_max = gain[:, 0:2 * UNITS].rearrange("p (a u) -> p a u", a=2)
        row_max, neg_max = gain[:, 2 * UNITS:3 * UNITS], gain[0:UNITS, P:2 * P]
        max_rest = shift[0:UNITS, 0:P]
        max_parts = [shift[0:UNITS, P:P + 64].bitcast(BF16), shift[0:UNITS, P + 64:2 * P].bitcast(BF16),
                     heads[0:UNITS, 0:64].bitcast(BF16)]
        inv3 = head_scale[:, :].rearrange("p (i h) -> p i h", i=TT)

        def sync_layer2(sp):
            for b in range(BATCH):
                sp.dma_start(L2[b].mask, mask2_row[b:b + 1, :].to_broadcast([P, SEQ])).then_inc(ld_mask2, 16)

        def sync_layer3(sp):
            for b in range(BATCH):
                if b:
                    sp.wait_ge(mask_split, b)
                sp.dma_start(bc_raw, mask3_row[b:b + 1, :].to_broadcast([XP - RANK, SEQ])).then_inc(ld_mask3, 16)
                sp.wait_ge(mask_split, b + 1)
                for n in range(3):
                    sp.dma_start(scr_mask[b, n:n + 1, :], bcs[2 * NS * n:2 * NS * n + 1, :]).then_inc(mask_stored, 16)
                sp.wait_ge(mask_stored, 48 * (b + 1))

            def store_parts(b):
                for side, parts in enumerate((q_parts, k_parts)):
                    sp.wait_ge(qk_split, 2 * b + side + 1)
                    for n in range(3):
                        sp.dma_start(scr_qk[b, side, n].rearrange("(k p) t -> p k t", p=P),
                                     parts[n].rearrange("p (k t) -> p k t", k=KD)).then_inc(parts_stored, 16)
                sp.wait_ge(parts_stored, 96 * (b + 1))

            def load_stack(job):
                b, quad = job // QUADS, job % QUADS
                for r, pair in enumerate(TERMS):
                    for side in range(2):
                        src = scr_qk[b, side, pair[side]].rearrange("(g h d) t -> g d h t", g=QUADS, d=HD)[quad]
                        sp.dma_start(stacks[quad][r * HD:(r + 1) * HD, side], src).then_inc(ld_stack[quad], 16)
                mask_src = scr_mask[b].rearrange("r (o t) -> r o t", o=1).to_broadcast([3, QH, SEQ])
                sp.dma_start(stacks[quad][K_MAX - 3:K_MAX, 1], mask_src).then_inc(ld_stack[quad], 16)

            def load_max(job):
                sp.wait_ge(max_split, job + 1)
                for n in range(3):
                    sp.dma_start(scr_max[job, n], max_parts[n]).then_inc(max_stored, 16)
                sp.wait_ge(max_stored, 48 * (job + 1))
                quad = job % QUADS
                sp.dma_start(stacks[quad][K_MAX:K_EXP, 0], scr_max[job].rearrange("r (h i) n -> r h (i n)", i=TT)).then_inc(ld_max[quad], 16)

            store_parts(0)
            sp.wait_ge(ones_set, 1)
            for job in range(QUADS):
                load_stack(job)
            store_parts(1)
            for job in range(AHEAD):
                load_max(job)
            for job in range(JOBS):
                if job + AHEAD < JOBS:
                    load_max(job + AHEAD)
                if job + QUADS < JOBS:
                    sp.wait_ge(shifted, (job + 1) * UNITS)
                    load_stack(job + QUADS)

        def pool_chunk(pool, s, c):
            cc = s * CHUNKS + c

            def state(n, k):
                pool.wait_ge(c_out, cc * NS + n + 1)
                for p in range(PAIRS):
                    if c < CHUNKS - 1:
                        pool.wait_ge(saved, s * (CHUNKS - 1) * NS * PAIRS + n * PAIRS + p + 1)
                    else:
                        pool.wait_ge(scanned, cc * NS * KE + n * KE + 2 * p + 2)
                    h = hbuf[:, k, 2 * p:2 * p + 2, :]
                    pool.tensor_tensor(h, h, cbuf[:, k:k + 1, :].to_broadcast([P, 2, TC]), ALU.mult).then_inc(weighed, 1)

            with pool.Fori(0, NS // 2) as i:
                for k in range(2):
                    state(i * 2 + k, k)

        def pool_attention(pool):
            pool.wait_ge(x_updated, 3 * BATCH)
            pool.memset(slots[96:K_EXP, A:E + 1, :], TWO_ONES).then_inc(ones_set, 1)
            pool.wait_ge(ones_set, 1)
            pool.wait_ge(qk_split, 2 * BATCH)
            for n in range(2):
                ins = pool.memset(v_quad[n], 0.0)
            ins.then_inc(quads_clear, 1)
            pool.wait_ge(quads_clear, 1)
            for n in range(2):
                ins = pool.memset(v_quad[n][:, :, :, HD:HD + 1], 1.0)
            ins.then_inc(quads_clear, 1)
            for job in range(JOBS):
                b, quad = job // QUADS, job % QUADS
                pool.wait_ge(v3_ready, b + 1)
                if job == 0:
                    pool.wait_ge(quads_clear, 2)
                if job >= 2:
                    pool.wait_ge(weighed_v, (job - 1) * UNITS + 4)
                pool.tensor_copy(v_quad[job % 2][:, :, :, 0:HD],
                                 v3[b].rearrange("p i (g h d) -> p i g h d", g=QUADS, d=HD)[:, :, quad]).then_inc(v_quad_ready, 1)

        def tensor_attention(pe, bank, to_wide, project, to_tokens):
            w2, w3 = (wl23[:, n, :].rearrange("p (w k m) -> p w k m", w=4, k=KD) for n in range(2))
            if LAYERS < 3:
                return
            pe.wait_ge(ld_w23, 48)
            for b in range(BATCH):
                pe.wait_ge(xn_ready, 2 * BATCH + b + 1)
                to_wide(FIRST["2xT", b], L2[b].xn)
            for b in range(BATCH):
                pe.wait_ge(evac, FIRST["2xT", b] + 4)
                to_tokens(FIRST["2q", b], L2[b].xT, w2[:, 0], KD)
                to_tokens(FIRST["2v", b], L2[b].xT, w2[:, 2], KD)
                project(FIRST["2kT", b], w2[:, 1], L2[b].xT, KD, KD)
            for b in range(BATCH):
                pe.wait_ge(kn_ready, b + 1)
                g = FIRST["2k", b]
                for pair in range(TT // 2):
                    ps = bank(g)
                    for q in range(2):
                        t0 = (pair * 2 + q) * P
                        for k in range(KD):
                            last = pe.transpose(ps[:, q * D + k * P:q * D + (k + 1) * P], L2[b].kT[:, k, t0:t0 + P], ident[:, :])
                    last.then_inc(prod, 1)
                    g += 1
            for b in range(BATCH):
                pe.wait_ge(evac, FIRST["2k", b] + 4)
                pe.wait_ge(v_ready, b + 1)
                ps = bank(FIRST["2m", b])
                for k in range(KD):
                    for i in range(TT):
                        last = pe.matmul(ps[:, k * P:(k + 1) * P], L2[b].v[:, i, k * P:(k + 1) * P],
                                         L2[b].k[:, i, k * P:(k + 1) * P], start=i == 0, stop=i == TT - 1)
                last.then_inc(prod, 1)
            for b in range(BATCH):
                pe.wait_ge(qn_ready, b + 1)
                to_wide(FIRST["2qT", b], L2[b].q)
            for b in range(BATCH):
                pe.wait_ge(evac, FIRST["2qT", b] + 4)
                pe.wait_ge(outer_ready, b + 1)
                g = FIRST["2y", b]
                for pair in range(TT // 2):
                    ps = bank(g)
                    for q in range(2):
                        t0 = (pair * 2 + q) * P
                        for k in range(KD):
                            last = pe.matmul(ps[:, q * D + k * P:q * D + (k + 1) * P], L2[b].qT[:, k, t0:t0 + P],
                                             L2[b].outer[:, k, :], start=True, stop=True)
                    last.then_inc(prod, 1)
                    g += 1
            film_products(pe, "2", 0, [m.y for m in L2], [m.hT for m in L2], w2[:, 3], to_wide, to_tokens)
            if LAYERS < 4:
                return
            pe.sem_inc(weighed_v, 4)
            for b in range(BATCH):
                pe.wait_ge(xn_ready, 3 * BATCH + b + 1)
                to_wide(FIRST["3xT", b], x3)
                pe.wait_ge(evac, FIRST["3qT", b])
                project(FIRST["3qT", b], w3[:, 0], x3T, KD, KD)
                to_tokens(FIRST["3v", b], x3T, w3[:, 2], KD)
                project(FIRST["3kT", b], w3[:, 1], x3T, KD, KD)
            pe.wait_ge(evac, FIRST["3hT", 0])

            def max_tile(job, i, n, banks):
                st, h, half = stacks[job % QUADS], n // 2, n % 2
                lhs = st[0:K_MAX, 0, h, bass.ds(i * P, P)] if not isinstance(i, int) else st[0:K_MAX, 0, h, i * P:(i + 1) * P]
                pe.wait_ge(maxed, i * (2 * QH) + (job * 2 * UNITS + n + 5 - banks))
                pe.matmul(psum[:, 8 - banks + n % banks, :], lhs, st[0:K_MAX, 1, h, half * 512:half * 512 + 512],
                          start=True, stop=True).then_inc(scored, 1)

            def start_max(job):
                pe.wait_ge(ld_stack[job % QUADS], 16 * LOADS * (job // QUADS + 1))
                if job:
                    pe.wait_ge(max_read, job)

            def turn_max(job):
                pe.wait_ge(max_found, job + 1)
                pe.transpose(psum[0:UNITS, 6, 0:P], row_max, ident[:, :]).then_inc(max_turned, 1)

            def scores(job, i, h):
                st = stacks[job % QUADS]
                lhs = st[0:K_EXP, 1, h, bass.ds(i * P, P)] if not isinstance(i, int) else st[0:K_EXP, 1, h, i * P:(i + 1) * P]
                pe.wait_ge(exped, i * QH + (job * UNITS + h + 1))
                for half in range(2):
                    last = pe.matmul(psum[:, 2 + h % 2 * 2 + half, :], lhs, st[0:K_EXP, 0, h, half * 512:half * 512 + 512],
                                     start=True, stop=True)
                last.then_inc(shifted, 1)

            def first_scores(job):
                pe.wait_ge(ld_max[job % QUADS], 16 * (job // QUADS + 1))
                scores(job, 0, 0)
                scores(job, 0, 1)

            def weigh(job, i, h, half):
                if half == 0:
                    if i == 0 and h == 0:
                        pe.wait_ge(v_quad_ready, job + 1)
                        pe.wait_ge(normalized, job + 1)
                    pe.wait_ge(exped, job * UNITS + i * QH + h + 3)
                ins = pe.matmul(psum[h * 32:h * 32 + 32, half, :], v_quad[job % 2][:, i, h, :],
                                probs[:, h, half * 512:half * 512 + 512], start=i == 0, stop=i == TT - 1)
                if half:
                    ins.then_inc(weighed_v, 1)

            for job in range(AHEAD):
                start_max(job)
                with pe.Fori(0, TT) as i:
                    for n in range(2 * QH):
                        max_tile(job, i, n, 4)
                turn_max(job)
            first_scores(0)
            for job in range(JOBS):
                ahead = job + AHEAD < JOBS
                if ahead:
                    start_max(job + AHEAD)
                for i in range(TT):
                    half_tiles = iter(range(2 * QH))
                    for h in range(QH):
                        for half in range(2):
                            if ahead and (h, half) != (1, 1):
                                max_tile(job + AHEAD, i, next(half_tiles), 2)
                            if half == 0 and i + (h + 2) // QH < TT:
                                scores(job, i + (h + 2) // QH, (h + 2) % QH)
                            if h == 0 and half == 0:
                                if ahead:
                                    max_tile(job + AHEAD, i, next(half_tiles), 2)
                            weigh(job, i, h, half)
                if ahead:
                    turn_max(job + AHEAD)
                if job + 1 < JOBS:
                    first_scores(job + 1)
                pe.wait_ge(o_out, job + 1)
                for i in range(TT):
                    last = pe.transpose(psum[:, i // 4, i % 4 * P:(i % 4 + 1) * P], oT[:, i * P:(i + 1) * P], ident[:, :])
                last.then_inc(o_turned, 1)
            pe.wait_ge(normalized, JOBS + 1)
            film_products(pe, "3", 1, y3, h3T, w3[:, 3], to_wide, to_tokens)

        def film_products(pe, layer, n, h, hT, w, to_wide, to_tokens):
            for b in range(BATCH):
                pe.wait_ge(h_ready, n * BATCH + b + 1)
                to_wide(FIRST[layer + "hT", b], h[b])
            for b in range(BATCH):
                pe.wait_ge(evac, FIRST[layer + "hT", b] + 4)
                to_tokens(FIRST[layer + "out", b], hT[b], w, KD)

        def scalar_attention(act, move, wide_out, tokens_out, project_out, deviation, link):
            if LAYERS < 3:
                return
            for b in range(BATCH):
                deviation()
                wide_out(FIRST["2xT", b], L2[b].xT)
            for b in range(BATCH):
                tokens_out(FIRST["2q", b], L2[b].q)
                tokens_out(FIRST["2v", b], L2[b].v)
                project_out(FIRST["2kT", b], L2[b].kT, KD, bias=C_BK2)
            for b in range(BATCH):
                act.wait_ge(q_shifted, b + 1)
                act.activation(L2[b].q_flat, L2[b].q_flat, ACT.Exp).then_inc(q_exp, 1)
                act.wait_ge(k_masked, b + 1)
                for k in range(KD):
                    ins = act.activation(L2[b].kT[:, k, :], L2[b].kT[:, k, :], ACT.Exp, bias=L2[b].k_neg_max[:, k:k + 1],
                                         accum_out=L2[b].k_den[:, k:k + 1])
                ins.then_inc(k_exp, 1)
            for b in range(BATCH):
                tokens_out(FIRST["2k", b], L2[b].k)
            for b in range(BATCH):
                g = FIRST["2m", b]
                move(g, L2[b].outer, psum[:, g % 8, 0:KD * P].rearrange("p (k e) -> p k e", k=KD))
            for b in range(BATCH):
                wide_out(FIRST["2qT", b], L2[b].qT)
            for b in range(BATCH):
                tokens_out(FIRST["2y", b], L2[b].y)
            film_moves(act, "2", 0, [m.y for m in L2], [m.hT for m in L2], [m.o for m in L2], wide_out, tokens_out, deviation)
            if LAYERS < 4:
                return
            act.sem_inc(exped, 2)
            for b in range(BATCH):
                deviation()
                if b:
                    act.wait_ge(parts_stored, 96 * b)
                wide_out(FIRST["3xT", b], x3T)
                project_out(FIRST["3qT", b], q3T, KD, bias=C_BQ3)
                act.wait_ge(mask_split, BATCH)
                tokens_out(FIRST["3v", b], v3[b])
                project_out(FIRST["3kT", b], k3T, KD, bias=C_BK3)
            act.wait_ge(parts_stored, 96 * BATCH)
            for job in range(JOBS):
                with act.Fori(0, TT) as i:
                    for h in range(QH):
                        act.wait_ge(shifted, i * QH + (job * UNITS + h + 1))
                        act.wait_ge(weighed_v, i * QH + (job * UNITS + h + 1))
                        act.activation(probs[:, h, :], psum[:, 2 + h % 2 * 2:4 + h % 2 * 2, :].rearrange("p a t -> p (a t)"),
                                       ACT.Exp).then_inc(exped, 1)
            film_moves(act, "3", 1, y3, h3T, o3, wide_out, tokens_out, deviation)

        def film_moves(act, layer, n, h, hT, o, wide_out, tokens_out, deviation):
            for b in range(BATCH):
                deviation()
                act.wait_ge(h_conditioned, n * BATCH + b + 1)
                act.activation(h[b], h[b], ACT.Silu).then_inc(h_ready, 1)
                wide_out(FIRST[layer + "hT", b], hT[b])
            for b in range(BATCH):
                tokens_out(FIRST[layer + "out", b], o[b])

        def vector_attention(dve, link, normalize, condition, split_rows):
            def affine(t, at):
                link(dve.tensor_tensor(t, t, per_column(rows[:, at:at + D]), ALU.mult))
                return dve.tensor_tensor(t, t, per_column(rows[:, at + D:at + 2 * D]), ALU.add)

            def film(layer, n, h, o):
                for b in range(BATCH):
                    normalize(h[b], h[b])
                    condition((ada[:, b, 0:D], ada[:, b, D:2 * D]), b, R_FG, R_FB, h[b]).then_inc(h_conditioned, 1)
                    dve.wait_ge(h_conditioned, n * BATCH + b + 1)
                for b in range(BATCH):
                    dve.wait_ge(evac, FIRST[layer + "out", b] + 4)
                    xb = xt[:, b * TT:(b + 1) * TT, :]
                    link(dve.tensor_tensor(o[b], o[b], per_column(rows[:, R_OB:R_OB + D]), ALU.add))
                    dve.tensor_tensor(xb, xb, o[b], ALU.add).then_inc(x_updated, 1)
                dve.wait_ge(x_updated, (int(layer) + 1) * BATCH)

            by_head = lambda t: t.rearrange("p i (h d) -> p (i h) d", d=HD)
            over_head = lambda v: v.rearrange("p (n o) -> p n o", o=1).to_broadcast([P, TT * HEADS, HD])
            if LAYERS < 3:
                return
            dve.wait_ge(x_updated, 2 * BATCH)
            dve.sem_inc(rows_used, 1)
            dve.wait_ge(ld_w23, 48)
            dve.tensor_scalar(keep2[:, :], m2c[:, :], 1.0, None, ALU.not_equal)
            for b in range(BATCH):
                xb = xt[:, b * TT:(b + 1) * TT, :]
                normalize(xb, L2[b].xn)
                if b == 0:
                    dve.wait_ge(ld_rows, 32)
                    dve.wait_ge(ld_adarows, 96)
                affine(L2[b].xn, R_NG).then_inc(xn_ready, 1)
            dve.wait_ge(ld_mask2, 16 * BATCH)
            for b in range(BATCH):
                dve.tensor_scalar(L2[b].never, L2[b].mask, 1.0, NEVER, ALU.is_equal, ALU.mult)
            for b in range(BATCH):
                m = L2[b]
                dve.wait_ge(evac, FIRST["2q", b] + 4)
                link(dve.tensor_tensor(m.q, m.q, per_column(rows[:, R_BQ:R_BQ + D]), ALU.add))
                link(dve.tensor_reduce(m.head_max, by_head(m.q), AX.X, ALU.max))
                dve.tensor_tensor(by_head(m.q), by_head(m.q), over_head(m.head_max), ALU.subtract).then_inc(q_shifted, 1)
                dve.wait_ge(evac, FIRST["2v", b] + 4)
                link(dve.tensor_tensor(m.v, m.v, per_column(rows[:, R_BV:R_BV + D]), ALU.add))
                dve.tensor_tensor(m.v, m.v, per_token(keep2[:, b * TT:(b + 1) * TT]), ALU.mult).then_inc(v_ready, 1)
                dve.wait_ge(evac, FIRST["2kT", b] + 4)
                link(dve.tensor_tensor(m.kT, m.kT, m.never.rearrange("p (o t) -> p o t", o=1).to_broadcast([P, KD, SEQ]), ALU.add))
                dve.tensor_reduce(m.k_neg_max, m.kT, AX.X, ALU.max, negate=True).then_inc(k_masked, 1)
            for b in range(BATCH):
                m = L2[b]
                dve.wait_ge(k_exp, b + 1)
                link(dve.reciprocal(m.k_inv, m.k_den))
                for k in range(KD):
                    ins = dve.tensor_scalar(m.kT[:, k, :], m.kT[:, k, :], m.k_inv[:, k:k + 1], None, ALU.mult)
                ins.then_inc(kn_ready, 1)
                dve.wait_ge(q_exp, b + 1)
                link(dve.tensor_reduce(m.head_inv, by_head(m.q), AX.X, ALU.add))
                link(dve.reciprocal(m.head_inv, m.head_inv))
                dve.tensor_tensor(by_head(m.q), by_head(m.q), over_head(m.head_inv), ALU.mult).then_inc(qn_ready, 1)
            for b in range(BATCH):
                dve.wait_ge(evac, FIRST["2m", b] + 1)
                dve.tensor_tensor(L2[b].outer, L2[b].outer, heads[:, :].rearrange("p (o e) -> p o e", o=1).to_broadcast([P, KD, P]),
                                  ALU.mult).then_inc(outer_ready, 1)
            dve.wait_ge(evac, FIRST["2y", BATCH - 1] + 4)
            film("2", 0, [m.y for m in L2], [m.o for m in L2])
            if LAYERS < 4:
                return
            dve.sem_inc(rows_used, 1)
            dve.sem_inc(maxed, 4)
            dve.sem_inc(normalized, 1)

            def split_mask(b):
                dve.wait_ge(ld_mask3, 16 * (b + 1))
                if b:
                    dve.wait_ge(mask_stored, 48 * b)
                link(dve.tensor_scalar(bc_raw, bc_raw, 1.0, -MASKED, ALU.subtract, ALU.mult))
                split_rows().then_inc(mask_split, 1)

            for b in range(BATCH):
                xb = xt[:, b * TT:(b + 1) * TT, :]
                if b:
                    dve.wait_ge(evac, FIRST["3xT", b - 1] + 4)
                normalize(xb, x3)
                if b == 0:
                    dve.wait_ge(ld_rows, 48)
                    dve.wait_ge(ld_adarows, 128)
                affine(x3, R_NG).then_inc(xn_ready, 1)
                if b == 0:
                    for n in range(BATCH):
                        split_mask(n)
                for side, (src, parts) in enumerate(((q3T, q_parts), (k3T, k_parts))):
                    dve.wait_ge(evac, FIRST[("3qT", "3kT")[side], b] + 4)
                    if b and side == 0:
                        dve.wait_ge(parts_stored, 96 * b)
                    flat = src.rearrange("p k t -> p (k t)")
                    link(dve.tensor_copy(parts[0], flat))
                    link(dve.tensor_tensor(rest3, flat, parts[0], ALU.subtract))
                    link(dve.tensor_copy(parts[1], rest3))
                    dve.tensor_tensor(parts[2], rest3, parts[1], ALU.subtract).then_inc(qk_split, 1)
                    dve.wait_ge(qk_split, 2 * b + side + 1)
                token_mask = m3c[:, b * TT:(b + 1) * TT].rearrange("p (i o) -> p i o", o=1).to_broadcast([P, TT, D])
                link(dve.tensor_tensor(v3[b], v3[b], per_column(rows[:, R_BV:R_BV + D]), ALU.add))
                dve.tensor_tensor(v3[b], v3[b], token_mask, ALU.mult).then_inc(v3_ready, 1)

            def find_max(job, banks):
                with dve.Fori(0, TT) as i:
                    for h in range(QH):
                        for half in range(2):
                            dve.wait_ge(scored, i * (2 * QH) + (job * 2 * UNITS + 2 * h + half + 1))
                            dve.tensor_reduce(half_max[:, half, bass.ds(i + h * TT, 1)], psum[:, 8 - banks + (2 * h + half) % banks, :],
                                              AX.X, ALU.max).then_inc(maxed, 1)
                dve.wait_ge(maxed, (job + 1) * 2 * UNITS + 4)
                if job:
                    dve.wait_ge(max_turned, job)
                dve.tensor_tensor(row_max, half_max[:, 0, :], half_max[:, 1, :], ALU.max).then_inc(max_found, 1)

            def split_max(job):
                dve.wait_ge(max_turned, job + 1)
                ins = dve.tensor_scalar(neg_max, psum[0:UNITS, 6, 0:P], -1.0, None, ALU.mult)
                ins.then_inc(max_read, 1)
                dve.wait_ge(max_read, job + 1)
                if job:
                    dve.wait_ge(max_stored, 48 * job)
                link(dve.tensor_copy(max_parts[0], neg_max))
                link(dve.tensor_tensor(max_rest, neg_max, max_parts[0], ALU.subtract))
                link(dve.tensor_copy(max_parts[1], max_rest))
                dve.tensor_tensor(max_parts[2], max_rest, max_parts[1], ALU.subtract).then_inc(max_split, 1)

            for job in range(AHEAD):
                find_max(job, 4)
                split_max(job)
            for job in range(JOBS):
                b, quad = job // QUADS, job % QUADS
                ahead = job + AHEAD < JOBS
                if ahead:
                    find_max(job + AHEAD, 2)
                dve.wait_ge(weighed_v, (job + 1) * UNITS + 4)
                dve.tensor_copy(oT, psum[:, 0:2, :].rearrange("p a t -> p (a t)")).then_inc(o_out, 1)
                if ahead:
                    split_max(job + AHEAD)
                dve.wait_ge(o_turned, job + 1)
                sums = psum[:, 0:2, :].rearrange("p a (i h c) -> p (a i) h c", h=QH, c=32)
                dve.reciprocal(inv3, sums[:, :, :, HD:HD + 1].rearrange("p i h o -> p i (h o)")).then_inc(inverted, 1)
                dve.wait_ge(inverted, job + 1)
                dst = y3[b].rearrange("p i (g h d) -> p i g h d", g=QUADS, d=HD)[:, :, quad]
                dve.tensor_tensor(dst, sums[:, :, :, 0:HD], inv3.rearrange("p i (h o) -> p i h o", o=1)
                                  .to_broadcast([P, TT, QH, HD]), ALU.mult).then_inc(normalized, 1)
            dve.wait_ge(normalized, JOBS + 1)
            film("3", 1, y3, o3)

        block = ctx.enter_context(nc.Block())

        @block.sync
        def _(sp):
            parts = (slice(0, ADA[0]), slice(ADA[0], NADA))
            x_in = x.rearrange("b (i p) d -> p b i d", p=P)

            def load_x(b):
                sp.dma_start(xt[:, b * TT:(b + 1) * TT, :], x_in[:, b]).then_inc(ld_x[b], 16)

            def load_conditioning(n):
                sp.dma_start(adab[n], ada_b[:, parts[n]].to_broadcast([BATCH, parts[n].stop - parts[n].start])).then_inc(ld_ada[n], 16)
                sp.dma_start(adaw[n], ada_w[:, :, parts[n]]).then_inc(ld_ada[n], 16)

            def store_conditioning(n):
                sp.wait_ge(ada_ready, n + 1)
                sp.dma_start(scr_ada[:, parts[n]], adas[n]).then_inc(ada_stored, 16)

            sp.dma_start(sct[:, :, :], cond_t).then_inc(ld_small, 16)
            sp.dma_start(cols[:, :], cols_in).then_inc(ld_small, 16)
            load_conditioning(0)
            load_x(0)
            sp.dma_start(rows[:, :], rows_in[0:1, :].to_broadcast([P, NROWS])).then_inc(ld_rows, 16)
            sp.dma_start(w0s[:, 0:NW0], w0).then_inc(ld_w0, 16)
            sp.dma_start(wdts[:, :, :], wdt).then_inc(ld_w0, 16)
            store_conditioning(0)
            sp.wait_ge(ada_stored, 16)
            for layer in range(LAYERS):
                if layer:
                    sp.wait_ge(rows_used, layer)
                for b in range(BATCH):
                    src = scr_ada[b:b + 1, ADA0[layer]:ADA0[layer] + ADA[layer]]
                    sp.dma_start(ada[:, b, 0:ADA[layer]], src.to_broadcast([P, ADA[layer]])).then_inc(ld_adarows, 16)
                if layer == 0:
                    load_x(1)
                    load_conditioning(1)
                    sp.dma_start(m2c[:, :], mask2_col).then_inc(ld_w23, 16)
                    sp.dma_start(m3c[:, :], mask3_col).then_inc(ld_w23, 16)
                    store_conditioning(1)
                    sp.dma_start(wl1[:, 0:NW1], w1).then_inc(ld_w1, 16)
                    sp.wait_ge(ada_stored, 32)
                    sp.dma_start(wl23[:, :, :], w23).then_inc(ld_w23, 16)
                if layer >= 2:
                    sp.dma_start(rows[:, :], rows_in[layer - 1:layer, :].to_broadcast([P, NROWS])).then_inc(ld_rows, 16)
                if layer == 2:
                    sync_layer2(sp)
                if layer == 3:
                    sync_layer3(sp)
            for b in range(BATCH):
                sp.wait_ge(x_updated, LAYERS * BATCH - BATCH + b + 1)
                sp.dma_start(out[b].rearrange("(i p) d -> p i d", p=P), xt[:, b * TT:(b + 1) * TT, :]).then_inc(stored, 16)
            sp.wait_ge(stored, 16 * BATCH)

        @block.gpsimd
        def _(pool):
            pool.memset(ident[:, :], 0.0).then_inc(made, 1)
            pool.memset(pick[:, :], 0.0).then_inc(made, 1)
            pool.memset(heads[:, :], 1.0).then_inc(made, 1)
            pool.wait_ge(made, 3)
            pool.affine_select(out=ident[:, :], in_=ident[:, :], compare_op=ALU.not_equal, fill=1.0, base=0,
                               pattern=[[-1, P]], channel_multiplier=1).then_inc(made, 1)
            for part in range(3):
                pool.affine_select(out=pick[:, :], in_=pick[:, :], compare_op=ALU.not_equal, fill=1.0,
                                   base=-2 * NS * part, pattern=[[-1, 2 * NS]], channel_multiplier=1).then_inc(made, 1)
                pool.wait_ge(made, 5 + part)
            by_head = heads[:, :].rearrange("p (j d) -> p j d", d=HD)
            pool.affine_select(out=by_head, in_=by_head, compare_op=ALU.is_ge, fill=0.0, base=0,
                               pattern=[[-HD, P // HD], [0, HD]], channel_multiplier=1).then_inc(made, 1)
            pool.wait_ge(made, 8)
            pool.affine_select(out=by_head, in_=by_head, compare_op=ALU.is_ge, fill=0.0, base=HD - 1,
                               pattern=[[HD, P // HD], [0, HD]], channel_multiplier=-1).then_inc(made, 1)
            pool.wait_ge(made, 9)
            pool.memset(eps[:, :], EPS).then_inc(consts_ready, 1)

            for s in range(len(SCANS) if LAYERS > 1 else 2):
                for c in range(CHUNKS):
                    pool_chunk(pool, s, c)
            if LAYERS == 4:
                pool_attention(pool)

        @block.tensor
        def _(pe):
            def bank(g):
                if g >= 8:
                    pe.wait_ge(evac, g - 7)
                return psum[:, g % 8, :]

            def to_wide(g, src):
                for k in range(KD):
                    for half in range(2):
                        ps = bank(g)
                        for q in range(4):
                            last = pe.transpose(ps[:, q * P:(q + 1) * P], src[:, half * 4 + q, k * P:(k + 1) * P], ident[:, :])
                        last.then_inc(prod, 1)
                        g += 1

            def project(g, w, src, m_tiles, k_tiles, m=P):
                for mt in range(m_tiles):
                    for half in range(2):
                        ps = bank(g)
                        for k in range(k_tiles):
                            last = pe.matmul(ps[0:m, :], w[:, k, mt * m:(mt + 1) * m], src[:, k, half * 512:half * 512 + 512],
                                             start=k == 0, stop=k == k_tiles - 1)
                        last.then_inc(prod, 1)
                        g += 1

            def to_tokens(g, src, w, k_tiles):
                for pair in range(TT // 2):
                    ps = bank(g)
                    for q in range(2):
                        t0 = (pair * 2 + q) * P
                        for k in range(k_tiles):
                            last = pe.matmul(ps[:, q * D:(q + 1) * D], src[:, k, t0:t0 + P], w[:, k, :],
                                             start=k == 0, stop=k == k_tiles - 1)
                    last.then_inc(prod, 1)
                    g += 1

            def conditioning(n):
                pe.wait_ge(ld_ada[n], 32)
                for g, (at, size) in enumerate(ADA_PIECES[n]):
                    ps = bank(FIRST["ada", n] + g)
                    for k in range(KE):
                        a0 = at - ADA0[n]
                        last = pe.matmul(ps[0:BATCH, 0:size], sct[:, k, :], adaw[n][:, k, a0:a0 + size], start=k == 0, stop=k == KE - 1)
                    last.then_inc(prod, 1)

            pe.wait_ge(sct_ready, 1)
            conditioning(0)
            pe.wait_ge(consts_ready, 1)
            pe.wait_ge(ld_w0, 32)
            w_in = w0s[:, W0_IN:W0_XP].rearrange("p (k m) -> p k m", k=KD)
            w_xp = w0s[:, W0_XP:W0_OUT].rearrange("p (k m) -> p k m", k=KE)
            w_out = w0s[:, W0_OUT:NW0].rearrange("p (k m) -> p k m", k=KE)

            def scan_inputs(s, b, xp, dt, wx, wt, src):
                project(FIRST[xp, b], wx, src, 1, KE, XP)
                pe.wait_ge(evac, FIRST[xp, b] + 2)
                g = FIRST[dt, b]
                for mt in range(KE):
                    for half in range(2):
                        pe.matmul(bank(g), wt[:, mt * P:(mt + 1) * P], dt_low[:, half * 512:half * 512 + 512],
                                  start=True, stop=True).then_inc(prod, 1)
                        g += 1
                pe.wait_ge(evac, g)
                pe.wait_ge(bc_ready, s + 1)
                for c in range(CHUNKS):
                    chunk(s, c)
                pe.wait_ge(y_out, (s + 1) * CHUNKS * KE)

            def chunk(s, c):
                _, b, which, slot, backward = SCANS[s]
                cc = s * CHUNKS + c
                at = (CHUNKS - 1 - c if backward else c) * TC

                def spread(n, c=c):
                    cc = s * CHUNKS + c
                    at = (CHUNKS - 1 - c if backward else c) * TC
                    if cc or not isinstance(n, int) or n:
                        pe.wait_ge(dbu, n * PAIRS + cc * NS * PAIRS)
                        pe.wait_ge(c_out, cc * NS + n)
                    for half in range(2):
                        row = pick[:, half * NS + n:half * NS + n + 1] if isinstance(n, int) else \
                            pick[:, bass.ds(n + half * NS, 1)]
                        last = pe.matmul(psum[:, 4 + half, :], row.to_broadcast([96, P]), bcs[:, at:at + TC],
                                         start=True, stop=True)
                    last.then_inc(bcast, 1)

                def add_state(n, k, pair, final=False):
                    for e in (2 * pair, 2 * pair + 1):
                        if e % 2 == 0:
                            pe.wait_ge(weighed, cc * NS * PAIRS + n * PAIRS + e // 2 + 1)
                        pe.matmul(psum[:, e, :], ident[:, :], hbuf[:, k, e, :], start=False, stop=final,
                                  skip_group_check=True).then_inc(summed, 1)

                if c == 0:
                    spread(0)
                src = chan(slot)
                for e in range(KE):
                    if c:
                        pe.wait_ge(y_out, (cc - 1) * KE + e + 1)
                    pe.matmul(psum[:, e, :], diag_d[:, which, e, :], src[:, e, at:at + TC], start=True, stop=False,
                              skip_group_check=True)
                if c == 0:
                    spread(1)
                with pe.Fori(0, NS // 2 - 1) as i:
                    for k in range(2):
                        add_state(i * 2 + k, k, 0)
                        spread(i * 2 + (k + 2))
                        add_state(i * 2 + k, k, 1)
                for k in range(2):
                    add_state(NS - 2 + k, k, 0, k == 1)
                    if c < CHUNKS - 1:
                        spread(k, c + 1)
                    add_state(NS - 2 + k, k, 1, k == 1)

            pe.wait_ge(a_ready, 1)
            for b in range(BATCH):
                pe.wait_ge(xn_ready, b + 1)
                to_wide(FIRST["0xT", b], tok(E, 0))
                pe.wait_ge(evac, FIRST["0in", b])
                project(FIRST["0in", b], w_in, wide(E, 1), 2 * KE, KD)
                pe.wait_ge(u_ready, (b + 1) * KE)
                scan_inputs(b, b, "0xp", "0dt", w_xp, wdts[:, 0, :], chan(C))
                pe.wait_ge(gated, (b + 1) * KE)
                to_tokens(FIRST["0out", b], chan(C), w_out, KE)
                if b == 0:
                    conditioning(1)

            if LAYERS < 2:
                return
            pe.wait_ge(ld_w1, 16)
            wx1 = wl1[:, W1_X:W1_Z].rearrange("p (k m) -> p k m", k=KD)
            wz1 = wl1[:, W1_Z:W1_C].rearrange("p (k m) -> p k m", k=KD)
            wc1 = wl1[:, W1_C:W1_XP].rearrange("p (d k m) -> p d k m", d=2, k=KE)
            wxp1 = wl1[:, W1_XP:W1_F].rearrange("p (d k m) -> p d k m", d=2, k=KE)
            wf1 = wl1[:, W1_F:NW1].rearrange("p (k m) -> p k m", k=KE)
            for b in range(BATCH):
                pe.wait_ge(xn_ready, BATCH + b + 1)
                to_wide(FIRST["1xT", b], tok(E, 0))
                pe.wait_ge(evac, FIRST["1xz", b])
                project(FIRST["1xz", b], wx1, wide(E, 1), KE, KD)
                project(FIRST["1xz", b] + 8, wz1, wide(E, 1), KE, KD)
                pe.wait_ge(evac, FIRST["1c", b])
                for d in range(2):
                    project(FIRST["1c", b] + 8 * d, wc1[:, d], chan(A), KE, KE)
                pe.wait_ge(evac, FIRST["1xp0", b])
                for d in range(2):
                    scan_inputs(2 + 2 * b + d, b, f"1xp{d}", f"1dt{d}", wxp1[:, d], wdts[:, 1 + d, :], chan((C, F)[d]))
                pe.wait_ge(gated, (BATCH + b + 1) * KE)
                to_tokens(FIRST["1out", b], chan(C), wf1, KE)
            tensor_attention(pe, bank, to_wide, project, to_tokens)

        @block.scalar
        def _(act):
            steps = [0]

            def link(ins):
                steps[0] += 1
                ins.then_inc(act_step, 1)
                act.wait_ge(act_step, steps[0])

            def move(g, dst, src=None, func=ACT.Identity, **kw):
                act.wait_ge(prod, g + 1)
                ps = psum[:, g % 8, :] if src is None else src
                act.activation(dst, ps, func, **kw).then_inc(evac, 1)

            def wide_out(g, dst):
                for k in range(KD):
                    for half in range(2):
                        move(g, dst[:, k, half * 512:half * 512 + 512])
                        g += 1

            def tokens_out(g, dst):
                for pair in range(TT // 2):
                    move(g, dst[:, pair * 2:pair * 2 + 2, :], psum[:, g % 8, :].rearrange("p (q d) -> p q d", q=2))
                    g += 1

            def project_out(g, dst, m_tiles, func=ACT.Identity, bias=None):
                for mt in range(m_tiles):
                    for half in range(2):
                        kw = {} if bias is None else {"bias": cols[:, bias + mt:bias + mt + 1]}
                        move(g, dst[:, mt, half * 512:half * 512 + 512], func=func, **kw)
                        g += 1

            norms = [0]

            def deviation():
                norms[0] += 1
                act.wait_ge(var_ready, norms[0])
                act.activation(std[:, :], mv[:, :, 1], ACT.Sqrt, bias=eps[:, 0:1]).then_inc(std_ready, 1)

            def scan_inputs(s, b, xp, dt, c_dtb):
                g = FIRST[xp, b]
                for half in range(2):
                    move(g + half, xp_out[:, half * 512:half * 512 + 512], psum[0:XP, (g + half) % 8, :])
                tmp = chan(E)
                for step in range(KE + 2):
                    if step < KE:
                        project_out(FIRST[dt, b] + 2 * step, chan(A)[:, step:step + 1, :], 1, bias=c_dtb + step)
                    if 0 <= step - 1 < KE:
                        e = step - 1
                        act.wait_ge(abs_ready, s * KE + e + 1)
                        act.activation(tmp[:, e, :], tmp[:, e, :], ACT.Exp).then_inc(exp_ready, 1)
                    if step >= 2:
                        e = step - 2
                        act.wait_ge(exp_ready, s * KE + e + 1)
                        act.activation(tmp[:, e, :], tmp[:, e, :], ACT.Ln, bias=1.0).then_inc(log_ready, 1)
                act.wait_ge(dt_ready, (s + 1) * KE)
                for c in range(CHUNKS):
                    chunk(s, c)

            def chunk(s, c):
                _, b, which, slot, backward = SCANS[s]
                cc = s * CHUNKS + c
                at = (CHUNKS - 1 - c if backward else c) * TC
                end = 0 if backward else TC - 1
                dt = chan(A)
                c_a = C_A if which == 0 else C_A1 + (which - 1) * KE * NS

                def state(n, k, first):
                    act.wait_ge(bcast, cc * NS + n + 1)
                    if not first:
                        act.wait_ge(weighed, cc * NS * PAIRS + (n - 1) * PAIRS)
                    elif cc:
                        act.wait_ge(weighed, (cc - 1) * NS * PAIRS + (NS - 1 + k) * PAIRS)
                    act.activation(cbuf[:, k, :], psum[:, 5, :], ACT.Identity).then_inc(c_out, 1)
                    for e in range(KE):
                        u = cc * NS * KE + n * KE + e
                        if not (isinstance(u, int) and u < 2):
                            act.wait_ge(scanned, u - 1)
                        a = cols[:, bass.ds(n + (c_a + e * NS), 1)] if not isinstance(n, int) else \
                            cols[:, c_a + e * NS + n:c_a + e * NS + n + 1]
                        if c < CHUNKS - 1 and e == 1 and not (first and k == 0):
                            save(n + (-1), 1 - k, 1)
                        if c < CHUNKS - 1 and e == 3:
                            save(n, k, 0)
                        act.activation(psum[:, 6 + e % 2, :], dt[:, e, at:at + TC], ACT.Exp, scale=a).then_inc(decay, 1)

                def save(n, k, pair):
                    col = hlast[:, 2 * pair:2 * pair + 2, n:n + 1] if isinstance(n, int) else \
                        hlast[:, 2 * pair:2 * pair + 2, bass.ds(n, 1)]
                    act.activation(col, hbuf[:, k, 2 * pair:2 * pair + 2, end:end + 1], ACT.Identity).then_inc(saved, 1)

                def sums_out(c):
                    cc = s * CHUNKS + c
                    at = (CHUNKS - 1 - c if backward else c) * TC
                    act.wait_ge(summed, (cc + 1) * NS * KE)
                    for e in range(KE):
                        act.activation(chan(slot)[:, e, at:at + TC], psum[:, e, :], ACT.Identity).then_inc(y_out, 1)

                state(0, 0, True)
                if c:
                    sums_out(c - 1)
                state(1, 1, True)
                with act.Fori(1, NS // 2) as i:
                    for k in range(2):
                        state(i * 2 + k, k, False)
                if c < CHUNKS - 1:
                    act.wait_ge(scanned, (cc + 1) * NS * KE)
                    save(NS - 1, 1, 1)
                else:
                    sums_out(c)

            def conditioning_out(n):
                for g, (at, size) in enumerate(ADA_PIECES[n], FIRST["ada", n]):
                    move(g, adas[n][:, at - ADA0[n]:at - ADA0[n] + size], psum[0:BATCH, g % 8, 0:size])

            act.wait_ge(ld_small, 32)
            act.activation(sct[:, :, :], sct[:, :, :], ACT.Silu).then_inc(sct_ready, 1)
            act.activation(cols[:, C_A:C_A + KE * NS], cols[:, C_A:C_A + KE * NS], ACT.Exp).then_inc(cols_ready, 1)
            act.activation(cols[:, C_A1:C_A1 + 2 * KE * NS], cols[:, C_A1:C_A1 + 2 * KE * NS], ACT.Exp).then_inc(cols_ready, 1)
            conditioning_out(0)
            act.wait_ge(consts_ready, 1)
            for b in range(BATCH):
                deviation()
                wide_out(FIRST["0xT", b], wide(E, 1))
                project_out(FIRST["0in", b], chan(A), KE)
                for e in range(KE):
                    act.wait_ge(conv_ready, b * KE + e + 1)
                    act.activation(chan(C)[:, e, :], chan(C)[:, e, :], ACT.Silu,
                                   bias=cols[:, C_CONVB + e:C_CONVB + e + 1]).then_inc(u_ready, 1)
                    project_out(FIRST["0in", b] + 8 + 2 * e, chan(B)[:, e:e + 1, :], 1, ACT.Silu)
                scan_inputs(b, b, "0xp", "0dt", C_DTB)
                tokens_out(FIRST["0out", b], tok(E, 0))
                if b == 0:
                    act.wait_ge(ld_ada[1], 32)
                    conditioning_out(1)
            if LAYERS < 2:
                return
            for b in range(BATCH):
                deviation()
                deviation()
                wide_out(FIRST["1xT", b], wide(E, 1))
                project_out(FIRST["1xz", b], chan(B), KE, ACT.Silu, C_BX)
                project_out(FIRST["1xz", b] + 8, chan(A), KE, bias=C_BZ)
                for d in range(2):
                    if d == 0:
                        act.wait_ge(skip_added, b + 1)
                    project_out(FIRST["1c", b] + 8 * d, chan((C, F)[d]), KE, bias=C_BC + d * KE)
                for d in range(2):
                    scan_inputs(2 + 2 * b + d, b, f"1xp{d}", f"1dt{d}", C_BDT + d * KE)
                tokens_out(FIRST["1out", b], tok(E, 0))
            scalar_attention(act, move, wide_out, tokens_out, project_out, deviation, link)

        @block.vector
        def _(dve):
            steps = [0]

            def link(ins):
                steps[0] += 1
                ins.then_inc(dve_step, 1)
                dve.wait_ge(dve_step, steps[0])

            norms = [0]

            def normalize(src, dst):
                norms[0] += 1
                for i in range(TT):
                    last = dve.bn_stats(stats[:, i, :], src[:, i, :])
                link(last)
                for i in range(TT):
                    last = dve.bn_aggr(mv[:, i, :], stats[:, i, :])
                last.then_inc(var_ready, 1)
                dve.wait_ge(std_ready, norms[0])
                link(dve.reciprocal(rstd[:, :], std[:, :]))
                for i in range(TT):
                    last = dve.tensor_scalar(dst[:, i, :], src[:, i, :], mv[:, i, 0:1], rstd[:, i:i + 1], ALU.subtract, ALU.mult)
                link(last)

            def condition(g, b, r_gain, r_shift, dst):
                scale, sh = g
                dve.scalar_tensor_tensor(gain[:, :], scale, 1.0, rows[:, r_gain:r_gain + D], ALU.add, ALU.mult)
                link(dve.scalar_tensor_tensor(shift[:, :], scale, 1.0, rows[:, r_shift:r_shift + D], ALU.add, ALU.mult))
                link(dve.tensor_tensor(shift[:, :], shift[:, :], sh, ALU.add))
                link(dve.tensor_tensor(dst, dst, per_column(gain[:, :]), ALU.mult))
                return dve.tensor_tensor(dst, dst, per_column(shift[:, :]), ALU.add)

            def split_rows():
                link(dve.tensor_copy(bc_hi, bc_raw))
                link(dve.tensor_tensor(bc_rest, bc_raw, bc_hi, ALU.subtract))
                link(dve.tensor_copy(bc_mid, bc_rest))
                dve.tensor_copy(bcs[0:2 * NS, :], bc_hi)
                dve.tensor_copy(bcs[2 * NS:4 * NS, :], bc_mid)
                return dve.tensor_tensor(bcs[4 * NS:6 * NS, :], bc_rest, bc_mid, ALU.subtract)

            def scan_inputs(s, b, xp, dt, slot):
                dve.wait_ge(evac, FIRST[xp, b] + 2)
                split_rows().then_inc(bc_ready, 1)
                v, tmp, src = chan(A), chan(E), chan(slot)
                for e in range(KE):
                    dve.wait_ge(evac, FIRST[dt, b] + 2 * e + 2)
                    dve.scalar_tensor_tensor(tmp[:, e, :], v[:, e, :], -1.0, v[:, e, :], ALU.mult, ALU.min).then_inc(abs_ready, 1)
                for step in range(KE + 1):
                    if step < KE:
                        e = step
                        dve.wait_ge(log_ready, s * KE + e + 1)
                        dve.scalar_tensor_tensor(v[:, e, :], v[:, e, :], 0.0, tmp[:, e, :], ALU.max, ALU.add).then_inc(dt_ready, 1)
                    if step:
                        e = step - 1
                        dve.wait_ge(dt_ready, s * KE + e + 1)
                        dve.tensor_tensor(tmp[:, e, :], v[:, e, :], src[:, e, :], ALU.mult).then_inc(w_ready, 1)
                dve.wait_ge(w_ready, (s + 1) * KE)
                for c in range(CHUNKS):
                    chunk(s, c)

            def chunk(s, c):
                backward = SCANS[s][4]
                cc = s * CHUNKS + c
                at = (CHUNKS - 1 - c if backward else c) * TC
                w = chan(E)
                way = slice(None, None, -1) if backward else slice(None)

                def load(n, k, p, c=c):
                    cc = s * CHUNKS + c
                    at = (CHUNKS - 1 - c if backward else c) * TC
                    dve.wait_ge(bcast, n + (cc * NS + 1))
                    if cc or not isinstance(n, int) or n >= 2:
                        dve.wait_ge(summed, n * KE + ((cc * NS - 2) * KE + 2 * p + 2))
                    dve.tensor_tensor(hbuf[:, k, 2 * p:2 * p + 2, :], w[:, 2 * p:2 * p + 2, at:at + TC],
                                      psum[:, 4, :].rearrange("p (o t) -> p o t", o=1).to_broadcast([P, 2, TC]),
                                      ALU.mult).then_inc(dbu, 1)

                def scan(n, k, p):
                    dve.wait_ge(dbu, n * PAIRS + (cc * NS * PAIRS + p + 1))
                    for e in (2 * p, 2 * p + 1):
                        dve.wait_ge(decay, n * KE + (cc * NS * KE + e + 1))
                        h = hbuf[:, k, e, way]
                        if c == 0:
                            start = 0.0
                        else:
                            start = hlast[:, e, n:n + 1] if isinstance(n, int) else hlast[:, e, bass.ds(n, 1)]
                        dve.tensor_tensor_scan(h, psum[:, 6 + e % 2, way], h, start, ALU.mult, ALU.add).then_inc(scanned, 1)

                def state(n, k):
                    load(n, k, 1)
                    scan(n, k, 0)
                    load(n + 1, 1 - k, 0)
                    scan(n, k, 1)

                if c == 0:
                    load(0, 0, 0)
                else:
                    dve.wait_ge(saved, (s * (CHUNKS - 1) + c) * NS * PAIRS)
                for k in range(2):
                    state(k, k)
                with dve.Fori(1, NS // 2 - 1) as i:
                    for k in range(2):
                        state(i * 2 + k, k)
                state(NS - 2, 0)
                load(NS - 1, 1, 1)
                scan(NS - 1, 1, 0)
                if c < CHUNKS - 1:
                    load(0, 0, 0, c + 1)
                scan(NS - 1, 1, 1)

            dve.wait_ge(cols_ready, 2)
            for at, n in ((C_A, KE * NS), (C_A1, 2 * KE * NS)):
                dve.tensor_scalar(cols[:, at:at + n], cols[:, at:at + n], -1.0, None, ALU.mult)
            dve.wait_ge(consts_ready, 1)
            for which in range(3):
                for e in range(KE):
                    col = (C_D if which == 0 else C_D1 + (which - 1) * KE) + e
                    last = dve.tensor_scalar(diag_d[:, which, e, :], ident[:, :], cols[:, col:col + 1], None, ALU.mult)
            last.then_inc(a_ready, 1)

            def conditioning_bias(n):
                dve.wait_ge(evac, FIRST["ada", n] + len(ADA_PIECES[n]))
                dve.tensor_tensor(adas[n], adas[n], adab[n], ALU.add).then_inc(ada_ready, 1)

            conditioning_bias(0)
            for b in range(BATCH):
                xb = xt[:, b * TT:(b + 1) * TT, :]
                xn = tok(E, 0)
                dve.wait_ge(ld_x[b], 16)
                normalize(xb, xn)
                if b == 0:
                    dve.wait_ge(ld_rows, 16)
                    dve.wait_ge(ld_adarows, 32)
                condition((ada[:, b, D:2 * D], ada[:, b, 0:D]), b, R_G0, R_B0, xn).then_inc(xn_ready, 1)
                xi, u = chan(A), chan(C)
                for e in range(KE):
                    dve.wait_ge(evac, FIRST["0in", b] + 2 * e + 2)
                    for tap in range(CONV):
                        wcol = cols[:, C_CONVW + e * CONV + CONV - 1 - tap:C_CONVW + e * CONV + CONV - tap]
                        if tap == 0:
                            last = dve.tensor_scalar(u[:, e, :], xi[:, e, :], wcol, None, ALU.mult)
                        else:
                            last = dve.scalar_tensor_tensor(u[:, e, tap:SEQ], xi[:, e, 0:SEQ - tap], wcol, u[:, e, tap:SEQ],
                                                            ALU.mult, ALU.add)
                        if tap < CONV - 1:
                            link(last)
                    last.then_inc(conv_ready, 1)
                scan_inputs(b, b, "0xp", "0dt", C)
                for e in range(KE):
                    dve.wait_ge(y_out, ((b + 1) * CHUNKS - 1) * KE + e + 1)
                    dve.tensor_tensor(chan(C)[:, e, :], chan(C)[:, e, :], chan(B)[:, e, :], ALU.mult).then_inc(gated, 1)
                dve.wait_ge(evac, FIRST["0out", b] + 4)
                ssm = tok(E, 0)
                link(dve.tensor_tensor(ssm, ssm, per_column(ada[:, b, 2 * D:3 * D]), ALU.mult))
                ins = dve.tensor_tensor(xb, xb, ssm, ALU.add)
                ins.then_inc(x_updated, 1)
                dve.wait_ge(x_updated, b + 1)
                if b == 0:
                    conditioning_bias(1)
            if LAYERS < 2:
                return
            dve.wait_ge(x_updated, BATCH)
            dve.sem_inc(rows_used, 1)
            for b in range(BATCH):
                xb = xt[:, b * TT:(b + 1) * TT, :]
                x1, xn = tok(C, 0), tok(E, 0)
                normalize(xb, x1)
                if b == 0:
                    dve.wait_ge(ld_adarows, 64)
                link(condition((ada[:, b, D:2 * D], ada[:, b, 0:D]), b, R_G1, R_B1, x1))
                normalize(x1, xn)
                link(dve.tensor_tensor(xn, xn, per_column(rows[:, R_G2:R_G2 + D]), ALU.mult))
                dve.tensor_tensor(xn, xn, per_column(rows[:, R_B2:R_B2 + D]), ALU.add).then_inc(xn_ready, 1)
                gate = per_column(ada[:, b, 2 * D:3 * D])
                link(dve.tensor_tensor(x1, x1, per_column(rows[:, R_BF:R_BF + D]), ALU.add))
                link(dve.tensor_tensor(x1, x1, gate, ALU.mult))
                dve.tensor_tensor(xb, xb, x1, ALU.add).then_inc(skip_added, 1)
                for d in range(2):
                    scan_inputs(2 + 2 * b + d, b, f"1xp{d}", f"1dt{d}", (C, F)[d])
                for step in range(KE + 1):
                    if step < KE:
                        dve.wait_ge(y_out, ((4 + 2 * b) * CHUNKS - 1) * KE + step + 1)
                        dve.tensor_tensor(chan(C)[:, step, :], chan(C)[:, step, :], chan(F)[:, step, :], ALU.add).then_inc(both_added, 1)
                    if step:
                        e = step - 1
                        dve.wait_ge(both_added, b * KE + e + 1)
                        dve.tensor_tensor(chan(C)[:, e, :], chan(C)[:, e, :], chan(B)[:, e, :], ALU.mult).then_inc(gated, 1)
                dve.wait_ge(evac, FIRST["1out", b] + 4)
                ssm = tok(E, 0)
                link(dve.tensor_tensor(ssm, ssm, gate, ALU.mult))
                dve.tensor_tensor(xb, xb, ssm, ALU.add).then_inc(x_updated, 1)
                dve.wait_ge(x_updated, BATCH + b + 1)
            vector_attention(dve, link, normalize, condition, split_rows)


def pack(inputs):
    import numpy as np

    def arr(name):
        return np.asarray(inputs[name])

    def kmajor(w):
        k, m = w.shape
        return w.reshape(k // P, P, m).transpose(1, 0, 2).reshape(P, -1)

    def xproj(w):
        return kmajor(w.T)

    def chans(v):
        v = v.reshape(v.shape[0], -1)
        return v.reshape(-1, P, v.shape[1]).transpose(1, 0, 2).reshape(P, -1)

    g0 = lambda n: arr("L0_cond_" + n)
    g1 = lambda n: arr("L1_cond_" + n)
    g2 = lambda n: arr("L2_cond_" + n)
    g3 = lambda n: arr("L3_cond_" + n)
    cols = np.zeros((P, NCOLS), np.float32)

    def put(at, v):
        v = chans(v)
        cols[:, at:at + v.shape[1]] = v

    put(C_CONVW, g0("conv_w")), put(C_CONVB, g0("conv_b")), put(C_DTB, g0("dt_proj_b"))
    put(C_D, g0("D_param")), put(C_A, g0("A_log"))
    put(C_BX, g1("bx")), put(C_BZ, g1("bz"))
    for d in range(2):
        put(C_BC + d * KE, g1(f"bc{d + 1}")), put(C_BDT + d * KE, g1(f"bdt{d + 1}"))
        put(C_D1 + d * KE, g1(f"Dp{d + 1}")), put(C_A1 + d * KE * NS, g1(f"Alog{d + 1}"))
    put(C_BK2, g2("bk")), put(C_BQ3, g3("q_b")), put(C_BK3, g3("k_b"))
    rows = np.stack([
        np.concatenate([g0("ln_g"), g0("ln_b"), g1("norm1_g"), g1("norm1_b"), g1("norm2_g"), g1("norm2_b"), g1("bf")]),
        np.concatenate([g2(n) for n in ("norm_scale", "norm_bias", "film_norm_scale", "film_norm_bias", "bq", "bv", "film_out_b")]),
        np.concatenate([g3(n) for n in ("norm_w", "norm_b", "sb_norm_w", "sb_norm_b", "q_b", "v_b", "out_b")]),
    ])
    ada_w = np.concatenate([g0("ada_w").T, g1("Wada").T, g2("film_emb_W"), g3("emb_w")], 1)
    ada_b = np.concatenate([g0("ada_b"), g1("bada"), g2("film_emb_b"), g3("emb_b")])[None]
    w0 = np.concatenate([kmajor(g0("in_proj_w").T), xproj(g0("x_proj_w")), kmajor(g0("out_proj_w").T)], 1)
    w1 = np.concatenate([kmajor(g1("Wx").T), kmajor(g1("Wz").T), kmajor(g1("Wc1").T), kmajor(g1("Wc2").T),
                         xproj(g1("Wdbc1")), xproj(g1("Wdbc2")), kmajor(g1("Wf").T)], 1)
    wdt = np.stack([g0("dt_proj_w").T, g1("Wdt1").T, g1("Wdt2").T], 1)
    w23 = np.stack([np.concatenate([kmajor(w) for w in (g2("Wq"), g2("Wk"), g2("Wv"), g2("film_out_W"))], 1),
                    np.concatenate([kmajor(w) for w in (g3("q_w"), g3("k_w"), g3("v_w"), g3("out_w"))], 1)], 1)

    def by_token(m):
        return m.reshape(BATCH * TT, P).T

    m2, m3 = arr("mask_BxS_ik0"), arr("mask_BxS_ff1")
    return {
        "x": arr("x"), "cond_t": arr("cond_2048").T.reshape(KE, P, BATCH).transpose(1, 0, 2), "cols_in": cols, "rows_in": rows,
        "ada_w": ada_w.reshape(KE, P, NADA).transpose(1, 0, 2), "ada_b": ada_b, "w0": w0, "w1": w1, "wdt": wdt, "w23": w23,
        "mask2_row": m2, "mask2_col": by_token(m2), "mask3_row": m3, "mask3_col": by_token(m3),
    }


def kernel(**inputs):
    import numpy as np
    import concourse.bacc as bacc
    from concourse import mybir as mb
    from concourse.bass_utils import run_bass_kernel_spmd

    nc = bacc.Bacc("TRN2", target_bir_lowering=False, num_devices=1)
    arrays, args = {}, []
    for name, value in pack(inputs).items():
        value = np.ascontiguousarray(value)
        arrays["in_" + name] = value
        args.append(nc.dram_tensor("in_" + name, value.shape, mb.dt.from_np(value.dtype), kind="ExternalInput").ap())
    args.append(nc.dram_tensor("out_0", (BATCH, SEQ, D), mb.dt.float32, kind="ExternalOutput").ap())
    build(nc, *args)
    r = run_bass_kernel_spmd(nc, [arrays], core_ids=[0])
    return r.results[0]["out_0"]
```

```python
import concourse.bass as bass
import concourse.mybir as mybir
from concourse.alu_op_type import AluOpType as ALU
from contextlib import ExitStack

F32 = mybir.dt.float32
BF16 = mybir.dt.bfloat16
I32 = mybir.dt.int32
ACT = mybir.ActivationFunctionType
AX = mybir.AxisListType

P = 128
BATCH = 2
SEQ = 1024
D = 256
DI = 512
NS = 16
RANK = 64
CONV = 4
HEADS = 16
HD = D // HEADS
EPS = 1e-5
KD = D // P
KE = DI // P
TT = SEQ // P
TC = 512
CHUNKS = SEQ // TC
XP = RANK + 2 * NS
PAIRS = KE // 2

C_CONVW, C_CONVB, C_DTB, C_A = 0, 16, 20, 32
C_D = 24
C_BX, C_BZ, C_BC, C_BDT, C_D1, C_A1 = 96, 100, 104, 112, 120, 128
C_BK2, C_BQ3, C_BK3 = 256, 258, 260
NCOLS = 262

R_G0, R_B0, R_G1, R_B1, R_G2, R_B2, R_BF = 0, 256, 512, 768, 1024, 1280, 1536
R_NG, R_NB, R_FG, R_FB, R_BQ, R_BV, R_OB = 0, 256, 512, 768, 1024, 1280, 1536
NROWS = 1792
ADA = [768, 768, 512, 512]
ADA0 = [0, 768, 1536, 2048]
NADA = sum(ADA)
ADA_PIECES = [[(0, 384), (384, 384)], [(768, 384), (1152, 384), (1536, 512), (2048, 512)]]
NREST = NADA - ADA[0]

W0_IN, W0_XP, W0_OUT, NW0 = 0, KD * 2 * DI, KD * 2 * DI + KE * XP, KD * 2 * DI + KE * XP + KE * D
W1_X, W1_Z = 0, KD * DI
W1_C = 2 * KD * DI
W1_XP = W1_C + 2 * KE * DI
W1_F = W1_XP + 2 * KE * XP
NW1 = W1_F + KE * D
WA_Q, WA_K, WA_V, WA_O, NWA = 0, KD * D, 2 * KD * D, 3 * KD * D, 4 * KD * D

TERMS = [(0, 0), (0, 1), (1, 0), (1, 1), (0, 2), (2, 0)]
K_MAX = len(TERMS) * HD + 3
K_EXP = K_MAX + 3
MASKED = -1000000.0
QH = 4
QUADS = HEADS // QH
JOBS = BATCH * QUADS
LEAD = TT + 2
UNITS = QH * TT
LOADS = 2 * len(TERMS) + 1
TWO_ONES = 1.0019378662109375
NEVER = -1e30

STAGES = [("ada", 0, len(ADA_PIECES[0]))]
for _b in range(BATCH):
    STAGES += [("0xT", _b, 4), ("0in", _b, 16), ("0xp", _b, 2), ("0dt", _b, 8)]
    if _b == 0:
        STAGES += [("ada", 1, len(ADA_PIECES[1]))]
    else:
        STAGES += [("1xT", 0, 4), ("1z", 0, 8)]
    STAGES += [("0out", _b, 4)]
for _b in range(BATCH):
    STAGES += [("1x", _b, 8), ("1c", _b, 16)]
    for _d in range(2):
        STAGES += [(f"1xp{_d}", _b, 2), (f"1dt{_d}", _b, 8)]
    STAGES += [("1xT", _b + 1, 4), ("1z", _b + 1, 8)] if _b + 1 < BATCH else [("2xT", 0, 4), ("2q", 0, 4)]
    STAGES += [("1out", _b, 4)]
STAGES += [("2v", 0, 4), ("2kT", 0, 4)]
for _b in range(1, BATCH):
    STAGES += [("2xT", _b, 4), ("2q", _b, 4), ("2v", _b, 4), ("2kT", _b, 4)]
for _name, _count in (("2k", 4), ("2m", 1), ("2qT", 4), ("2y", 4)):
    STAGES += [(_name, _b, _count) for _b in range(BATCH)]
for _b in range(BATCH):
    STAGES += [("2hT", _b, 4), ("2out", _b, 4)]
for _b in range(BATCH):
    STAGES += [("3xT", _b, 4), ("3qT", _b, 4), ("3v", _b, 4), ("3kT", _b, 4)]
for _b in range(BATCH):
    STAGES += [("3hT", _b, 4), ("3out", _b, 4)]
FIRST = {}
_n = 0
for _name, _b, _count in STAGES:
    FIRST[_name, _b] = _n
    _n += _count


def build(nc, x, cond_t, cols_in, rows_in, ada_w, ada_b, w0, w1, wdt, w23, mask2_row, mask2_col, mask3_row, mask3_col,
          out):
    ctx = ExitStack()
    with ctx:
        def sb(name, shape, dt=F32):
            return ctx.enter_context(nc.sbuf_tensor(name, shape, dt))

        def sem(name):
            return ctx.enter_context(nc.semaphore(name))

        xt = sb("xt", [P, BATCH * TT, D])
        xn_next = sb("xn_next", [P, TT, D])
        slots = sb("slots", [P, 5, KE * SEQ])
        wl1 = sb("wl1", [P, max(NW1, 4 * TT * D)])
        wdts = sb("wdts", [RANK, 3, DI])
        wl23 = sb("wl23", [P, 2, NWA])
        rows = sb("rows", [P, NROWS])
        ada = sb("ada", [P, BATCH, 768])
        cols = sb("cols", [P, NCOLS])
        hbuf = sb("hbuf", [P, 2, KE, TC])
        cbuf = sb("cbuf", [P, 2, TC])
        hlast = sb("hlast", [P, KE, NS])
        bcs = sb("bcs", [3 * 2 * NS, SEQ], BF16)
        ident = sb("ident", [P, P])
        pick = sb("pick", [3 * 2 * NS, 2 * NS], BF16)
        heads = sb("heads", [P, P])
        diag_d = sb("diag_d", [P, 3, KE, P])
        stats = sb("stats", [P, TT, 6])
        mv = sb("mv", [P, TT, 2])
        std = sb("std", [P, TT])
        rstd = sb("rstd", [P, TT])
        gain = sb("gain", [P, D])
        shift = sb("shift", [P, D])
        sct = sb("sct", [P, KE, BATCH])
        eps = sb("eps", [P, 1])
        warm = sb("warm", [P, 64])
        keep2 = sb("keep2", [P, BATCH * TT])
        m2c = sb("m2c", [P, BATCH * TT], I32)
        m3c = sb("m3c", [P, BATCH * TT])
        small = sb("small", [P, 6 * KD])
        head_scale = sb("head_scale", [P, 32])
        psum = ctx.enter_context(nc.psum_tensor("psum", [P, 8, 512], F32))

        scr_ada = nc.dram_tensor("scr_ada", [BATCH, NADA], F32)
        scr_qk = nc.dram_tensor("scr_qk", [BATCH, 2, 3, D, SEQ], BF16)
        scr_mask = nc.dram_tensor("scr_mask", [BATCH, 3, SEQ], BF16)
        scr_max = nc.dram_tensor("scr_max", [JOBS, 3, UNITS, P], BF16)

        A, B, C, E, F = range(5)

        def chan(s):
            return slots[:, s, :].rearrange("p (e t) -> p e t", e=KE)

        def tok(s, half):
            return slots[:, s, half * TT * D:(half + 1) * TT * D].rearrange("p (i d) -> p i d", i=TT)

        def wide(s, half):
            return slots[:, s, half * KD * SEQ:(half + 1) * KD * SEQ].rearrange("p (k t) -> p k t", k=KD)

        def per_token(v):
            return v.rearrange("p (i o) -> p i o", o=1).to_broadcast([P, TT, D])

        def per_column(v):
            return v.rearrange("p (o d) -> p o d", o=1).to_broadcast([P, TT, D])

        w0s = slots[:, F, :]
        adaw = [slots[:, A, 0:KE * ADA[0]].rearrange("p (k n) -> p k n", k=KE),
                wl1[:, 0:KE * NREST].rearrange("p (k n) -> p k n", k=KE)]
        hflat = hbuf[:, :, :, :].rearrange("p a e t -> p (a e t)")
        adas = [hflat[0:BATCH, 0:ADA[0]], wl23[0:BATCH, 0, 0:NREST]]
        adab = [slots[0:BATCH, E, 0:ADA[0]], wl23[0:BATCH, 1, 0:NREST]]
        x1 = wl23[:, 0, :].rearrange("p (i d) -> p i d", i=TT)
        ada1 = wl23[:, 1, 0:BATCH * ADA[1]].rearrange("p (b n) -> p b n", b=BATCH)
        xp_out = hflat[0:XP, 0:SEQ]
        xp_late = ada[:, :, :].rearrange("p b n -> p (b n)")[0:XP, 0:SEQ]
        dt_low, bc_raw, bc_rest = xp_out[0:RANK, :], xp_out[RANK:XP, :], hflat[RANK:XP, SEQ:2 * SEQ]
        bc_hi = hflat[RANK:XP, 2 * SEQ:2 * SEQ + SEQ // 2].bitcast(BF16)
        bc_mid = hflat[RANK:XP, 2 * SEQ + SEQ // 2:3 * SEQ].bitcast(BF16)
        SCANS = [("0", 0, 0, C, False), ("0", 1, 0, C, False)]
        for b in range(BATCH):
            SCANS += [("1", b, 1, C, False), ("1", b, 2, F, True)]

        ld_x, ld_ada = ([sem(f"{n}{i}") for i in range(2)] for n in ("ld_x", "ld_ada"))
        ld_small, ld_masks, ld_w0, ld_w1, ld_w23 = (sem(n) for n in ("ld_small", "ld_masks", "ld_w0", "ld_w1", "ld_w23"))
        x1_normalized, x1_conditioned, xn_normalized = sem("x1_normalized"), sem("x1_conditioned"), sem("xn_normalized")
        ld_rows, ld_adarows = sem("ld_rows"), sem("ld_adarows")
        made, consts_ready = sem("made"), sem("consts_ready")
        prod, evac = sem("prod"), sem("evac")
        dve_step, act_step, pool_step = sem("dve_step"), sem("act_step"), sem("pool_step")
        sct_ready, ada_ready, ada_stored = sem("sct_ready"), sem("ada_ready"), sem("ada_stored")
        cols_ready = sem("cols_ready")
        a_ready = sem("a_ready")
        var_ready, std_ready, xn_ready = sem("var_ready"), sem("std_ready"), sem("xn_ready")
        conv_ready, u_ready = sem("conv_ready"), sem("u_ready")
        bc_ready = sem("bc_ready")
        abs_ready, exp_ready, log_ready, dt_ready, w_ready, w_late = (sem(n) for n in (
            "abs_ready", "exp_ready", "log_ready", "dt_ready", "w_ready", "w_late"))
        bcast, c_out = sem("bcast"), sem("c_out")
        dbu, decay = sem("dbu"), sem("decay")
        scanned, weighed, summed = sem("scanned"), sem("weighed"), sem("summed")
        saved = sem("saved")
        y_out = sem("y_out")
        both_added, gated, x_updated = sem("both_added"), sem("gated"), sem("x_updated")
        rows_used = sem("rows_used")
        stored = sem("stored")
        ld_mask2, q_shifted, q_exp, qn_ready = sem("ld_mask2"), sem("q_shifted"), sem("q_exp"), sem("qn_ready")
        v_ready, k_masked, k_exp, kn_ready = sem("v_ready"), sem("k_masked"), sem("k_exp"), sem("kn_ready")
        outer_ready, h_conditioned, h_ready = sem("outer_ready"), sem("h_conditioned"), sem("h_ready")
        ld_mask3, mask_split, mask_stored = sem("ld_mask3"), sem("mask_split"), sem("mask_stored")
        qk_split, parts_stored, ones_set = sem("qk_split"), sem("parts_stored"), sem("ones_set")
        ld_stack = [sem(f"ld_stack{n}") for n in range(QUADS)]
        ld_max = [sem(f"ld_max{n}") for n in range(QUADS)]
        scored, maxed = sem("scored"), sem("maxed")
        max_found, max_turned, max_read = sem("max_found"), sem("max_turned"), sem("max_read")
        max_split, max_stored = sem("max_split"), sem("max_stored")
        v3_ready, quads_clear, v_quad_ready = sem("v3_ready"), sem("quads_clear"), sem("v_quad_ready")
        shifted, exped, weighed_v = sem("shifted"), sem("exped"), sem("weighed_v")
        o_out, o_turned, inverted, normalized = sem("o_out"), sem("o_turned"), sem("inverted"), sem("normalized")

        class Layer2:
            def __init__(self, areas, scalars, head_scalars):
                as_tok = lambda a: a.rearrange("p (i d) -> p i d", i=TT)
                as_wide = lambda a: a.rearrange("p (k t) -> p k t", k=KD)
                self.xn, self.xT = as_tok(areas[0]), as_wide(areas[1])
                self.k, self.o, self.qT = as_tok(areas[0]), as_tok(areas[0]), as_wide(areas[1])
                self.q_flat, self.q, self.y, self.v = areas[2], as_tok(areas[2]), as_tok(areas[2]), as_tok(areas[3])
                self.kT, self.hT = as_wide(areas[4]), as_wide(areas[4])
                self.outer = areas[5][:, 0:KD * P].rearrange("p (k e) -> p k e", k=KD)
                self.never = areas[5][:, KD * P:KD * P + SEQ]
                self.mask = self.never.bitcast(I32)
                self.head_max, self.head_inv = (head_scalars[:, n * TT * HEADS:(n + 1) * TT * HEADS] for n in range(2))
                self.k_neg_max, self.k_den, self.k_inv = (scalars[:, n * KD:(n + 1) * KD] for n in range(3))

        half_slot = TT * D
        halves = ((A, 0), (A, 1), (E, 1), (B, 0), (B, 1), (C, 1))
        L2 = [Layer2([slots[:, n, h * half_slot:(h + 1) * half_slot] for n, h in halves], small[:, 0:3 * KD], gain[:, :]),
              Layer2([wl1[:, n * half_slot:(n + 1) * half_slot] for n in range(4)] +
                     [hflat[:, n * half_slot:(n + 1) * half_slot] for n in range(2)], small[:, 3 * KD:6 * KD],
                     hflat[:, 2 * half_slot - 2 * TT * HEADS:2 * half_slot])]

        def part(flat, dims, **kw):
            return flat.rearrange(dims, **kw)

        x3 = [part(wl1[:, 0:2048], "p (i d) -> p i d", i=TT), xn_next[:, :, :]]
        x3T = [part(a, "p (k t) -> p k t", k=KD) for a in (wl1[:, 2048:4096], slots[:, E, 0:2048])]
        q3T = [part(a, "p (k t) -> p k t", k=KD) for a in (wl1[:, 4096:6144], slots[:, E, 2048:4096])]
        k3T = part(wl1[:, 6144:8192], "p (k t) -> p k t", k=KD)
        v3 = [part(hflat[:, b * 2048:(b + 1) * 2048], "p (i d) -> p i d", i=TT) for b in range(BATCH)]
        rest3 = wl1[:, 0:2048]
        q_parts = [slots[:, F, n * 1024:n * 1024 + 1024].bitcast(BF16) for n in range(3)]
        k_parts = [slots[:, F, 3072:4096].bitcast(BF16), wl1[:, 2048:3072].bitcast(BF16), wl1[:, 3072:4096].bitcast(BF16)]
        stacks = [slots[:, n, :].bitcast(BF16).rearrange("p (s h t) -> p s h t", s=2, h=QH) for n in range(QUADS)]
        y3 = [part(wl1[:, b * 2048:(b + 1) * 2048], "p (i d) -> p i d", i=TT) for b in range(BATCH)]
        h3T = [part(wl1[:, a:a + 2048], "p (k t) -> p k t", k=KD) for a in (4096, 6144)]
        v_quad = [part(wl1[:, a:a + 1024], "p (i h c) -> p i h c", i=TT, h=QH) for a in (4096, 5120)]
        oT = wl1[:, 6144:7168]
        o3 = [tok(F, b) for b in range(BATCH)]
        probs = slots[:, F, :].rearrange("p (n t) -> p n t", n=4)
        half_max = gain[:, 0:2 * UNITS].rearrange("p (a u) -> p a u", a=2)
        row_max, neg_max = gain[:, 2 * UNITS:3 * UNITS], gain[0:UNITS, P:2 * P]
        max_rest = shift[0:UNITS, 0:P]
        max_parts = [shift[0:UNITS, P:P + 64].bitcast(BF16), shift[0:UNITS, P + 64:2 * P].bitcast(BF16),
                     heads[0:UNITS, 0:64].bitcast(BF16)]
        inv3 = head_scale[:, :].rearrange("p (i h) -> p i h", i=TT)

        def sync_layer2(sp):
            for b in range(BATCH):
                sp.dma_start(L2[b].mask, mask2_row[b:b + 1, :].to_broadcast([P, SEQ])).then_inc(ld_mask2, 16)

        def sync_mask3(sp):
            for b in range(BATCH):
                if b:
                    sp.wait_ge(mask_split, b)
                sp.dma_start(bc_raw, mask3_row[b:b + 1, :].to_broadcast([XP - RANK, SEQ])).then_inc(ld_mask3, 16)
                sp.wait_ge(mask_split, b + 1)
                for n in range(3):
                    sp.dma_start(scr_mask[b, n:n + 1, :], bcs[2 * NS * n:2 * NS * n + 1, :]).then_inc(mask_stored, 16)
                sp.wait_ge(mask_stored, 48 * (b + 1))

        def sync_layer3(sp):
            def store_parts(b):
                for side, parts in enumerate((q_parts, k_parts)):
                    sp.wait_ge(qk_split, 2 * b + side + 1)
                    for n in range(3):
                        sp.dma_start(scr_qk[b, side, n].rearrange("(k p) t -> p k t", p=P),
                                     parts[n].rearrange("p (k t) -> p k t", k=KD)).then_inc(parts_stored, 16)
                sp.wait_ge(parts_stored, 96 * (b + 1))

            def load_stack(job):
                b, quad = job // QUADS, job % QUADS
                for r, pair in enumerate(TERMS):
                    for side in range(2):
                        src = scr_qk[b, side, pair[side]].rearrange("(g h d) t -> g d h t", g=QUADS, d=HD)[quad]
                        sp.dma_start(stacks[quad][r * HD:(r + 1) * HD, side], src).then_inc(ld_stack[quad], 16)
                mask_src = scr_mask[b].rearrange("r (o t) -> r o t", o=1).to_broadcast([3, QH, SEQ])
                sp.dma_start(stacks[quad][K_MAX - 3:K_MAX, 1], mask_src).then_inc(ld_stack[quad], 16)

            def load_max(job):
                sp.wait_ge(max_split, job + 1)
                for n in range(3):
                    sp.dma_start(scr_max[job, n], max_parts[n]).then_inc(max_stored, 16)
                sp.wait_ge(max_stored, 48 * (job + 1))
                quad = job % QUADS
                sp.dma_start(stacks[quad][K_MAX:K_EXP, 0], scr_max[job].rearrange("r (h i) n -> r h (i n)", i=TT)).then_inc(ld_max[quad], 16)

            store_parts(0)
            sp.wait_ge(ones_set, 1)
            for job in range(QUADS - 1):
                load_stack(job)
            store_parts(1)
            sp.wait_ge(ones_set, 2)
            load_stack(QUADS - 1)
            load_max(0)
            for job in range(JOBS):
                if job + 1 < JOBS:
                    load_max(job + 1)
                if job + QUADS < JOBS:
                    sp.wait_ge(shifted, (job + 1) * UNITS)
                    load_stack(job + QUADS)

        def pool_chunk(pool, s, c):
            cc = s * CHUNKS + c

            def state(n, k):
                pool.wait_ge(c_out, cc * NS + n + 1)
                for p in range(PAIRS):
                    if c < CHUNKS - 1:
                        pool.wait_ge(saved, s * (CHUNKS - 1) * NS * PAIRS + n * PAIRS + p + 1)
                    else:
                        pool.wait_ge(scanned, cc * NS * KE + n * KE + 2 * p + 2)
                    h = hbuf[:, k, 2 * p:2 * p + 2, :]
                    pool.tensor_tensor(h, h, cbuf[:, k:k + 1, :].to_broadcast([P, 2, TC]), ALU.mult).then_inc(weighed, 1)

            with pool.Fori(0, NS // 2) as i:
                for k in range(2):
                    state(i * 2 + k, k)

        def pool_norms(pool, b):
            pool.wait_ge(x1_normalized, b + 1)
            pool.tensor_tensor(x1, x1, per_column(gain[:, :]), ALU.mult).then_inc(pool_step, 1)
            pool.wait_ge(pool_step, 2 * b + 1)
            pool.tensor_tensor(x1, x1, per_column(shift[:, :]), ALU.add).then_inc(x1_conditioned, 1)
            pool.wait_ge(xn_normalized, b + 1)
            pool.tensor_tensor(xn_next[:, :, :], xn_next[:, :, :], per_column(rows[:, R_G2:R_G2 + D]), ALU.mult).then_inc(pool_step, 1)
            pool.wait_ge(pool_step, 2 * b + 2)
            pool.tensor_tensor(xn_next[:, :, :], xn_next[:, :, :], per_column(rows[:, R_B2:R_B2 + D]), ALU.add).then_inc(xn_ready, 1)

        def pool_attention(pool):
            pool.wait_ge(x_updated, 3 * BATCH)
            pool.memset(slots[96:K_EXP, A:E, :], TWO_ONES).then_inc(ones_set, 1)
            pool.wait_ge(ones_set, 1)
            pool.wait_ge(qk_split, 2 * BATCH)
            pool.memset(slots[96:K_EXP, E:E + 1, :], TWO_ONES).then_inc(ones_set, 1)
            pool.wait_ge(ones_set, 2)
            for n in range(2):
                ins = pool.memset(v_quad[n], 0.0)
            ins.then_inc(quads_clear, 1)
            pool.wait_ge(quads_clear, 1)
            for n in range(2):
                ins = pool.memset(v_quad[n][:, :, :, HD:HD + 1], 1.0)
            ins.then_inc(quads_clear, 1)
            for job in range(JOBS):
                b, quad = job // QUADS, job % QUADS
                pool.wait_ge(v3_ready, b + 1)
                if job == 0:
                    pool.wait_ge(quads_clear, 2)
                if job >= 2:
                    pool.wait_ge(weighed_v, (job - 1) * UNITS + 4)
                pool.tensor_copy(v_quad[job % 2][:, :, :, 0:HD],
                                 v3[b].rearrange("p i (g h d) -> p i g h d", g=QUADS, d=HD)[:, :, quad]).then_inc(v_quad_ready, 1)

        def tensor_attention(pe, bank, to_wide, project, to_tokens):
            w2, w3 = (wl23[:, n, :].rearrange("p (w k m) -> p w k m", w=4, k=KD) for n in range(2))
            for b in range(BATCH):
                if b:
                    pe.wait_ge(xn_ready, 2 * BATCH + b + 1)
                    to_wide(FIRST["2xT", b], L2[b].xn)
                    pe.wait_ge(evac, FIRST["2xT", b] + 4)
                    to_tokens(FIRST["2q", b], L2[b].xT, w2[:, 0], KD)
                to_tokens(FIRST["2v", b], L2[b].xT, w2[:, 2], KD)
                project(FIRST["2kT", b], w2[:, 1], L2[b].xT, KD, KD)
            for b in range(BATCH):
                pe.wait_ge(kn_ready, b + 1)
                g = FIRST["2k", b]
                for pair in range(TT // 2):
                    ps = bank(g)
                    for q in range(2):
                        t0 = (pair * 2 + q) * P
                        for k in range(KD):
                            last = pe.transpose(ps[:, q * D + k * P:q * D + (k + 1) * P], L2[b].kT[:, k, t0:t0 + P], ident[:, :])
                    last.then_inc(prod, 1)
                    g += 1
            for b in range(BATCH):
                pe.wait_ge(evac, FIRST["2k", b] + 4)
                pe.wait_ge(v_ready, b + 1)
                ps = bank(FIRST["2m", b])
                for k in range(KD):
                    for i in range(TT):
                        last = pe.matmul(ps[:, k * P:(k + 1) * P], L2[b].v[:, i, k * P:(k + 1) * P],
                                         L2[b].k[:, i, k * P:(k + 1) * P], start=i == 0, stop=i == TT - 1)
                last.then_inc(prod, 1)
            for b in range(BATCH):
                pe.wait_ge(qn_ready, b + 1)
                to_wide(FIRST["2qT", b], L2[b].q)
            for b in range(BATCH):
                pe.wait_ge(evac, FIRST["2qT", b] + 4)
                pe.wait_ge(outer_ready, b + 1)
                g = FIRST["2y", b]
                for pair in range(TT // 2):
                    ps = bank(g)
                    for q in range(2):
                        t0 = (pair * 2 + q) * P
                        for k in range(KD):
                            last = pe.matmul(ps[:, q * D + k * P:q * D + (k + 1) * P], L2[b].qT[:, k, t0:t0 + P],
                                             L2[b].outer[:, k, :], start=True, stop=True)
                    last.then_inc(prod, 1)
                    g += 1
            film_products(pe, "2", 0, [m.y for m in L2], [m.hT for m in L2], w2[:, 3], to_wide, to_tokens)
            pe.wait_ge(ld_w23, 32)
            pe.sem_inc(weighed_v, 4)
            for b in range(BATCH):
                pe.wait_ge(xn_ready, 3 * BATCH + b + 1)
                to_wide(FIRST["3xT", b], x3[b])
                pe.wait_ge(evac, FIRST["3qT", b])
                project(FIRST["3qT", b], w3[:, 0], x3T[b], KD, KD)
                to_tokens(FIRST["3v", b], x3T[b], w3[:, 2], KD)
                project(FIRST["3kT", b], w3[:, 1], x3T[b], KD, KD)
            pe.wait_ge(evac, FIRST["3hT", 0])

            def max_tile(job, i, n, banks):
                st, h, half = stacks[job % QUADS], n // 2, n % 2
                lhs = st[0:K_MAX, 0, h, bass.ds(i * P, P)] if not isinstance(i, int) else st[0:K_MAX, 0, h, i * P:(i + 1) * P]
                pe.wait_ge(maxed, i * (2 * QH) + (job * 2 * UNITS + n + 5 - banks))
                pe.matmul(psum[:, 8 - banks + n % banks, :], lhs, st[0:K_MAX, 1, h, half * 512:half * 512 + 512],
                          start=True, stop=True).then_inc(scored, 1)

            def start_max(job):
                pe.wait_ge(ld_stack[job % QUADS], 16 * LOADS * (job // QUADS + 1))
                if job:
                    pe.wait_ge(max_read, job)

            def turn_max(job):
                pe.wait_ge(max_found, job + 1)
                pe.transpose(psum[0:UNITS, 6, 0:P], row_max, ident[:, :]).then_inc(max_turned, 1)

            def scores(job, i, h):
                st = stacks[job % QUADS]
                lhs = st[0:K_EXP, 1, h, bass.ds(i * P, P)] if not isinstance(i, int) else st[0:K_EXP, 1, h, i * P:(i + 1) * P]
                pe.wait_ge(exped, i * QH + (job * UNITS + h + 1))
                for half in range(2):
                    last = pe.matmul(psum[:, 2 + h % 2 * 2 + half, :], lhs, st[0:K_EXP, 0, h, half * 512:half * 512 + 512],
                                     start=True, stop=True)
                last.then_inc(shifted, 1)

            def first_scores(job):
                pe.wait_ge(ld_max[job % QUADS], 16 * (job // QUADS + 1))
                scores(job, 0, 0)
                scores(job, 0, 1)

            def weigh(job, i, h, half):
                if half == 0:
                    if i == 0 and h == 0:
                        pe.wait_ge(v_quad_ready, job + 1)
                        pe.wait_ge(normalized, job + 1)
                    pe.wait_ge(exped, job * UNITS + i * QH + h + 3)
                ins = pe.matmul(psum[h * 32:h * 32 + 32, half, :], v_quad[job % 2][:, i, h, :],
                                probs[:, h, half * 512:half * 512 + 512], start=i == 0, stop=i == TT - 1)
                if half:
                    ins.then_inc(weighed_v, 1)

            def max_tiles(job, tiles):
                start_max(job)
                with pe.Fori(0, tiles) as i:
                    for n in range(2 * QH):
                        max_tile(job, i, n, 4)

            max_tiles(0, TT)
            turn_max(0)
            max_tiles(1, LEAD - TT)
            pe.wait_ge(maxed, LEAD * 2 * QH + 4)
            first_scores(0)
            for job in range(JOBS):
                for i in range(TT):
                    max_job, max_i = divmod(job * TT + i + LEAD, TT)
                    ahead, turn = max_job < JOBS, max_i == 0 and max_job <= JOBS
                    half_tiles = iter(range(2 * QH))

                    def find(count):
                        if ahead:
                            for _ in range(count):
                                max_tile(max_job, max_i, next(half_tiles), 2)

                    for h in range(QH):
                        later = i + (h + 2) // QH
                        if not (turn and h == 0):
                            find(1)
                        if later < TT:
                            scores(job, later, (h + 2) % QH)
                        if turn and h == 0:
                            turn_max(max_job - 1)
                            weigh(job, i, 0, 0)
                            if ahead:
                                start_max(max_job)
                                find(2)
                            continue
                        find(1)
                        if h == 0:
                            weigh(job, i, 0, 0)
                        else:
                            if h == 1:
                                weigh(job, i, 0, 1)
                            weigh(job, i, h, 0)
                            weigh(job, i, h, 1)
                if job + 1 < JOBS:
                    first_scores(job + 1)
                pe.wait_ge(o_out, job + 1)
                for i in range(TT):
                    last = pe.transpose(psum[:, i // 4, i % 4 * P:(i % 4 + 1) * P], oT[:, i * P:(i + 1) * P], ident[:, :])
                last.then_inc(o_turned, 1)
            pe.wait_ge(normalized, JOBS + 1)
            film_products(pe, "3", 1, y3, h3T, w3[:, 3], to_wide, to_tokens)

        def film_products(pe, layer, n, h, hT, w, to_wide, to_tokens):
            for b in range(BATCH):
                pe.wait_ge(h_ready, n * BATCH + b + 1)
                to_wide(FIRST[layer + "hT", b], h[b])
                pe.wait_ge(evac, FIRST[layer + "hT", b] + 4)
                to_tokens(FIRST[layer + "out", b], hT[b], w, KD)

        def scalar_attention(act, move, wide_out, tokens_out, project_out, deviation, load_table):
            for b in range(BATCH):
                if b:
                    deviation()
                    wide_out(FIRST["2xT", b], L2[b].xT)
                    tokens_out(FIRST["2q", b], L2[b].q)
                tokens_out(FIRST["2v", b], L2[b].v)
                project_out(FIRST["2kT", b], L2[b].kT, KD, bias=C_BK2)
            load_table(ACT.Exp)
            for b in range(BATCH):
                act.wait_ge(q_shifted, b + 1)
                act.activation(L2[b].q_flat, L2[b].q_flat, ACT.Exp).then_inc(q_exp, 1)
                act.wait_ge(k_masked, b + 1)
                for k in range(KD):
                    ins = act.activation(L2[b].kT[:, k, :], L2[b].kT[:, k, :], ACT.Exp, bias=L2[b].k_neg_max[:, k:k + 1],
                                         accum_out=L2[b].k_den[:, k:k + 1])
                ins.then_inc(k_exp, 1)
            for b in range(BATCH):
                tokens_out(FIRST["2k", b], L2[b].k)
            for b in range(BATCH):
                g = FIRST["2m", b]
                move(g, L2[b].outer, psum[:, g % 8, 0:KD * P].rearrange("p (k e) -> p k e", k=KD))
            for b in range(BATCH):
                wide_out(FIRST["2qT", b], L2[b].qT)
            for b in range(BATCH):
                tokens_out(FIRST["2y", b], L2[b].y)
            film_moves(act, "2", 0, [m.y for m in L2], [m.hT for m in L2], [m.o for m in L2], wide_out, tokens_out, deviation, load_table)
            act.sem_inc(exped, 2)
            def split_out(g, dst, hi, bias):
                hi = part(hi, "p (k t) -> p k t", k=KD)
                for mt in range(KD):
                    for half in range(2):
                        at = half * 512
                        act.wait_ge(prod, g + 1)
                        act.activation(hi[:, mt, at:at + 512], psum[:, g % 8, :], ACT.Identity, bias=cols[:, bias + mt:bias + mt + 1])
                        move(g, dst[:, mt, at:at + 512], bias=cols[:, bias + mt:bias + mt + 1])
                        g += 1

            for b in range(BATCH):
                deviation()
            for b in range(BATCH):
                wide_out(FIRST["3xT", b], x3T[b])
                if b:
                    act.wait_ge(parts_stored, 96 * b)
                split_out(FIRST["3qT", b], q3T[b], q_parts[0], C_BQ3)
                tokens_out(FIRST["3v", b], v3[b])
                if b:
                    act.wait_ge(qk_split, 2 * b)
                split_out(FIRST["3kT", b], k3T, k_parts[0], C_BK3)
            load_table(ACT.Exp)
            act.wait_ge(parts_stored, 96 * BATCH)
            for job in range(JOBS):
                with act.Fori(0, TT) as i:
                    for h in range(QH):
                        act.wait_ge(shifted, i * QH + (job * UNITS + h + 1))
                        act.wait_ge(weighed_v, i * QH + (job * UNITS + h + 1))
                        act.activation(probs[:, h, :], psum[:, 2 + h % 2 * 2:4 + h % 2 * 2, :].rearrange("p a t -> p (a t)"),
                                       ACT.Exp).then_inc(exped, 1)
            film_moves(act, "3", 1, y3, h3T, o3, wide_out, tokens_out, deviation, load_table)

        def film_moves(act, layer, n, h, hT, o, wide_out, tokens_out, deviation, load_table):
            deviation()
            for b in range(BATCH):
                load_table(ACT.Silu)
                act.wait_ge(h_conditioned, n * BATCH + b + 1)
                act.activation(h[b], h[b], ACT.Silu).then_inc(h_ready, 1)
                wide_out(FIRST[layer + "hT", b], hT[b])
                if b + 1 < BATCH:
                    deviation()
                tokens_out(FIRST[layer + "out", b], o[b])

        def vector_attention(dve, link, normalize, condition, affine, shift_queries):
            def film(layer, n, h, o):
                for b in range(BATCH):
                    normalize(h[b], h[b])
                    condition((ada[:, b, 0:D], ada[:, b, D:2 * D]), R_FG, R_FB, h[b]).then_inc(h_conditioned, 1)
                    dve.wait_ge(h_conditioned, n * BATCH + b + 1)
                for b in range(BATCH):
                    dve.wait_ge(evac, FIRST[layer + "out", b] + 4)
                    xb = xt[:, b * TT:(b + 1) * TT, :]
                    link(dve.tensor_tensor(o[b], o[b], per_column(rows[:, R_OB:R_OB + D]), ALU.add))
                    dve.tensor_tensor(xb, xb, o[b], ALU.add).then_inc(x_updated, 1)
                dve.wait_ge(x_updated, (int(layer) + 1) * BATCH)

            dve.wait_ge(x_updated, 2 * BATCH)
            dve.sem_inc(rows_used, 1)
            dve.wait_ge(ld_masks, 32)
            dve.tensor_scalar(keep2[:, :], m2c[:, :], 1.0, None, ALU.not_equal)
            for b in range(1, BATCH):
                normalize(xt[:, b * TT:(b + 1) * TT, :], L2[b].xn)
                affine(L2[b].xn, R_NG).then_inc(xn_ready, 1)
            dve.wait_ge(ld_adarows, 96)
            dve.wait_ge(ld_mask2, 16 * BATCH)
            for b in range(BATCH):
                dve.tensor_scalar(L2[b].never, L2[b].mask, 1.0, NEVER, ALU.is_equal, ALU.mult)
            for b in range(BATCH):
                m = L2[b]
                if b:
                    shift_queries(b)
                dve.wait_ge(evac, FIRST["2v", b] + 4)
                link(dve.tensor_tensor(m.v, m.v, per_column(rows[:, R_BV:R_BV + D]), ALU.add))
                dve.tensor_tensor(m.v, m.v, per_token(keep2[:, b * TT:(b + 1) * TT]), ALU.mult).then_inc(v_ready, 1)
                dve.wait_ge(evac, FIRST["2kT", b] + 4)
                link(dve.tensor_tensor(m.kT, m.kT, m.never.rearrange("p (o t) -> p o t", o=1).to_broadcast([P, KD, SEQ]), ALU.add))
                dve.tensor_reduce(m.k_neg_max, m.kT, AX.X, ALU.max, negate=True).then_inc(k_masked, 1)
            for b in range(BATCH):
                m = L2[b]
                dve.wait_ge(k_exp, b + 1)
                link(dve.reciprocal(m.k_inv, m.k_den))
                for k in range(KD):
                    ins = dve.tensor_scalar(m.kT[:, k, :], m.kT[:, k, :], m.k_inv[:, k:k + 1], None, ALU.mult)
                ins.then_inc(kn_ready, 1)
                dve.wait_ge(q_exp, b + 1)
                link(dve.tensor_reduce(m.head_inv, by_head(m.q), AX.X, ALU.add))
                link(dve.reciprocal(m.head_inv, m.head_inv))
                dve.tensor_tensor(by_head(m.q), by_head(m.q), over_head(m.head_inv), ALU.mult).then_inc(qn_ready, 1)
            for b in range(BATCH):
                dve.wait_ge(evac, FIRST["2m", b] + 1)
                dve.tensor_tensor(L2[b].outer, L2[b].outer, heads[:, :].rearrange("p (o e) -> p o e", o=1).to_broadcast([P, KD, P]),
                                  ALU.mult).then_inc(outer_ready, 1)
            dve.wait_ge(evac, FIRST["2y", BATCH - 1] + 4)
            film("2", 0, [m.y for m in L2], [m.o for m in L2])
            dve.sem_inc(rows_used, 1)
            dve.sem_inc(maxed, 4)
            dve.sem_inc(normalized, 1)

            for b in range(BATCH):
                normalize(xt[:, b * TT:(b + 1) * TT, :], x3[b])
                if b == 0:
                    dve.wait_ge(ld_rows, 48)
                    dve.wait_ge(ld_adarows, 128)
                affine(x3[b], R_NG).then_inc(xn_ready, 1)
            for b in range(BATCH):
                for side, (src, parts) in enumerate(((q3T[b], q_parts), (k3T, k_parts))):
                    dve.wait_ge(evac, FIRST[("3qT", "3kT")[side], b] + 4)
                    if b and side == 0:
                        dve.wait_ge(parts_stored, 96 * b)
                    flat = src.rearrange("p k t -> p (k t)")
                    link(dve.tensor_tensor(rest3, flat, parts[0], ALU.subtract))
                    link(dve.tensor_copy(parts[1], rest3))
                    dve.tensor_tensor(parts[2], rest3, parts[1], ALU.subtract).then_inc(qk_split, 1)
                    dve.wait_ge(qk_split, 2 * b + side + 1)
                token_mask = m3c[:, b * TT:(b + 1) * TT].rearrange("p (i o) -> p i o", o=1).to_broadcast([P, TT, D])
                link(dve.tensor_tensor(v3[b], v3[b], per_column(rows[:, R_BV:R_BV + D]), ALU.add))
                dve.tensor_tensor(v3[b], v3[b], token_mask, ALU.mult).then_inc(v3_ready, 1)

            def max_tiles(job, start, stop, banks):
                with dve.Fori(start, stop) as i:
                    for h in range(QH):
                        for half in range(2):
                            dve.wait_ge(scored, i * (2 * QH) + (job * 2 * UNITS + 2 * h + half + 1))
                            dve.tensor_reduce(half_max[:, half, bass.ds(i + h * TT, 1)], psum[:, 8 - banks + (2 * h + half) % banks, :],
                                              AX.X, ALU.max).then_inc(maxed, 1)

            def close_max(job):
                dve.wait_ge(maxed, (job + 1) * 2 * UNITS + 4)
                if job:
                    dve.wait_ge(max_turned, job)
                dve.tensor_tensor(row_max, half_max[:, 0, :], half_max[:, 1, :], ALU.max).then_inc(max_found, 1)

            def split_max(job):
                dve.wait_ge(max_turned, job + 1)
                ins = dve.tensor_scalar(neg_max, psum[0:UNITS, 6, 0:P], -1.0, None, ALU.mult)
                ins.then_inc(max_read, 1)
                dve.wait_ge(max_read, job + 1)
                if job:
                    dve.wait_ge(max_stored, 48 * job)
                link(dve.tensor_copy(max_parts[0], neg_max))
                link(dve.tensor_tensor(max_rest, neg_max, max_parts[0], ALU.subtract))
                link(dve.tensor_copy(max_parts[1], max_rest))
                dve.tensor_tensor(max_parts[2], max_rest, max_parts[1], ALU.subtract).then_inc(max_split, 1)

            max_tiles(0, 0, TT, 4)
            close_max(0)
            split_max(0)
            max_tiles(1, 0, LEAD - TT, 4)
            for job in range(JOBS):
                b, quad = job // QUADS, job % QUADS
                if job + 1 < JOBS:
                    max_tiles(job + 1, LEAD - TT, TT, 2)
                    close_max(job + 1)
                    split_max(job + 1)
                if job + 2 < JOBS:
                    max_tiles(job + 2, 0, LEAD - TT, 2)
                dve.wait_ge(weighed_v, (job + 1) * UNITS + 4)
                dve.tensor_copy(oT, psum[:, 0:2, :].rearrange("p a t -> p (a t)")).then_inc(o_out, 1)
                dve.wait_ge(o_turned, job + 1)
                sums = psum[:, 0:2, :].rearrange("p a (i h c) -> p (a i) h c", h=QH, c=32)
                dve.reciprocal(inv3, sums[:, :, :, HD:HD + 1].rearrange("p i h o -> p i (h o)")).then_inc(inverted, 1)
                dve.wait_ge(inverted, job + 1)
                dst = y3[b].rearrange("p i (g h d) -> p i g h d", g=QUADS, d=HD)[:, :, quad]
                dve.tensor_tensor(dst, sums[:, :, :, 0:HD], inv3.rearrange("p i (h o) -> p i h o", o=1)
                                  .to_broadcast([P, TT, QH, HD]), ALU.mult).then_inc(normalized, 1)
            dve.wait_ge(normalized, JOBS + 1)
            film("3", 1, y3, o3)

        def by_head(t):
            return t.rearrange("p i (h d) -> p (i h) d", d=HD)

        def over_head(v):
            return v.rearrange("p (n o) -> p n o", o=1).to_broadcast([P, TT * HEADS, HD])

        block = ctx.enter_context(nc.Block())

        @block.sync
        def _(sp):
            parts = (slice(0, ADA[0]), slice(ADA[0], NADA))
            x_in = x.rearrange("b (i p) d -> p b i d", p=P)

            def load_x(b):
                sp.dma_start(xt[:, b * TT:(b + 1) * TT, :], x_in[:, b]).then_inc(ld_x[b], 16)

            def load_conditioning(n):
                sp.dma_start(adab[n], ada_b[:, parts[n]].to_broadcast([BATCH, parts[n].stop - parts[n].start])).then_inc(ld_ada[n], 16)
                sp.dma_start(adaw[n], ada_w[:, :, parts[n]]).then_inc(ld_ada[n], 16)

            def store_conditioning(n):
                sp.wait_ge(ada_ready, n + 1)
                sp.dma_start(scr_ada[:, parts[n]], adas[n]).then_inc(ada_stored, 16)

            sp.dma_start(sct[:, :, :], cond_t).then_inc(ld_small, 16)
            sp.dma_start(cols[:, :], cols_in).then_inc(ld_small, 16)
            load_conditioning(0)
            load_x(0)
            sp.dma_start(rows[:, :], rows_in[0:1, :].to_broadcast([P, NROWS])).then_inc(ld_rows, 16)
            sp.dma_start(w0s[:, 0:NW0], w0).then_inc(ld_w0, 16)
            sp.dma_start(wdts[:, :, :], wdt).then_inc(ld_w0, 16)
            store_conditioning(0)
            sp.wait_ge(ada_stored, 16)
            def load_rows(layer):
                sp.dma_start(rows[:, :], rows_in[layer - 1:layer, :].to_broadcast([P, NROWS])).then_inc(ld_rows, 16)

            def load_conditioning_rows(layer, dst):
                for b in range(BATCH):
                    src = scr_ada[b:b + 1, ADA0[layer]:ADA0[layer] + ADA[layer]]
                    sp.dma_start(dst[:, b, 0:ADA[layer]], src.to_broadcast([P, ADA[layer]])).then_inc(ld_adarows, 16)

            load_conditioning_rows(0, ada)
            load_x(1)
            load_conditioning(1)
            sp.dma_start(m2c[:, :], mask2_col).then_inc(ld_masks, 16)
            sp.dma_start(m3c[:, :], mask3_col).then_inc(ld_masks, 16)
            store_conditioning(1)
            sp.dma_start(wl1[:, 0:NW1], w1).then_inc(ld_w1, 16)
            sp.wait_ge(ada_stored, 32)
            load_conditioning_rows(1, ada1)
            sp.wait_ge(rows_used, 1)
            load_rows(2)
            sp.dma_start(wl23[:, 0, :], w23[:, 0, :]).then_inc(ld_w23, 16)
            sp.wait_ge(x_updated, BATCH + 1)
            sync_mask3(sp)
            sp.wait_ge(rows_used, 2)
            load_conditioning_rows(2, ada)
            sync_layer2(sp)
            sp.dma_start(wl23[:, 1, :], w23[:, 1, :]).then_inc(ld_w23, 16)
            sp.wait_ge(rows_used, 3)
            load_rows(3)
            load_conditioning_rows(3, ada)
            sync_layer3(sp)
            for b in range(BATCH):
                sp.wait_ge(x_updated, (len(ADA) - 1) * BATCH + b + 1)
                sp.dma_start(out[b].rearrange("(i p) d -> p i d", p=P), xt[:, b * TT:(b + 1) * TT, :]).then_inc(stored, 16)
            sp.wait_ge(stored, 16 * BATCH)

        @block.gpsimd
        def _(pool):
            pool.memset(ident[:, :], 0.0).then_inc(made, 1)
            pool.memset(pick[:, :], 0.0).then_inc(made, 1)
            pool.memset(heads[:, :], 1.0).then_inc(made, 1)
            pool.wait_ge(made, 3)
            pool.affine_select(out=ident[:, :], in_=ident[:, :], compare_op=ALU.not_equal, fill=1.0, base=0,
                               pattern=[[-1, P]], channel_multiplier=1).then_inc(made, 1)
            for part in range(3):
                pool.affine_select(out=pick[:, :], in_=pick[:, :], compare_op=ALU.not_equal, fill=1.0,
                                   base=-2 * NS * part, pattern=[[-1, 2 * NS]], channel_multiplier=1).then_inc(made, 1)
                pool.wait_ge(made, 5 + part)
            by_head = heads[:, :].rearrange("p (j d) -> p j d", d=HD)
            pool.affine_select(out=by_head, in_=by_head, compare_op=ALU.is_ge, fill=0.0, base=0,
                               pattern=[[-HD, P // HD], [0, HD]], channel_multiplier=1).then_inc(made, 1)
            pool.wait_ge(made, 8)
            pool.affine_select(out=by_head, in_=by_head, compare_op=ALU.is_ge, fill=0.0, base=HD - 1,
                               pattern=[[HD, P // HD], [0, HD]], channel_multiplier=-1).then_inc(made, 1)
            pool.wait_ge(made, 9)
            pool.memset(eps[:, :], EPS).then_inc(consts_ready, 1)

            for s in range(len(SCANS)):
                if s in (1, 2):
                    pool_norms(pool, s - 1)
                _, _, _, slot, _ = SCANS[s]
                for e in range(KE // 2, KE):
                    pool.wait_ge(dt_ready, s * KE + e + 1)
                    pool.tensor_tensor(chan(E)[:, e, :], chan(A)[:, e, :], chan(slot)[:, e, :], ALU.mult).then_inc(w_late, 1)
                for c in range(CHUNKS):
                    pool_chunk(pool, s, c)
            pool_attention(pool)

        @block.tensor
        def _(pe):
            def bank(g):
                if g >= 8:
                    pe.wait_ge(evac, g - 7)
                return psum[:, g % 8, :]

            def to_wide(g, src):
                for k in range(KD):
                    for half in range(2):
                        ps = bank(g)
                        for q in range(4):
                            last = pe.transpose(ps[:, q * P:(q + 1) * P], src[:, half * 4 + q, k * P:(k + 1) * P], ident[:, :])
                        last.then_inc(prod, 1)
                        g += 1

            def project(g, w, src, m_tiles, k_tiles, m=P):
                for mt in range(m_tiles):
                    for half in range(2):
                        ps = bank(g)
                        for k in range(k_tiles):
                            last = pe.matmul(ps[0:m, :], w[:, k, mt * m:(mt + 1) * m], src[:, k, half * 512:half * 512 + 512],
                                             start=k == 0, stop=k == k_tiles - 1)
                        last.then_inc(prod, 1)
                        g += 1

            def to_tokens(g, src, w, k_tiles):
                for pair in range(TT // 2):
                    ps = bank(g)
                    for q in range(2):
                        t0 = (pair * 2 + q) * P
                        for k in range(k_tiles):
                            last = pe.matmul(ps[:, q * D:(q + 1) * D], src[:, k, t0:t0 + P], w[:, k, :],
                                             start=k == 0, stop=k == k_tiles - 1)
                    last.then_inc(prod, 1)
                    g += 1

            def conditioning(n):
                pe.wait_ge(ld_ada[n], 32)
                for g, (at, size) in enumerate(ADA_PIECES[n]):
                    ps = bank(FIRST["ada", n] + g)
                    for k in range(KE):
                        a0 = at - ADA0[n]
                        last = pe.matmul(ps[0:BATCH, 0:size], sct[:, k, :], adaw[n][:, k, a0:a0 + size], start=k == 0, stop=k == KE - 1)
                    last.then_inc(prod, 1)
                return FIRST["ada", n] + len(ADA_PIECES[n])

            pe.wait_ge(sct_ready, 1)
            conditioning(0)
            pe.wait_ge(consts_ready, 1)
            pe.wait_ge(ld_w0, 32)
            w_in = w0s[:, W0_IN:W0_XP].rearrange("p (k m) -> p k m", k=KD)
            w_xp = w0s[:, W0_XP:W0_OUT].rearrange("p (k m) -> p k m", k=KE)
            w_out = w0s[:, W0_OUT:NW0].rearrange("p (k m) -> p k m", k=KE)

            def scan_inputs(s, b, xp, dt, wt, low, beside=None):
                pe.wait_ge(evac, FIRST[xp, b] + 2)
                g = FIRST[dt, b]
                for mt in range(KE):
                    for half in range(2):
                        pe.matmul(bank(g), wt[:, mt * P:(mt + 1) * P], low[:, half * 512:half * 512 + 512],
                                  start=True, stop=True).then_inc(prod, 1)
                        g += 1
                if beside:
                    g = beside()
                pe.wait_ge(evac, g)
                pe.wait_ge(bc_ready, s + 1)
                for c in range(CHUNKS):
                    chunk(s, c)
                pe.wait_ge(y_out, (s + 1) * CHUNKS * KE)

            def chunk(s, c):
                _, b, which, slot, backward = SCANS[s]
                cc = s * CHUNKS + c
                at = (CHUNKS - 1 - c if backward else c) * TC

                def spread(n, c=c):
                    cc = s * CHUNKS + c
                    at = (CHUNKS - 1 - c if backward else c) * TC
                    if cc or not isinstance(n, int) or n:
                        pe.wait_ge(dbu, n * PAIRS + cc * NS * PAIRS)
                        pe.wait_ge(c_out, cc * NS + n)
                    for half in range(2):
                        row = pick[:, half * NS + n:half * NS + n + 1] if isinstance(n, int) else \
                            pick[:, bass.ds(n + half * NS, 1)]
                        last = pe.matmul(psum[:, 4 + half, :], row.to_broadcast([96, P]), bcs[:, at:at + TC],
                                         start=True, stop=True)
                    last.then_inc(bcast, 1)

                def add_state(n, k, pair, final=False):
                    for e in (2 * pair, 2 * pair + 1):
                        if e % 2 == 0:
                            pe.wait_ge(weighed, cc * NS * PAIRS + n * PAIRS + e // 2 + 1)
                        pe.matmul(psum[:, e, :], ident[:, :], hbuf[:, k, e, :], start=False, stop=final,
                                  skip_group_check=True).then_inc(summed, 1)

                if c == 0:
                    spread(0)
                src = chan(slot)
                for e in range(KE):
                    if c:
                        pe.wait_ge(y_out, (cc - 1) * KE + e + 1)
                    pe.matmul(psum[:, e, :], diag_d[:, which, e, :], src[:, e, at:at + TC], start=True, stop=False,
                              skip_group_check=True)
                if c == 0:
                    spread(1)
                with pe.Fori(0, NS // 2 - 1) as i:
                    for k in range(2):
                        add_state(i * 2 + k, k, 0)
                        spread(i * 2 + (k + 2))
                        add_state(i * 2 + k, k, 1)
                for k in range(2):
                    add_state(NS - 2 + k, k, 0, k == 1)
                    if c < CHUNKS - 1:
                        spread(k, c + 1)
                    add_state(NS - 2 + k, k, 1, k == 1)

            wx1 = wl1[:, W1_X:W1_Z].rearrange("p (k m) -> p k m", k=KD)
            wz1 = wl1[:, W1_Z:W1_C].rearrange("p (k m) -> p k m", k=KD)
            wc1 = wl1[:, W1_C:W1_XP].rearrange("p (d k m) -> p d k m", d=2, k=KE)
            wxp1 = wl1[:, W1_XP:W1_F].rearrange("p (d k m) -> p d k m", d=2, k=KE)
            wf1 = wl1[:, W1_F:NW1].rearrange("p (k m) -> p k m", k=KE)
            w2 = wl23[:, 0, :].rearrange("p (w k m) -> p w k m", w=4, k=KD)

            def layer1_head(b):
                pe.wait_ge(xn_ready, BATCH + b + 1)
                to_wide(FIRST["1xT", b], xn_next)
                pe.wait_ge(ld_w1, 16)
                pe.wait_ge(evac, FIRST["1z", b])
                project(FIRST["1z", b], wz1, wide(E, 1), KE, KD)

            def layer2_head():
                pe.wait_ge(xn_ready, 2 * BATCH + 1)
                to_wide(FIRST["2xT", 0], xn_next)
                pe.wait_ge(ld_w23, 16)
                pe.wait_ge(evac, FIRST["2q", 0])
                to_tokens(FIRST["2q", 0], L2[0].xT, w2[:, 0], KD)

            pe.wait_ge(a_ready, 1)
            for b in range(BATCH):
                pe.wait_ge(xn_ready, b + 1)
                to_wide(FIRST["0xT", b], xn_next if b else tok(E, 0))
                pe.wait_ge(evac, FIRST["0in", b])
                project(FIRST["0in", b], w_in, wide(E, 1), 2 * KE, KD)
                pe.wait_ge(u_ready, (b + 1) * KE)
                project(FIRST["0xp", b], w_xp, chan(C), 1, KE, XP)
                scan_inputs(b, b, "0xp", "0dt", wdts[:, 0, :], dt_low, None if b else lambda: conditioning(1))
                if b == BATCH - 1:
                    layer1_head(0)
                pe.wait_ge(gated, (b + 1) * KE)
                to_tokens(FIRST["0out", b], chan(C), w_out, KE)

            for b in range(BATCH):
                project(FIRST["1x", b], wx1, wide(E, 1), KE, KD)
                pe.wait_ge(evac, FIRST["1z", b] + 8)
                for d in range(2):
                    project(FIRST["1c", b] + 8 * d, wc1[:, d], chan(A), KE, KE)
                pe.wait_ge(evac, FIRST["1xp0", b])
                project(FIRST["1xp0", b], wxp1[:, 0], chan(C), 1, KE, XP)

                def backward_projection():
                    project(FIRST["1xp1", b], wxp1[:, 1], chan(F), 1, KE, XP)
                    return FIRST["1xp1", b] + 2

                scan_inputs(2 + 2 * b, b, "1xp0", "1dt0", wdts[:, 1, :], dt_low, backward_projection)
                scan_inputs(3 + 2 * b, b, "1xp1", "1dt1", wdts[:, 2, :], xp_late[0:RANK, :])
                if b + 1 < BATCH:
                    layer1_head(b + 1)
                else:
                    layer2_head()
                pe.wait_ge(gated, (BATCH + b + 1) * KE)
                to_tokens(FIRST["1out", b], chan(C), wf1, KE)
            tensor_attention(pe, bank, to_wide, project, to_tokens)

        @block.scalar
        def _(act):
            steps = [0]

            def link(ins):
                steps[0] += 1
                ins.then_inc(act_step, 1)
                act.wait_ge(act_step, steps[0])

            def move(g, dst, src=None, func=ACT.Identity, **kw):
                act.wait_ge(prod, g + 1)
                ps = psum[:, g % 8, :] if src is None else src
                act.activation(dst, ps, func, **kw).then_inc(evac, 1)

            def wide_out(g, dst):
                for k in range(KD):
                    for half in range(2):
                        move(g, dst[:, k, half * 512:half * 512 + 512])
                        g += 1

            def tokens_out(g, dst):
                for pair in range(TT // 2):
                    move(g, dst[:, pair * 2:pair * 2 + 2, :], psum[:, g % 8, :].rearrange("p (q d) -> p q d", q=2))
                    g += 1

            def project_out(g, dst, m_tiles, func=ACT.Identity, bias=None):
                for mt in range(m_tiles):
                    for half in range(2):
                        kw = {} if bias is None else {"bias": cols[:, bias + mt:bias + mt + 1]}
                        move(g, dst[:, mt, half * 512:half * 512 + 512], func=func, **kw)
                        g += 1

            norms = [0]
            loads = [0]

            def load_table(func):
                act.activation(warm[:, loads[0]:loads[0] + 1], eps[:, :], func)
                loads[0] += 1

            def deviation():
                norms[0] += 1
                load_table(ACT.Sqrt)
                act.wait_ge(var_ready, norms[0])
                act.activation(std[:, :], mv[:, :, 1], ACT.Sqrt, bias=eps[:, 0:1]).then_inc(std_ready, 1)

            def projection_out(g, dst):
                for half in range(2):
                    move(g + half, dst[:, half * 512:half * 512 + 512], psum[0:XP, (g + half) % 8, :])

            def scan_inputs(s, b, xp, dt, c_dtb):
                if s == 4:
                    act.wait_ge(mask_split, BATCH)
                if xp != "1xp1":
                    projection_out(FIRST[xp, b], xp_out)
                tmp = chan(E)
                load_table(ACT.Exp)
                for step in range(KE + 1):
                    if step < KE:
                        project_out(FIRST[dt, b] + 2 * step, chan(A)[:, step:step + 1, :], 1, bias=c_dtb + step)
                    if step:
                        e = step - 1
                        act.wait_ge(abs_ready, s * KE + e + 1)
                        act.activation(tmp[:, e, :], tmp[:, e, :], ACT.Exp).then_inc(exp_ready, 1)
                for e in range(KE):
                    act.wait_ge(exp_ready, s * KE + e + 1)
                    act.activation(tmp[:, e, :], tmp[:, e, :], ACT.Ln, bias=1.0).then_inc(log_ready, 1)
                load_table(ACT.Exp)
                if s == 0:
                    act.wait_ge(ld_ada[1], 32)
                    conditioning_out(1)
                if xp == "1xp0":
                    projection_out(FIRST["1xp1", b], xp_late)
                act.wait_ge(dt_ready, (s + 1) * KE)
                for c in range(CHUNKS):
                    chunk(s, c)

            def chunk(s, c):
                _, b, which, slot, backward = SCANS[s]
                cc = s * CHUNKS + c
                at = (CHUNKS - 1 - c if backward else c) * TC
                end = 0 if backward else TC - 1
                dt = chan(A)
                c_a = C_A if which == 0 else C_A1 + (which - 1) * KE * NS

                def state(n, k, first):
                    act.wait_ge(bcast, cc * NS + n + 1)
                    if not first:
                        act.wait_ge(weighed, cc * NS * PAIRS + (n - 1) * PAIRS)
                    elif cc:
                        act.wait_ge(weighed, (cc - 1) * NS * PAIRS + (NS - 1 + k) * PAIRS)
                    act.activation(cbuf[:, k, :], psum[:, 5, :], ACT.Identity).then_inc(c_out, 1)
                    for e in range(KE):
                        u = cc * NS * KE + n * KE + e
                        if not (isinstance(u, int) and u < 2):
                            act.wait_ge(scanned, u - 1)
                        a = cols[:, bass.ds(n + (c_a + e * NS), 1)] if not isinstance(n, int) else \
                            cols[:, c_a + e * NS + n:c_a + e * NS + n + 1]
                        if c < CHUNKS - 1 and e == 1 and not (first and k == 0):
                            save(n + (-1), 1 - k, 1)
                        if c < CHUNKS - 1 and e == 3:
                            save(n, k, 0)
                        act.activation(psum[:, 6 + e % 2, :], dt[:, e, at:at + TC], ACT.Exp, scale=a).then_inc(decay, 1)

                def save(n, k, pair):
                    col = hlast[:, 2 * pair:2 * pair + 2, n:n + 1] if isinstance(n, int) else \
                        hlast[:, 2 * pair:2 * pair + 2, bass.ds(n, 1)]
                    act.activation(col, hbuf[:, k, 2 * pair:2 * pair + 2, end:end + 1], ACT.Identity).then_inc(saved, 1)

                def sums_out(c):
                    cc = s * CHUNKS + c
                    at = (CHUNKS - 1 - c if backward else c) * TC
                    act.wait_ge(summed, (cc + 1) * NS * KE)
                    for e in range(KE):
                        act.activation(chan(slot)[:, e, at:at + TC], psum[:, e, :], ACT.Identity).then_inc(y_out, 1)

                state(0, 0, True)
                if c:
                    sums_out(c - 1)
                state(1, 1, True)
                with act.Fori(1, NS // 2) as i:
                    for k in range(2):
                        state(i * 2 + k, k, False)
                if c < CHUNKS - 1:
                    act.wait_ge(scanned, (cc + 1) * NS * KE)
                    save(NS - 1, 1, 1)
                else:
                    sums_out(c)

            def conditioning_out(n):
                for g, (at, size) in enumerate(ADA_PIECES[n], FIRST["ada", n]):
                    move(g, adas[n][:, at - ADA0[n]:at - ADA0[n] + size], psum[0:BATCH, g % 8, 0:size])

            act.wait_ge(ld_small, 32)
            act.activation(sct[:, :, :], sct[:, :, :], ACT.Silu).then_inc(sct_ready, 1)
            act.activation(cols[:, C_A:C_A + KE * NS], cols[:, C_A:C_A + KE * NS], ACT.Exp).then_inc(cols_ready, 1)
            act.activation(cols[:, C_A1:C_A1 + 2 * KE * NS], cols[:, C_A1:C_A1 + 2 * KE * NS], ACT.Exp).then_inc(cols_ready, 1)
            conditioning_out(0)
            act.wait_ge(consts_ready, 1)
            def layer1_head_out(b):
                wide_out(FIRST["1xT", b], wide(E, 1))
                project_out(FIRST["1z", b], chan(A), KE, bias=C_BZ)

            deviation()
            for b in range(BATCH):
                wide_out(FIRST["0xT", b], wide(E, 1))
                deviation()
                project_out(FIRST["0in", b], chan(A), KE)
                load_table(ACT.Silu)
                for e in range(KE):
                    act.wait_ge(conv_ready, b * KE + e + 1)
                    act.activation(chan(C)[:, e, :], chan(C)[:, e, :], ACT.Silu,
                                   bias=cols[:, C_CONVB + e:C_CONVB + e + 1]).then_inc(u_ready, 1)
                    project_out(FIRST["0in", b] + 8 + 2 * e, chan(B)[:, e:e + 1, :], 1, ACT.Silu)
                if b == BATCH - 1:
                    deviation()
                scan_inputs(b, b, "0xp", "0dt", C_DTB)
                if b == BATCH - 1:
                    layer1_head_out(0)
                tokens_out(FIRST["0out", b], tok(E, 0))
            for b in range(BATCH):
                load_table(ACT.Silu)
                project_out(FIRST["1x", b], chan(B), KE, ACT.Silu, C_BX)
                for d in range(2):
                    if b == 0 or d == 0:
                        deviation()
                    project_out(FIRST["1c", b] + 8 * d, chan((C, F)[d]), KE, bias=C_BC + d * KE)
                for d in range(2):
                    scan_inputs(2 + 2 * b + d, b, f"1xp{d}", f"1dt{d}", C_BDT + d * KE)
                if b + 1 < BATCH:
                    layer1_head_out(b + 1)
                else:
                    wide_out(FIRST["2xT", 0], L2[0].xT)
                    tokens_out(FIRST["2q", 0], L2[0].q)
                tokens_out(FIRST["1out", b], tok(E, 0))
            scalar_attention(act, move, wide_out, tokens_out, project_out, deviation, load_table)

        @block.vector
        def _(dve):
            steps = [0]

            def link(ins):
                steps[0] += 1
                ins.then_inc(dve_step, 1)
                dve.wait_ge(dve_step, steps[0])

            norms = [0]

            def normalize(src, dst, signal=None):
                norms[0] += 1
                for i in range(TT):
                    last = dve.bn_stats(stats[:, i, :], src[:, i, :])
                link(last)
                for i in range(TT):
                    last = dve.bn_aggr(mv[:, i, :], stats[:, i, :])
                last.then_inc(var_ready, 1)
                dve.wait_ge(std_ready, norms[0])
                link(dve.reciprocal(rstd[:, :], std[:, :]))
                for i in range(TT):
                    last = dve.tensor_scalar(dst[:, i, :], src[:, i, :], mv[:, i, 0:1], rstd[:, i:i + 1], ALU.subtract, ALU.mult)
                if signal is None:
                    link(last)
                else:
                    last.then_inc(signal, 1)

            def conditioning_rows(g, r_gain, r_shift):
                scale, sh = g
                dve.scalar_tensor_tensor(gain[:, :], scale, 1.0, rows[:, r_gain:r_gain + D], ALU.add, ALU.mult)
                link(dve.scalar_tensor_tensor(shift[:, :], scale, 1.0, rows[:, r_shift:r_shift + D], ALU.add, ALU.mult))
                return dve.tensor_tensor(shift[:, :], shift[:, :], sh, ALU.add)

            def condition(g, r_gain, r_shift, dst):
                link(conditioning_rows(g, r_gain, r_shift))
                link(dve.tensor_tensor(dst, dst, per_column(gain[:, :]), ALU.mult))
                return dve.tensor_tensor(dst, dst, per_column(shift[:, :]), ALU.add)

            def split_rows(raw):
                link(dve.tensor_copy(bc_hi, raw))
                link(dve.tensor_tensor(bc_rest, raw, bc_hi, ALU.subtract))
                link(dve.tensor_copy(bc_mid, bc_rest))
                dve.tensor_copy(bcs[0:2 * NS, :], bc_hi)
                dve.tensor_copy(bcs[2 * NS:4 * NS, :], bc_mid)
                return dve.tensor_tensor(bcs[4 * NS:6 * NS, :], bc_rest, bc_mid, ALU.subtract)

            def affine(t, at):
                link(dve.tensor_tensor(t, t, per_column(rows[:, at:at + D]), ALU.mult))
                return dve.tensor_tensor(t, t, per_column(rows[:, at + D:at + 2 * D]), ALU.add)

            def shift_queries(b):
                m = L2[b]
                dve.wait_ge(evac, FIRST["2q", b] + 4)
                link(dve.tensor_tensor(m.q, m.q, per_column(rows[:, R_BQ:R_BQ + D]), ALU.add))
                link(dve.tensor_reduce(m.head_max, by_head(m.q), AX.X, ALU.max))
                dve.tensor_tensor(by_head(m.q), by_head(m.q), over_head(m.head_max), ALU.subtract).then_inc(q_shifted, 1)

            def split_mask(b):
                dve.wait_ge(ld_mask3, 16 * (b + 1))
                if b:
                    dve.wait_ge(mask_stored, 48 * b)
                link(dve.tensor_scalar(bc_raw, bc_raw, 1.0, -MASKED, ALU.subtract, ALU.mult))
                split_rows(bc_raw).then_inc(mask_split, 1)

            def scan_inputs(s, b, xp, dt, slot):
                dve.wait_ge(evac, FIRST[xp, b] + 2)
                if s:
                    dve.wait_ge(summed, s * CHUNKS * NS * KE)
                split_rows(xp_late[RANK:XP, :] if xp == "1xp1" else bc_raw).then_inc(bc_ready, 1)
                v, tmp, src = chan(A), chan(E), chan(slot)
                for e in range(KE):
                    dve.wait_ge(evac, FIRST[dt, b] + 2 * e + 2)
                    dve.scalar_tensor_tensor(tmp[:, e, :], v[:, e, :], -1.0, v[:, e, :], ALU.mult, ALU.min).then_inc(abs_ready, 1)
                for e in range(KE):
                    dve.wait_ge(log_ready, s * KE + e + 1)
                    dve.scalar_tensor_tensor(v[:, e, :], v[:, e, :], 0.0, tmp[:, e, :], ALU.max, ALU.add).then_inc(dt_ready, 1)
                for e in range(KE // 2):
                    dve.wait_ge(dt_ready, s * KE + e + 1)
                    dve.tensor_tensor(tmp[:, e, :], v[:, e, :], src[:, e, :], ALU.mult).then_inc(w_ready, 1)
                if s == 0:
                    conditioning_bias(1)
                dve.wait_ge(w_ready, (s + 1) * (KE // 2))
                for c in range(CHUNKS):
                    chunk(s, c)

            def chunk(s, c):
                backward = SCANS[s][4]
                cc = s * CHUNKS + c
                at = (CHUNKS - 1 - c if backward else c) * TC
                w = chan(E)
                way = slice(None, None, -1) if backward else slice(None)

                def load(n, k, p, c=c):
                    cc = s * CHUNKS + c
                    at = (CHUNKS - 1 - c if backward else c) * TC
                    if c == 0 and isinstance(n, int) and n == 0 and p == 1:
                        dve.wait_ge(w_late, (s + 1) * (KE // 2))
                    dve.wait_ge(bcast, n + (cc * NS + 1))
                    if cc or not isinstance(n, int) or n >= 2:
                        dve.wait_ge(summed, n * KE + ((cc * NS - 2) * KE + 2 * p + 2))
                    dve.tensor_tensor(hbuf[:, k, 2 * p:2 * p + 2, :], w[:, 2 * p:2 * p + 2, at:at + TC],
                                      psum[:, 4, :].rearrange("p (o t) -> p o t", o=1).to_broadcast([P, 2, TC]),
                                      ALU.mult).then_inc(dbu, 1)

                def scan(n, k, p):
                    dve.wait_ge(dbu, n * PAIRS + (cc * NS * PAIRS + p + 1))
                    for e in (2 * p, 2 * p + 1):
                        dve.wait_ge(decay, n * KE + (cc * NS * KE + e + 1))
                        h = hbuf[:, k, e, way]
                        if c == 0:
                            start = 0.0
                        else:
                            start = hlast[:, e, n:n + 1] if isinstance(n, int) else hlast[:, e, bass.ds(n, 1)]
                        dve.tensor_tensor_scan(h, psum[:, 6 + e % 2, way], h, start, ALU.mult, ALU.add).then_inc(scanned, 1)

                def state(n, k):
                    load(n, k, 1)
                    scan(n, k, 0)
                    load(n + 1, 1 - k, 0)
                    scan(n, k, 1)

                if c == 0:
                    load(0, 0, 0)
                else:
                    dve.wait_ge(saved, (s * (CHUNKS - 1) + c) * NS * PAIRS)
                for k in range(2):
                    state(k, k)
                with dve.Fori(1, NS // 2 - 1) as i:
                    for k in range(2):
                        state(i * 2 + k, k)
                state(NS - 2, 0)
                load(NS - 1, 1, 1)
                scan(NS - 1, 1, 0)
                if c < CHUNKS - 1:
                    load(0, 0, 0, c + 1)
                scan(NS - 1, 1, 1)

            dve.wait_ge(cols_ready, 2)
            for at, n in ((C_A, KE * NS), (C_A1, 2 * KE * NS)):
                dve.tensor_scalar(cols[:, at:at + n], cols[:, at:at + n], -1.0, None, ALU.mult)
            dve.wait_ge(consts_ready, 1)
            for which in range(3):
                for e in range(KE):
                    col = (C_D if which == 0 else C_D1 + (which - 1) * KE) + e
                    last = dve.tensor_scalar(diag_d[:, which, e, :], ident[:, :], cols[:, col:col + 1], None, ALU.mult)
            last.then_inc(a_ready, 1)

            def conditioning_bias(n):
                dve.wait_ge(evac, FIRST["ada", n] + len(ADA_PIECES[n]))
                dve.tensor_tensor(adas[n], adas[n], adab[n], ALU.add).then_inc(ada_ready, 1)

            conditioning_bias(0)
            def batch_rows(b):
                return xt[:, b * TT:(b + 1) * TT, :]

            def layer0_norm(b):
                xn = xn_next[:, :, :] if b else tok(E, 0)
                dve.wait_ge(ld_x[b], 16)
                normalize(batch_rows(b), xn)
                if b == 0:
                    dve.wait_ge(ld_rows, 16)
                    dve.wait_ge(ld_adarows, 32)
                condition((ada[:, b, D:2 * D], ada[:, b, 0:D]), R_G0, R_B0, xn).then_inc(xn_ready, 1)

            def layer1_first_norm(b):
                if b == 0:
                    dve.wait_ge(ld_adarows, 64)
                normalize(batch_rows(b), x1)
                conditioning_rows((ada1[:, b, D:2 * D], ada1[:, b, 0:D]), R_G1, R_B1).then_inc(x1_normalized, 1)

            def layer1_second_norm(b):
                dve.wait_ge(x1_conditioned, b + 1)
                dve.wait_ge(evac, (FIRST["1xT", b - 1] if b else FIRST["0xT", BATCH - 1]) + 4)
                normalize(x1, xn_next[:, :, :], xn_normalized)

            def layer1_skip(b):
                xb = batch_rows(b)
                dve.wait_ge(xn_normalized, b + 1)
                link(dve.tensor_tensor(x1, x1, per_column(rows[:, R_BF:R_BF + D]), ALU.add))
                link(dve.tensor_tensor(x1, x1, per_column(ada1[:, b, 2 * D:3 * D]), ALU.mult))
                link(dve.tensor_tensor(xb, xb, x1, ALU.add))

            for b in range(BATCH):
                layer0_norm(b)
            for b in range(BATCH):
                xb = batch_rows(b)
                if b == BATCH - 1:
                    layer1_first_norm(0)
                xi, u = chan(A), chan(C)
                for e in range(KE):
                    dve.wait_ge(evac, FIRST["0in", b] + 2 * e + 2)
                    for tap in range(CONV):
                        wcol = cols[:, C_CONVW + e * CONV + CONV - 1 - tap:C_CONVW + e * CONV + CONV - tap]
                        if tap == 0:
                            last = dve.tensor_scalar(u[:, e, :], xi[:, e, :], wcol, None, ALU.mult)
                        else:
                            last = dve.scalar_tensor_tensor(u[:, e, tap:SEQ], xi[:, e, 0:SEQ - tap], wcol, u[:, e, tap:SEQ],
                                                            ALU.mult, ALU.add)
                        if tap < CONV - 1:
                            link(last)
                    last.then_inc(conv_ready, 1)
                if b == BATCH - 1:
                    layer1_second_norm(0)
                scan_inputs(b, b, "0xp", "0dt", C)
                for e in range(KE):
                    dve.wait_ge(y_out, ((b + 1) * CHUNKS - 1) * KE + e + 1)
                    dve.tensor_tensor(chan(C)[:, e, :], chan(C)[:, e, :], chan(B)[:, e, :], ALU.mult).then_inc(gated, 1)
                dve.wait_ge(evac, FIRST["0out", b] + 4)
                ssm = tok(E, 0)
                link(dve.tensor_tensor(ssm, ssm, per_column(ada[:, b, 2 * D:3 * D]), ALU.mult))
                ins = dve.tensor_tensor(xb, xb, ssm, ALU.add)
                ins.then_inc(x_updated, 1)
                dve.wait_ge(x_updated, b + 1)
            dve.wait_ge(x_updated, BATCH)
            for b in range(BATCH):
                xb = batch_rows(b)
                if b == 0:
                    layer1_skip(0)
                    layer1_first_norm(1)
                    layer1_second_norm(1)
                    layer1_skip(1)
                    dve.wait_ge(xn_ready, 2 * BATCH)
                    dve.sem_inc(rows_used, 1)
                else:
                    dve.wait_ge(evac, FIRST["1xT", b] + 4)
                    normalize(batch_rows(0), xn_next[:, :, :])
                    dve.wait_ge(ld_rows, 32)
                    affine(xn_next[:, :, :], R_NG).then_inc(xn_ready, 1)
                    for n in range(BATCH):
                        split_mask(n)
                    dve.wait_ge(mask_stored, 48 * BATCH)
                for d in range(2):
                    scan_inputs(2 + 2 * b + d, b, f"1xp{d}", f"1dt{d}", (C, F)[d])
                for step in range(KE + 1):
                    if step < KE:
                        dve.wait_ge(y_out, ((4 + 2 * b) * CHUNKS - 1) * KE + step + 1)
                        dve.tensor_tensor(chan(C)[:, step, :], chan(C)[:, step, :], chan(F)[:, step, :], ALU.add).then_inc(both_added, 1)
                    if step:
                        e = step - 1
                        dve.wait_ge(both_added, b * KE + e + 1)
                        dve.tensor_tensor(chan(C)[:, e, :], chan(C)[:, e, :], chan(B)[:, e, :], ALU.mult).then_inc(gated, 1)
                if b == BATCH - 1:
                    shift_queries(0)
                dve.wait_ge(evac, FIRST["1out", b] + 4)
                ssm = tok(E, 0)
                link(dve.tensor_tensor(ssm, ssm, per_column(ada1[:, b, 2 * D:3 * D]), ALU.mult))
                dve.tensor_tensor(xb, xb, ssm, ALU.add).then_inc(x_updated, 1)
                dve.wait_ge(x_updated, BATCH + b + 1)
            vector_attention(dve, link, normalize, condition, affine, shift_queries)


def pack(inputs):
    import numpy as np

    def arr(name):
        return np.asarray(inputs[name])

    def kmajor(w):
        k, m = w.shape
        return w.reshape(k // P, P, m).transpose(1, 0, 2).reshape(P, -1)

    def xproj(w):
        return kmajor(w.T)

    def chans(v):
        v = v.reshape(v.shape[0], -1)
        return v.reshape(-1, P, v.shape[1]).transpose(1, 0, 2).reshape(P, -1)

    g0 = lambda n: arr("L0_cond_" + n)
    g1 = lambda n: arr("L1_cond_" + n)
    g2 = lambda n: arr("L2_cond_" + n)
    g3 = lambda n: arr("L3_cond_" + n)
    cols = np.zeros((P, NCOLS), np.float32)

    def put(at, v):
        v = chans(v)
        cols[:, at:at + v.shape[1]] = v

    put(C_CONVW, g0("conv_w")), put(C_CONVB, g0("conv_b")), put(C_DTB, g0("dt_proj_b"))
    put(C_D, g0("D_param")), put(C_A, g0("A_log"))
    put(C_BX, g1("bx")), put(C_BZ, g1("bz"))
    for d in range(2):
        put(C_BC + d * KE, g1(f"bc{d + 1}")), put(C_BDT + d * KE, g1(f"bdt{d + 1}"))
        put(C_D1 + d * KE, g1(f"Dp{d + 1}")), put(C_A1 + d * KE * NS, g1(f"Alog{d + 1}"))
    put(C_BK2, g2("bk")), put(C_BQ3, g3("q_b")), put(C_BK3, g3("k_b"))
    rows = np.stack([
        np.concatenate([g0("ln_g"), g0("ln_b"), g1("norm1_g"), g1("norm1_b"), g1("norm2_g"), g1("norm2_b"), g1("bf")]),
        np.concatenate([g2(n) for n in ("norm_scale", "norm_bias", "film_norm_scale", "film_norm_bias", "bq", "bv", "film_out_b")]),
        np.concatenate([g3(n) for n in ("norm_w", "norm_b", "sb_norm_w", "sb_norm_b", "q_b", "v_b", "out_b")]),
    ])
    ada_w = np.concatenate([g0("ada_w").T, g1("Wada").T, g2("film_emb_W"), g3("emb_w")], 1)
    ada_b = np.concatenate([g0("ada_b"), g1("bada"), g2("film_emb_b"), g3("emb_b")])[None]
    w0 = np.concatenate([kmajor(g0("in_proj_w").T), xproj(g0("x_proj_w")), kmajor(g0("out_proj_w").T)], 1)
    w1 = np.concatenate([kmajor(g1("Wx").T), kmajor(g1("Wz").T), kmajor(g1("Wc1").T), kmajor(g1("Wc2").T),
                         xproj(g1("Wdbc1")), xproj(g1("Wdbc2")), kmajor(g1("Wf").T)], 1)
    wdt = np.stack([g0("dt_proj_w").T, g1("Wdt1").T, g1("Wdt2").T], 1)
    w23 = np.stack([np.concatenate([kmajor(w) for w in (g2("Wq"), g2("Wk"), g2("Wv"), g2("film_out_W"))], 1),
                    np.concatenate([kmajor(w) for w in (g3("q_w"), g3("k_w"), g3("v_w"), g3("out_w"))], 1)], 1)

    def by_token(m):
        return m.reshape(BATCH * TT, P).T

    m2, m3 = arr("mask_BxS_ik0"), arr("mask_BxS_ff1")
    return {
        "x": arr("x"), "cond_t": arr("cond_2048").T.reshape(KE, P, BATCH).transpose(1, 0, 2), "cols_in": cols, "rows_in": rows,
        "ada_w": ada_w.reshape(KE, P, NADA).transpose(1, 0, 2), "ada_b": ada_b, "w0": w0, "w1": w1, "wdt": wdt, "w23": w23,
        "mask2_row": m2, "mask2_col": by_token(m2), "mask3_row": m3, "mask3_col": by_token(m3),
    }


def kernel(**inputs):
    import numpy as np
    import concourse.bacc as bacc
    from concourse import mybir as mb
    from concourse.bass_utils import run_bass_kernel_spmd

    nc = bacc.Bacc("TRN2", target_bir_lowering=False, num_devices=1)
    arrays, args = {}, []
    for name, value in pack(inputs).items():
        value = np.ascontiguousarray(value)
        arrays["in_" + name] = value
        args.append(nc.dram_tensor("in_" + name, value.shape, mb.dt.from_np(value.dtype), kind="ExternalInput").ap())
    args.append(nc.dram_tensor("out_0", (BATCH, SEQ, D), mb.dt.float32, kind="ExternalOutput").ap())
    build(nc, *args)
    r = run_bass_kernel_spmd(nc, [arrays], core_ids=[0])
    return r.results[0]["out_0"]
```
